# Optimizing a Trainium2 kernel written in Bass

```python
import numpy as np
import jax
import jax.numpy as jnp

def _softmax(x, axis=-1):
    return jax.nn.softmax(x, axis=axis)

def _gelu(x):
    return jax.nn.gelu(x, approximate=True)

def _silu(x):
    return jax.nn.silu(x)

def _sigmoid(x):
    return jax.nn.sigmoid(x)

def _layernorm(x, axis=-1, eps=1e-05):
    m = jnp.mean(x, axis=axis, keepdims=True)
    v = jnp.var(x, axis=axis, keepdims=True)
    return (x - m) / jnp.sqrt(v + eps)

def _scatter_add(tgt, idx, src, axis=0):
    return tgt.at[idx].add(src)

def _segment_sum(src, seg, n):
    return jax.ops.segment_sum(src, seg, n)
kernel_name = 'mk_flamingo_gated_d4_seqx_r8_027d01'

def setup_inputs(seed: int=0):
    np.random.seed(seed)
    _w = jnp.asarray

    def _rec_inputs():
        import jax
        import jax.numpy as jnp
        _rk = jax.random.key(seed)
        x = -0.0002928 + 1 * jax.random.normal(jax.random.fold_in(_rk, 1), (32, 128, 128), jnp.float32)
        _lenS = 128 - jax.random.randint(jax.random.fold_in(_rk, 7), (32,), 0, max(1, 128 // 4) + 1, jnp.int32)
        _lenS2 = 77 - jax.random.randint(jax.random.fold_in(_rk, 8), (32,), 0, max(1, 77 // 4) + 1, jnp.int32)
        _ctx_1024P = jax.random.normal(jax.random.fold_in(_rk, 11), (32, 16, 128), jnp.float32)
        _ctx_1024c = jax.random.dirichlet(jax.random.fold_in(_rk, 511), 0.3 * jnp.ones((16,), jnp.float32), (32, 77))
        _ctx_1024t = jnp.einsum('bsk,bkd->bsd', _ctx_1024c, _ctx_1024P)
        _ctx_1024t = _ctx_1024t * jax.lax.rsqrt(jnp.mean(jnp.square(_ctx_1024t)) + 1e-12) * 0.953939
        ctx_1024 = 4.13588e-05 + 0.999923 * (_ctx_1024t + 0.3 * jax.random.normal(jax.random.fold_in(_rk, 611), (32, 77, 128), jnp.float32))
        _g = jax.random.normal(jax.random.fold_in(_rk, 9001), (2, 4), jnp.float32)
        _g = jnp.sign(_g) * jnp.maximum(jnp.abs(_g), 1.0) + (_g == 0) * 1.0
        g_xattn = _g[0]
        g_ffn = _g[1]
        return (x, ctx_1024, g_xattn, g_ffn)
    x, ctx_1024, g_xattn, g_ffn = _rec_inputs()

    def _L0_xattn_setup():
        import jax, jax.numpy as jnp
        import numpy as np
        import math
        EMBED_DIM = 128
        NUM_HEADS = 16
        D_K = EMBED_DIM // NUM_HEADS
        B, S_DEC, S_ENC = (4, 128, 256)
        key = jax.random.key(seed)
        ks = jax.random.split(key, 12)
        s = 1.0 / math.sqrt(EMBED_DIM)
        return {'Q_decoder': jax.random.normal(ks[0], (B, S_DEC, EMBED_DIM), jnp.float32), 'K_encoder': jax.random.normal(ks[1], (B, S_ENC, EMBED_DIM), jnp.float32), 'V_encoder': jax.random.normal(ks[2], (B, S_ENC, EMBED_DIM), jnp.float32), 'Wq': jax.random.normal(ks[3], (EMBED_DIM, EMBED_DIM), jnp.float32) * s, 'bq': jnp.zeros((EMBED_DIM,), jnp.float32), 'Wk': jax.random.normal(ks[4], (EMBED_DIM, EMBED_DIM), jnp.float32) * s, 'bk': jnp.zeros((EMBED_DIM,), jnp.float32), 'Wv': jax.random.normal(ks[5], (EMBED_DIM, EMBED_DIM), jnp.float32) * s, 'bv': jnp.zeros((EMBED_DIM,), jnp.float32), 'Wo': jax.random.normal(ks[6], (EMBED_DIM, EMBED_DIM), jnp.float32) * s, 'bo': jnp.zeros((EMBED_DIM,), jnp.float32)}
    _L0_xattn_all = _L0_xattn_setup()
    _L0_xattn_in = {k: v for k, v in _L0_xattn_all.items() if k in ('Wq', 'bq', 'Wk', 'bk', 'Wv', 'bv', 'Wo', 'bo')}
    del _L0_xattn_all

    def _L0_ffn_setup():
        import jax, jax.numpy as jnp
        import numpy as np
        B, S, D, H, E = (2, 256, 128, 512, 8)
        key = jax.random.key(seed)
        k0, k1, k2, k3 = jax.random.split(key, 4)
        x = jax.random.normal(k0, (B, S, D), dtype=jnp.float32)
        router_w = jax.random.normal(k1, (E, D), dtype=jnp.float32) * 0.02
        w1 = jax.random.normal(k2, (E, D, H), dtype=jnp.float32) * 0.02
        w2 = jax.random.normal(k3, (E, H, D), dtype=jnp.float32) * 0.02
        return {'x': x, 'router_w': router_w, 'w1': w1, 'w2': w2}
    _L0_ffn_all = _L0_ffn_setup()
    _L0_ffn_in = {k: v for k, v in _L0_ffn_all.items() if k in ('router_w', 'w1', 'w2')}
    del _L0_ffn_all

    def _L1_xattn_setup():
        import jax, jax.numpy as jnp
        import numpy as np
        key = jax.random.key(seed)
        k1, k2 = jax.random.split(key)
        B, T, K, D = (8, 512, 64, 128)
        X = jax.random.normal(k1, (B, T, D), dtype=jnp.float32)
        C = jax.random.normal(k2, (B, K, D), dtype=jnp.float32)
        sim_alpha = jnp.ones((1,), dtype=jnp.float32)
        sim_beta = jnp.zeros((1,), dtype=jnp.float32)
        return {'X': X, 'C': C, 'sim_alpha': sim_alpha, 'sim_beta': sim_beta}
    _L1_xattn_all = _L1_xattn_setup()
    _L1_xattn_in = {k: v for k, v in _L1_xattn_all.items() if k in ('sim_alpha', 'sim_beta')}
    del _L1_xattn_all

    def _L1_ffn_setup():
        import jax, jax.numpy as jnp
        import numpy as np
        B, S, D, F, E = (2, 256, 128, 512, 8)
        LN_EPS = 1e-05

        def _xavier(key, shape, fan_in, fan_out):
            a = np.sqrt(6.0 / (fan_in + fan_out))
            return jax.random.uniform(key, shape, jnp.float32, -a, a)
        key = jax.random.key(seed)
        ks = jax.random.split(key, 8)
        tgt = jax.random.normal(ks[0], (B, S, D), jnp.float32)
        router_w = _xavier(ks[1], (E, D), D, E)
        router_b = jnp.zeros((E,), jnp.float32)
        w1 = _xavier(ks[2], (E, D, F), D, F)
        b1 = jnp.zeros((E, F), jnp.float32)
        w2 = _xavier(ks[3], (E, F, D), F, D)
        b2 = jnp.zeros((E, D), jnp.float32)
        gamma = jnp.ones((D,), jnp.float32)
        beta = jnp.zeros((D,), jnp.float32)
        return {'tgt': tgt, 'router_w': router_w, 'router_b': router_b, 'w1': w1, 'b1': b1, 'w2': w2, 'b2': b2, 'gamma': gamma, 'beta': beta}
    _L1_ffn_all = _L1_ffn_setup()
    _L1_ffn_in = {k: v for k, v in _L1_ffn_all.items() if k in ('router_w', 'router_b', 'w1', 'b1', 'w2', 'b2', 'gamma', 'beta')}
    del _L1_ffn_all

    def _L2_xattn_setup():
        import jax, jax.numpy as jnp
        import numpy as np
        B, S, D = (2, 256, 128)
        H = 16
        DK = D // H
        key = jax.random.key(seed)
        ks = jax.random.split(key, 7)
        scale = 1.0 / np.sqrt(D)
        return {'Query': jax.random.normal(ks[0], (B, S, D), dtype=jnp.float32), 'Key': jax.random.normal(ks[1], (B, S, D), dtype=jnp.float32), 'Value': jax.random.normal(ks[2], (B, S, D), dtype=jnp.float32), 'Wq': jax.random.normal(ks[3], (D, D), dtype=jnp.float32) * scale, 'Wk': jax.random.normal(ks[4], (D, D), dtype=jnp.float32) * scale, 'Wv': jax.random.normal(ks[5], (D, D), dtype=jnp.float32) * scale, 'Wo': jax.random.normal(ks[6], (D, D), dtype=jnp.float32) * scale}
    _L2_xattn_all = _L2_xattn_setup()
    _L2_xattn_in = {k: v for k, v in _L2_xattn_all.items() if k in ('Wq', 'Wk', 'Wv', 'Wo')}
    del _L2_xattn_all

    def _L2_ffn_setup():
        import jax, jax.numpy as jnp
        import numpy as np
        D_MODEL, D_FF, D2, DL = (128, 512, 64, 64)
        D1 = D_FF // D2
        BATCH, SEQ = (2, 128)
        KERNEL_SCALE = D2 ** 0.5
        key = jax.random.key(seed)
        ks = jax.random.split(key, 7)
        xav = lambda k, shape, fan: jax.random.normal(k, shape, jnp.float32) * (2.0 / sum(fan)) ** 0.5
        x = jax.random.normal(ks[0], (BATCH, SEQ, D_MODEL), jnp.float32)
        m1 = xav(ks[1], (D_MODEL, DL), (D_MODEL, DL))
        m2 = xav(ks[2], (DL, D1, D2), (DL, D_FF))
        mb = jax.random.normal(ks[3], (D1, D2), jnp.float32)
        w1 = xav(ks[4], (D_MODEL, D1, D2), (D_MODEL, D_FF))
        w2 = xav(ks[5], (D2, D1, D_MODEL), (D_FF, D_MODEL)) * KERNEL_SCALE
        b2 = jax.random.normal(ks[6], (D_MODEL,), jnp.float32)
        return {'x': x, 'm1': m1, 'm2': m2, 'mb': mb, 'w1': w1, 'w2': w2, 'b2': b2}
    _L2_ffn_all = _L2_ffn_setup()
    _L2_ffn_in = {k: v for k, v in _L2_ffn_all.items() if k in ('m1', 'm2', 'mb', 'w1', 'w2', 'b2')}
    del _L2_ffn_all

    def _L3_xattn_setup():
        import jax, jax.numpy as jnp
        import numpy as np
        B, M, N, DIM, DH, H = (8, 512, 64, 128, 128, 8)
        INNER = DH * H
        EPS = 1e-05

        def _layernorm(x, g, b):
            mu = jnp.mean(x, axis=-1, keepdims=True)
            var = jnp.var(x, axis=-1, keepdims=True)
            return (x - mu) * jax.lax.rsqrt(var + EPS) * g + b
        key = jax.random.key(seed)
        ks = jax.random.split(key, 8)
        sd = 0.02
        return {'x': jax.random.normal(ks[0], (B, M, DIM), jnp.float32), 'latents': jax.random.normal(ks[1], (B, N, DIM), jnp.float32), 'gamma_media': jnp.ones((DIM,), jnp.float32), 'beta_media': jnp.zeros((DIM,), jnp.float32), 'gamma_lat': jnp.ones((DIM,), jnp.float32), 'beta_lat': jnp.zeros((DIM,), jnp.float32), 'Wq': jax.random.normal(ks[2], (DIM, INNER), jnp.float32) * sd, 'bq': jnp.zeros((INNER,), jnp.float32), 'Wkv': jax.random.normal(ks[3], (DIM, 2 * INNER), jnp.float32) * sd, 'bkv': jnp.zeros((2 * INNER,), jnp.float32), 'Wo': jax.random.normal(ks[4], (INNER, DIM), jnp.float32) * sd, 'bo': jnp.zeros((DIM,), jnp.float32)}
    _L3_xattn_all = _L3_xattn_setup()
    _L3_xattn_in = {k: v for k, v in _L3_xattn_all.items() if k in ('gamma_media', 'beta_media', 'gamma_lat', 'beta_lat', 'Wq', 'bq', 'Wkv', 'bkv', 'Wo', 'bo')}
    del _L3_xattn_all

    def _L3_ffn_setup():
        import jax, jax.numpy as jnp
        import numpy as np
        D_MODEL, FF_DIM = (128, 256)
        N_SHARED, N_ROUTED, TOP_K = (1, 8, 2)
        BATCH, SEQ = (2, 256)
        key = jax.random.key(seed)
        ks = jax.random.split(key, 8)
        init = lambda k, shape: jax.random.normal(k, shape, jnp.float32) * 0.02
        x = jax.random.normal(ks[0], (BATCH, SEQ, D_MODEL), jnp.float32)
        Wg = init(ks[1], (D_MODEL, N_ROUTED))
        Ws1 = init(ks[2], (D_MODEL, FF_DIM))
        Ws3 = init(ks[3], (D_MODEL, FF_DIM))
        Ws2 = init(ks[4], (FF_DIM, D_MODEL))
        We1 = init(ks[5], (N_ROUTED, D_MODEL, FF_DIM))
        We3 = init(ks[6], (N_ROUTED, D_MODEL, FF_DIM))
        We2 = init(ks[7], (N_ROUTED, FF_DIM, D_MODEL))
        return {'x': x, 'Wg': Wg, 'Ws1': Ws1, 'Ws3': Ws3, 'Ws2': Ws2, 'We1': We1, 'We3': We3, 'We2': We2}
    _L3_ffn_all = _L3_ffn_setup()
    _L3_ffn_in = {k: v for k, v in _L3_ffn_all.items() if k in ('Wg', 'Ws1', 'Ws3', 'Ws2', 'We1', 'We3', 'We2')}
    del _L3_ffn_all
    return {'x': x, 'ctx_1024': ctx_1024, 'g_xattn': g_xattn, 'g_ffn': g_ffn, 'L0_xattn_Wq': _L0_xattn_in['Wq'], 'L0_xattn_bq': _L0_xattn_in['bq'], 'L0_xattn_Wk': _L0_xattn_in['Wk'], 'L0_xattn_bk': _L0_xattn_in['bk'], 'L0_xattn_Wv': _L0_xattn_in['Wv'], 'L0_xattn_bv': _L0_xattn_in['bv'], 'L0_xattn_Wo': _L0_xattn_in['Wo'], 'L0_xattn_bo': _L0_xattn_in['bo'], 'L0_ffn_router_w': _L0_ffn_in['router_w'], 'L0_ffn_w1': _L0_ffn_in['w1'], 'L0_ffn_w2': _L0_ffn_in['w2'], 'L1_xattn_sim_alpha': _L1_xattn_in['sim_alpha'], 'L1_xattn_sim_beta': _L1_xattn_in['sim_beta'], 'L1_ffn_router_w': _L1_ffn_in['router_w'], 'L1_ffn_router_b': _L1_ffn_in['router_b'], 'L1_ffn_w1': _L1_ffn_in['w1'], 'L1_ffn_b1': _L1_ffn_in['b1'], 'L1_ffn_w2': _L1_ffn_in['w2'], 'L1_ffn_b2': _L1_ffn_in['b2'], 'L1_ffn_gamma': _L1_ffn_in['gamma'], 'L1_ffn_beta': _L1_ffn_in['beta'], 'L2_xattn_Wq': _L2_xattn_in['Wq'], 'L2_xattn_Wk': _L2_xattn_in['Wk'], 'L2_xattn_Wv': _L2_xattn_in['Wv'], 'L2_xattn_Wo': _L2_xattn_in['Wo'], 'L2_ffn_m1': _L2_ffn_in['m1'], 'L2_ffn_m2': _L2_ffn_in['m2'], 'L2_ffn_mb': _L2_ffn_in['mb'], 'L2_ffn_w1': _L2_ffn_in['w1'], 'L2_ffn_w2': _L2_ffn_in['w2'], 'L2_ffn_b2': _L2_ffn_in['b2'], 'L3_xattn_gamma_media': _L3_xattn_in['gamma_media'], 'L3_xattn_beta_media': _L3_xattn_in['beta_media'], 'L3_xattn_gamma_lat': _L3_xattn_in['gamma_lat'], 'L3_xattn_beta_lat': _L3_xattn_in['beta_lat'], 'L3_xattn_Wq': _L3_xattn_in['Wq'], 'L3_xattn_bq': _L3_xattn_in['bq'], 'L3_xattn_Wkv': _L3_xattn_in['Wkv'], 'L3_xattn_bkv': _L3_xattn_in['bkv'], 'L3_xattn_Wo': _L3_xattn_in['Wo'], 'L3_xattn_bo': _L3_xattn_in['bo'], 'L3_ffn_Wg': _L3_ffn_in['Wg'], 'L3_ffn_Ws1': _L3_ffn_in['Ws1'], 'L3_ffn_Ws3': _L3_ffn_in['Ws3'], 'L3_ffn_Ws2': _L3_ffn_in['Ws2'], 'L3_ffn_We1': _L3_ffn_in['We1'], 'L3_ffn_We3': _L3_ffn_in['We3'], 'L3_ffn_We2': _L3_ffn_in['We2']}

def reference(x, ctx_1024, g_xattn, g_ffn, L0_xattn_Wq, L0_xattn_bq, L0_xattn_Wk, L0_xattn_bk, L0_xattn_Wv, L0_xattn_bv, L0_xattn_Wo, L0_xattn_bo, L0_ffn_router_w, L0_ffn_w1, L0_ffn_w2, L1_xattn_sim_alpha, L1_xattn_sim_beta, L1_ffn_router_w, L1_ffn_router_b, L1_ffn_w1, L1_ffn_b1, L1_ffn_w2, L1_ffn_b2, L1_ffn_gamma, L1_ffn_beta, L2_xattn_Wq, L2_xattn_Wk, L2_xattn_Wv, L2_xattn_Wo, L2_ffn_m1, L2_ffn_m2, L2_ffn_mb, L2_ffn_w1, L2_ffn_w2, L2_ffn_b2, L3_xattn_gamma_media, L3_xattn_beta_media, L3_xattn_gamma_lat, L3_xattn_beta_lat, L3_xattn_Wq, L3_xattn_bq, L3_xattn_Wkv, L3_xattn_bkv, L3_xattn_Wo, L3_xattn_bo, L3_ffn_Wg, L3_ffn_Ws1, L3_ffn_Ws3, L3_ffn_Ws2, L3_ffn_We1, L3_ffn_We3, L3_ffn_We2):
    import jax
    import jax.numpy as jnp

    def _L0_xattn_ref(Q_decoder, K_encoder, V_encoder, Wq, bq, Wk, bk, Wv, bv, Wo, bo):
        import jax, jax.numpy as jnp
        import numpy as np
        import math
        EMBED_DIM = 128
        NUM_HEADS = 16
        D_K = EMBED_DIM // NUM_HEADS
        B, S_DEC, S_ENC = (4, 128, 256)
        b, sd, d = Q_decoder.shape
        se = K_encoder.shape[1]
        Q = (Q_decoder @ Wq + bq).reshape(b, sd, NUM_HEADS, D_K).transpose(0, 2, 1, 3)
        K = (K_encoder @ Wk + bk).reshape(b, se, NUM_HEADS, D_K).transpose(0, 2, 1, 3)
        V = (V_encoder @ Wv + bv).reshape(b, se, NUM_HEADS, D_K).transpose(0, 2, 1, 3)
        scores = jnp.einsum('bhqd,bhkd->bhqk', Q, K) / math.sqrt(D_K)
        attn = jax.nn.softmax(scores, axis=-1)
        out = jnp.einsum('bhqk,bhkd->bhqd', attn, V)
        out = out.transpose(0, 2, 1, 3).reshape(b, sd, d)
        return out @ Wo + bo

    def _L0_ffn_ref(x, router_w, w1, w2):
        import jax, jax.numpy as jnp
        import numpy as np
        B, S, D, H, E = (2, 256, 128, 512, 8)
        b, s, d = x.shape
        e = router_w.shape[0]
        xf = x.reshape(-1, d)
        probs = jax.nn.softmax(xf @ router_w.T, axis=-1)
        topv, topi = jax.lax.top_k(probs, 2)
        topv = topv / (topv.sum(axis=-1, keepdims=True) + 1e-09)
        cw = (jax.nn.one_hot(topi, e, dtype=xf.dtype) * topv[..., None]).sum(axis=1)
        h = jax.nn.gelu(jnp.einsum('td,edh->teh', xf, w1), approximate=False)
        y = jnp.einsum('teh,ehd->ted', h, w2)
        out = jnp.einsum('te,ted->td', cw, y)
        return out.reshape(b, s, d)

    def _L1_xattn_ref(X, C, sim_alpha, sim_beta):
        import jax, jax.numpy as jnp
        import numpy as np
        K = C.shape[1]
        sim = jax.nn.sigmoid(sim_beta + sim_alpha * jnp.einsum('bkd,btd->bkt', C, X))
        max_idx = jnp.argmax(sim, axis=1)
        mask = jax.nn.one_hot(max_idx, K, axis=1, dtype=sim.dtype)
        sim_out = sim * mask
        agg = jnp.einsum('bkt,btd->bkd', sim_out, X) + C
        denom = jnp.sum(mask, axis=-1, keepdims=True) + 1.0
        out_k = agg / denom
        out = jnp.einsum('bkt,bkd->btd', sim, out_k)
        return X + out

    def _L1_ffn_ref(tgt, router_w, router_b, w1, b1, w2, b2, gamma, beta):
        import jax, jax.numpy as jnp
        import numpy as np
        B, S, D, F, E = (2, 256, 128, 512, 8)
        LN_EPS = 1e-05

        def _xavier(key, shape, fan_in, fan_out):
            a = np.sqrt(6.0 / (fan_in + fan_out))
            return jax.random.uniform(key, shape, jnp.float32, -a, a)
        logits = jnp.einsum('bsd,ed->bse', tgt, router_w) + router_b
        rw = jax.nn.softmax(logits, axis=-1)
        rw = jnp.zeros_like(rw).at[..., 0].set(1.0)
        h = jax.nn.relu(jnp.einsum('bsd,edf->besf', tgt, w1) + b1[None, :, None, :])
        eo = jnp.einsum('besf,efd->besd', h, w2) + b2[None, :, None, :]
        tgt2 = jnp.einsum('besd,bse->bsd', eo, rw)
        x = tgt + tgt2
        mean = jnp.mean(x, axis=-1, keepdims=True)
        var = jnp.mean(jnp.square(x - mean), axis=-1, keepdims=True)
        return (x - mean) * jax.lax.rsqrt(var + LN_EPS) * gamma + beta

    def _L2_xattn_ref(Query, Key, Value, Wq, Wk, Wv, Wo):
        import jax, jax.numpy as jnp
        import numpy as np
        B, S, D = (2, 256, 128)
        H = 16
        DK = D // H
        b = Query.shape[0]
        q = (Query @ Wq.T).reshape(b, -1, H, DK).transpose(0, 2, 1, 3)
        k = (Key @ Wk.T).reshape(b, -1, H, DK).transpose(0, 2, 1, 3)
        v = (Value @ Wv.T).reshape(b, -1, H, DK).transpose(0, 2, 1, 3)
        scores = jnp.einsum('bhqd,bhkd->bhqk', q, k) / jnp.sqrt(jnp.float32(DK))
        attn = jax.nn.softmax(scores, axis=1)
        ctx = jnp.einsum('bhqk,bhkd->bhqd', attn, v)
        ctx = ctx.transpose(0, 2, 1, 3).reshape(b, -1, H * DK)
        return ctx @ Wo.T

    def _L2_ffn_ref(x, m1, m2, mb, w1, w2, b2):
        import jax, jax.numpy as jnp
        import numpy as np
        D_MODEL, D_FF, D2, DL = (128, 512, 64, 64)
        D1 = D_FF // D2
        BATCH, SEQ = (2, 128)
        KERNEL_SCALE = D2 ** 0.5
        x_shape = x.shape
        xf = x.reshape(-1, x_shape[-1])
        d1 = w1.shape[1]
        lr = xf @ m1
        mask_logits = jnp.einsum('bl,lxy->bxy', lr, m2) + mb
        quant_mask = jnp.argmax(mask_logits, axis=-1)
        w1p = jnp.transpose(w1, (1, 2, 0))
        w2p = jnp.transpose(w2, (1, 0, 2))
        j = jnp.arange(d1)[None, :]
        w = w1p[j, quant_mask]
        mid = jnp.einsum('ai,aji->aj', xf, w)
        relu = jax.nn.relu(mid)
        v = w2p[j, quant_mask]
        res = jnp.einsum('ai,aij->aj', relu, v) + b2
        return res.reshape(x_shape)

    def _L3_xattn_ref(x, latents, gamma_media, beta_media, gamma_lat, beta_lat, Wq, bq, Wkv, bkv, Wo, bo):
        import jax, jax.numpy as jnp
        import numpy as np
        B, M, N, DIM, DH, H = (8, 512, 64, 128, 128, 8)
        INNER = DH * H
        EPS = 1e-05

        def _layernorm(x, g, b):
            mu = jnp.mean(x, axis=-1, keepdims=True)
            var = jnp.var(x, axis=-1, keepdims=True)
            return (x - mu) * jax.lax.rsqrt(var + EPS) * g + b
        b = x.shape[0]
        xn = _layernorm(x, gamma_media, beta_media)
        ln = _layernorm(latents, gamma_lat, beta_lat)
        q = ln @ Wq + bq
        kv_input = jnp.concatenate([xn, ln], axis=1)
        kv = kv_input @ Wkv + bkv
        k, v = jnp.split(kv, 2, axis=-1)

        def to_heads(t):
            return t.reshape(b, t.shape[1], H, DH).transpose(0, 2, 1, 3)
        q, k, v = (to_heads(q), to_heads(k), to_heads(v))
        q = q * DH ** (-0.5)
        sim = jnp.einsum('bhid,bhjd->bhij', q, k)
        attn = jax.nn.softmax(sim, axis=-1)
        out = jnp.einsum('bhij,bhjd->bhid', attn, v)
        out = out.transpose(0, 2, 1, 3).reshape(b, -1, INNER)
        return out @ Wo + bo

    def _L3_ffn_ref(x, Wg, Ws1, Ws3, Ws2, We1, We3, We2):
        import jax, jax.numpy as jnp
        import numpy as np
        D_MODEL, FF_DIM = (128, 256)
        N_SHARED, N_ROUTED, TOP_K = (1, 8, 2)
        BATCH, SEQ = (2, 256)
        B, S, d = x.shape
        E = Wg.shape[1]
        xf = x.reshape(-1, d)
        T = xf.shape[0]
        gates = jax.nn.sigmoid(xf @ Wg)
        vals, idx = jax.lax.top_k(gates, TOP_K)
        vals = vals / vals.sum(axis=-1, keepdims=True)
        w = jnp.zeros((T, E), x.dtype).at[jnp.arange(T)[:, None], idx].add(vals)
        shared = jax.nn.silu(xf @ Ws1) * (xf @ Ws3) @ Ws2
        h = jax.nn.silu(jnp.einsum('td,edf->tef', xf, We1)) * jnp.einsum('td,edf->tef', xf, We3)
        routed = jnp.einsum('tef,efd,te->td', h, We2, w)
        out = (shared + routed) / (N_SHARED + TOP_K)
        return out.reshape(B, S, d)
    x = x + jnp.tanh(g_xattn[0]) * _L0_xattn_ref(_layernorm(x, axis=-1), ctx_1024, ctx_1024, L0_xattn_Wq, L0_xattn_bq, L0_xattn_Wk, L0_xattn_bk, L0_xattn_Wv, L0_xattn_bv, L0_xattn_Wo, L0_xattn_bo)
    x = x + jnp.tanh(g_ffn[0]) * _L0_ffn_ref(_layernorm(x, axis=-1), L0_ffn_router_w, L0_ffn_w1, L0_ffn_w2)
    x = x + jnp.tanh(g_xattn[1]) * _L1_xattn_ref(_layernorm(x, axis=-1), ctx_1024, L1_xattn_sim_alpha, L1_xattn_sim_beta)
    x = x + jnp.tanh(g_ffn[1]) * _L1_ffn_ref(_layernorm(x, axis=-1), L1_ffn_router_w, L1_ffn_router_b, L1_ffn_w1, L1_ffn_b1, L1_ffn_w2, L1_ffn_b2, L1_ffn_gamma, L1_ffn_beta)
    x = x + jnp.tanh(g_xattn[2]) * _L2_xattn_ref(_layernorm(x, axis=-1), ctx_1024, ctx_1024, L2_xattn_Wq, L2_xattn_Wk, L2_xattn_Wv, L2_xattn_Wo)
    x = x + jnp.tanh(g_ffn[2]) * _L2_ffn_ref(_layernorm(x, axis=-1), L2_ffn_m1, L2_ffn_m2, L2_ffn_mb, L2_ffn_w1, L2_ffn_w2, L2_ffn_b2)
    x = x + jnp.tanh(g_xattn[3]) * _L3_xattn_ref(ctx_1024, _layernorm(x, axis=-1), L3_xattn_gamma_media, L3_xattn_beta_media, L3_xattn_gamma_lat, L3_xattn_beta_lat, L3_xattn_Wq, L3_xattn_bq, L3_xattn_Wkv, L3_xattn_bkv, L3_xattn_Wo, L3_xattn_bo)
    x = x + jnp.tanh(g_ffn[3]) * _L3_ffn_ref(_layernorm(x, axis=-1), L3_ffn_Wg, L3_ffn_Ws1, L3_ffn_Ws3, L3_ffn_Ws2, L3_ffn_We1, L3_ffn_We3, L3_ffn_We2)
    return x

_drawn_inputs = setup_inputs


def setup_inputs(seed=0):
    import zlib

    import numpy as np

    out = dict(_drawn_inputs(seed))
    spreads = {'L0_xattn_bq': (0.0, 0.1),
     'L0_xattn_bk': (0.0, 0.8),
     'L0_xattn_bv': (0.0, 0.1),
     'L0_xattn_bo': (0.0, 0.1),
     'L1_ffn_router_b': (0.0, 0.1),
     'L1_ffn_b1': (0.0, 0.8),
     'L1_ffn_b2': (0.0, 0.8),
     'L1_ffn_gamma': (1.0, 0.6),
     'L1_ffn_beta': (0.0, 0.8),
     'L3_xattn_gamma_media': (1.0, 0.6),
     'L3_xattn_beta_media': (0.0, 0.8),
     'L3_xattn_gamma_lat': (1.0, 0.6),
     'L3_xattn_beta_lat': (0.0, 0.8),
     'L3_xattn_bq': (0.0, 0.8),
     'L3_xattn_bkv': (0.0, 0.8),
     'L3_xattn_bo': (0.0, 0.8)}
    factors = {'g_ffn': 8.0,
     'L3_xattn_Wq': 8.0,
     'L3_xattn_Wkv': 8.0,
     'L3_xattn_Wo': 8.0,
     'L3_ffn_Wg': 8.0,
     'L3_ffn_Ws1': 8.0,
     'L3_ffn_Ws3': 8.0,
     'L3_ffn_Ws2': 8.0,
     'L3_ffn_We1': 8.0,
     'L3_ffn_We3': 8.0,
     'L3_ffn_We2': 8.0}
    for name, (base, spread) in spreads.items():
        noise = np.random.default_rng([zlib.crc32(name.encode()), seed]).standard_normal(out[name].shape)
        drawn = base * np.exp(spread * noise) if base else spread * noise
        out[name] = jnp.asarray(drawn.astype(out[name].dtype))
    for name, factor in factors.items():
        out[name] = (out[name] * factor).astype(out[name].dtype)
    return out
```

```python
from contextlib import ExitStack

import concourse.bass as bass
from concourse import mybir

ALU = mybir.AluOpType
ACT = mybir.ActivationFunctionType
AX = mybir.AxisListType
F32 = mybir.dt.float32
BF16 = mybir.dt.bfloat16

B = 32
S = 128
D = 128
KC = 77
HEADS = 16
DK = D // HEADS
HG = 4
NG = HEADS // HG
GB = 4
NGB = B // GB
GT = GB * S
E0, F0 = 8, 512
MX, MY, ML = 8, 64, 64
E3, F3 = 8, 256
H3 = 8
KV = KC + S
EPS = 1e-5
VPAD = D // HG + DK


def wait(eng, sem, value):
    if isinstance(value, int) and value <= 0:
        return
    eng.wait_ge(sem, value)


def pipeline(eng, step, n=B):
    step(-1, 1, True, False, False)
    step(0, 0, True, True, False)
    step(1, 1, True, True, True)
    with eng.Fori(0, (n - 4) // 2) as i:
        step(i * 2 + 2, 0, True, True, True)
        step(i * 2 + 3, 1, True, True, True)
    step(n - 2, 0, True, True, True)
    step(n - 1, 1, False, True, True)
    step(n, 0, False, False, True)


class Memory:
    pass


def row_of(ap):
    return ap.partition_broadcast(128)


def column_of(ap):
    return ap.rearrange("(p a) -> p a", a=1)


def allocate(nc, ctx):
    def sb(name, shape, dtype=F32):
        return ctx.enter_context(nc.sbuf_tensor(name, shape, dtype))

    m = Memory()
    m.x = sb("x_residual", [S, B, D])
    m.ctx = sb("context_rows", [KC, B, D])
    m.ctx_t = sb("context_transposed", [D, B * KC])
    m.moments = sb("x_moments", [S, B, 6])
    m.mean2 = sb("x_mean_doubled", [S, B])
    m.halves = sb("x_halves_difference", [S, B])
    m.var = sb("x_variance", [S, B])
    m.sd = sb("x_deviation", [S, B])
    m.rstd = sb("x_rstd", [S, B])
    m.shift = sb("x_shift", [S, B])
    m.eps = sb("layernorm_eps", [128, 1])
    m.ident = sb("identity", [128, 128])
    m.ident_bf = sb("identity_bf16", [128, 128], BF16)
    m.group_mask = sb("head_in_group_mask", [128, HG])
    m.gate = sb("tanh_gates", [128, 8])
    m.down = sb("descending_count", [128, 128])
    m.psum = ctx.enter_context(nc.psum_tensor("psum", [128, 8, 512], F32))
    m.wq0, m.wk0, m.wv0, m.wo0 = (sb(f"L0_w{c}", [D, D]) for c in "qkvo")
    m.wq2, m.wk2, m.wv2, m.wo2 = (sb(f"L2_w{c}_transposed", [D, D]) for c in "qkvo")
    m.w2_raw = sb("L2_weights_raw", [D, 4, D])
    m.bias_columns = sb("L0_bias_columns", [D, 3])
    m.row_bo0 = sb("L0_bo_row", [128, D])
    m.router_raw = sb("L0_router_raw", [E0, D])
    m.router_t = sb("L0_router_transposed", [D, E0])
    m.wg3 = sb("L3_router", [D, E3])
    return m


def prepare(nc, ctx, m, a):
    def sem(name):
        return ctx.enter_context(nc.semaphore(name))

    x_loaded, ctx_loaded, small_loaded, w_loaded = (sem(n) for n in ("x_loaded", "ctx_loaded", "small_loaded", "w_loaded"))
    blank, ident_ready, mask_ready, down_ready = (sem(n) for n in ("blank", "ident_ready", "mask_ready", "down_ready"))
    identb_ready, tanh_done = sem("identb_ready"), sem("tanh_done")
    tr_done, tr_read = sem("tr_done"), sem("tr_read")
    gated = sem("gated")
    NT = B // GB
    LOADS_X = 4
    with nc.Block() as block:
        @block.sync
        def _(sync):
            for q in range(LOADS_X):
                rows = slice(q * B // LOADS_X, (q + 1) * B // LOADS_X)
                sync.dma_start(m.x[:, rows, :], a["x"][rows].rearrange("b s d -> s b d")).then_inc(x_loaded, 16)
            sync.dma_start(m.w2_raw[:, :, :][:, 0, :], a["L2_xattn_Wq"]).then_inc(w_loaded, 16)
            sync.dma_start(m.w2_raw[:, 1, :], a["L2_xattn_Wk"]).then_inc(w_loaded, 16)
            sync.dma_start(m.w2_raw[:, 2, :], a["L2_xattn_Wv"]).then_inc(w_loaded, 16)
            sync.dma_start(m.w2_raw[:, 3, :], a["L2_xattn_Wo"]).then_inc(w_loaded, 16)
            sync.dma_start(m.router_raw[:, :], a["L0_ffn_router_w"]).then_inc(w_loaded, 16)
            sync.wait_ge(small_loaded, 16 * 11)
            sync.wait_ge(ctx_loaded, 16)

        @block.scalar
        def _(act):
            act.dma_start(m.ctx[:, :, :], a["ctx_1024"].rearrange("b k d -> k b d")).then_inc(ctx_loaded, 16)
            act.dma_start(m.gate[:, 0:4], row_of(a["g_xattn"])).then_inc(small_loaded, 16)
            act.dma_start(m.gate[:, 4:8], row_of(a["g_ffn"])).then_inc(small_loaded, 16)
            act.dma_start(m.wq0[:, :], a["L0_xattn_Wq"]).then_inc(small_loaded, 16)
            act.dma_start(m.wk0[:, :], a["L0_xattn_Wk"]).then_inc(small_loaded, 16)
            act.dma_start(m.wv0[:, :], a["L0_xattn_Wv"]).then_inc(small_loaded, 16)
            act.dma_start(m.wo0[:, :], a["L0_xattn_Wo"]).then_inc(small_loaded, 16)
            act.dma_start(m.wg3[:, :], a["L3_ffn_Wg"]).then_inc(small_loaded, 16)
            act.dma_start(m.bias_columns[:, 0:1], column_of(a["L0_xattn_bq"])).then_inc(small_loaded, 16)
            act.dma_start(m.bias_columns[:, 1:2], column_of(a["L0_xattn_bk"])).then_inc(small_loaded, 16)
            act.dma_start(m.bias_columns[:, 2:3], column_of(a["L0_xattn_bv"])).then_inc(small_loaded, 16)
            act.dma_start(m.row_bo0[:, :], row_of(a["L0_xattn_bo"])).then_inc(small_loaded, 16)
            act.wait_ge(small_loaded, 16 * 11)
            nc.scalar.activation(m.gate[:, :], m.gate[:, :], ACT.Tanh).then_inc(tanh_done, 1)
            for t in range(1, NT, 2):
                act.wait_ge(tr_done, t + 1)
                nc.scalar.copy(m.ctx_t[:, t * GB * KC:(t + 1) * GB * KC],
                               m.psum[:, t % 8, 0:GB * KC]).then_inc(tr_read, 1)
            act.wait_ge(tr_done, NT + 2)
            nc.scalar.copy(m.router_t[:, :], m.psum[:, 1, 0:E0]).then_inc(tr_read, 1)

        @block.gpsimd
        def _(pool):
            nc.gpsimd.memset(m.ident[:, :], 0.0).then_inc(blank, 1)
            nc.gpsimd.memset(m.eps[:, :], EPS).then_inc(blank, 1)
            nc.gpsimd.iota(m.down[:, :], [[-1, 128]], base=128, channel_multiplier=0,
                           allow_small_or_imprecise_dtypes=True).then_inc(down_ready, 1)
            pool.wait_ge(blank, 2)
            nc.gpsimd.affine_select(out=m.ident[:, :], in_=m.ident[:, :], compare_op=ALU.not_equal, fill=1.0,
                                    base=0, pattern=[[-1, 128]], channel_multiplier=1).then_inc(ident_ready, 1)

        @block.tensor
        def _(pe):
            pe.wait_ge(ident_ready, 1)
            pe.wait_ge(ctx_loaded, 16)
            for t in range(NT):
                for u in range(GB):
                    last = nc.tensor.transpose(m.psum[:, t % 8, u * KC:(u + 1) * KC], m.ctx[:, t * GB + u, :],
                                               m.ident[0:KC, 0:KC])
                last.then_inc(tr_done, 1)
            pe.wait_ge(w_loaded, 16 * 5)
            pe.wait_ge(tr_read, NT)
            for u in range(4):
                last = nc.tensor.transpose(m.psum[:, 0, u * D:(u + 1) * D], m.w2_raw[:, u, :], m.ident[:, :])
            last.then_inc(tr_done, 1)
            nc.tensor.transpose(m.psum[:, 1, 0:E0], m.router_raw[:, :], m.ident[0:E0, 0:E0]).then_inc(tr_done, 1)

        @block.vector
        def _(dve):
            dve.wait_ge(ident_ready, 1)
            nc.vector.tensor_copy(m.ident_bf[:, :], m.ident[:, :]).then_inc(identb_ready, 1)
            nc.vector.tensor_reduce(m.group_mask[:, :], m.ident[:, :].rearrange("p (j h d) -> p h j d", h=HG, d=DK),
                                    AX.XY, ALU.add).then_inc(mask_ready, 1)
            for t in range(0, NT, 2):
                dve.wait_ge(tr_done, t + 1)
                nc.vector.tensor_copy(m.ctx_t[:, t * GB * KC:(t + 1) * GB * KC],
                                      m.psum[:, t % 8, 0:GB * KC]).then_inc(tr_read, 1)
            dve.wait_ge(tr_done, NT + 1)
            for u, w in enumerate((m.wq2, m.wk2, m.wv2, m.wo2)):
                nc.vector.tensor_copy(w[:, :], m.psum[:, 0, u * D:(u + 1) * D]).then_inc(tr_read, 1)
            dve.wait_ge(x_loaded, 16 * LOADS_X)
            dve.wait_ge(tanh_done, 1)
            nc.vector.tensor_scalar(m.row_bo0[:, :], m.row_bo0[:, :], m.gate[:, 0:1], None, ALU.mult).then_inc(gated, 1)
            for b in range(B):
                nc.vector.bn_stats(m.moments[:, b, :], m.x[:, b, :])


def variance_of_x(nc, m, dve, parts_ready, var_ready):
    even_mean, even_m2, odd_mean, odd_m2 = (m.moments[:, :, c] for c in (1, 2, 4, 5))
    nc.vector.tensor_tensor(m.mean2[:, :], even_mean, odd_mean, ALU.add).then_inc(parts_ready, 1)
    nc.vector.tensor_tensor(m.halves[:, :], even_mean, odd_mean, ALU.subtract).then_inc(parts_ready, 1)
    nc.vector.tensor_tensor(m.var[:, :], even_m2, odd_m2, ALU.add).then_inc(parts_ready, 1)
    dve.wait_ge(parts_ready, 3)
    nc.vector.scalar_tensor_tensor(m.halves[:, :], m.halves[:, :], 0.25, m.halves[:, :], ALU.mult, ALU.mult).then_inc(parts_ready, 1)
    dve.wait_ge(parts_ready, 4)
    nc.vector.scalar_tensor_tensor(m.var[:, :], m.var[:, :], 1.0 / D, m.halves[:, :], ALU.mult, ALU.add).then_inc(var_ready, 1)


def rstd_of_x(nc, m, dve, sd_ready, rstd_ready, shift_ready):
    dve.wait_ge(sd_ready, 1)
    nc.vector.reciprocal(m.rstd[:, :], m.sd[:, :]).then_inc(rstd_ready, 1)
    dve.wait_ge(rstd_ready, 1)
    nc.vector.scalar_tensor_tensor(m.shift[:, :], m.mean2[:, :], -0.5, m.rstd[:, :], ALU.mult, ALU.mult).then_inc(shift_ready, 1)
    dve.wait_ge(shift_ready, 1)


def head_attention(nc, m, sem, layer, w, clear):
    over_heads = layer == 2
    wq, wk, wv, wo = w
    n_rec = KC if over_heads else HEADS
    names = ("sd_ready rstd_ready shift_ready xn_ready xt_in_psum xt_ready proj_in_psum q_ready k_ready "
             "parts_ready var_ready scores_done negmax_ready shifted exp_ready sum_ready recip_ready probs_ready pt_in_psum pt_by_act "
             "pt_by_dve ct_ready heads_done heads_ready v_ready y_done x_done bias_added zeroed")
    s = {n: sem(f"{n}_{layer}") for n in names.split()}
    gate = m.gate[:, layer:layer + 1]
    with ExitStack() as ctx:
        def sb(name, shape, dtype=F32):
            return ctx.enter_context(nc.sbuf_tensor(f"{name}_{layer}", shape, dtype))

        xn = sb("xn", [S, 2, D])
        xt = sb("xt", [D, 2, S])
        qt = sb("qt", [D, 2, S])
        ktm = sb("kt_masked", [D, 2, HG, KC])
        vpad = sb("v_padded", [KC, 2, HEADS, VPAD])
        e = sb("exp_scores", [S, 2, HEADS, KC])
        negmax = sb("negated_max", [S, 2, n_rec], BF16)
        total = sb("softmax_sum", [S, 2, n_rec])
        recip = sb("softmax_recip", [S, 2, n_rec])
        pt = sb("probs_transposed", [KC, HEADS, S])
        ot = sb("heads_out", [D, 2, S])
        cts = sb("context_slot", [D, 2, KC])

        def scores_view():
            v = m.psum[:, 0:NG, 0:HG * KC]
            return v.rearrange("p j (h k) -> p k j h", k=KC) if over_heads else v.rearrange("p j (h k) -> p j h k", k=KC)

        def per_row(t, par):
            return t[:, par, :] if over_heads else t[:, par, :].rearrange("p (j h) -> p j h", h=HG)

        with nc.Block() as block:
            @block.gpsimd
            def _(pool):
                clear(pool)
                for par in range(2):
                    nc.gpsimd.memset(vpad[:, par, :, :], 0.0).then_inc(s["zeroed"], 1)

                def step(b, par, front, middle, back):
                    if front:
                        wait(pool, s["proj_in_psum"], b)
                        nc.gpsimd.tensor_copy(cts[:, 1 - par, :], m.ctx_t[:, bass.ds((b + 1) * KC, KC)]).then_inc(s["ct_ready"], 1)
                    if front and layer == 0:
                        wait(pool, s["xn_ready"], b + 2)
                        nc.gpsimd.tensor_tensor(m.x[:, b + 1, :], m.x[:, b + 1, :], m.row_bo0[:, :],
                                                ALU.add).then_inc(s["bias_added"], 1)
                    if middle:
                        wait(pool, s["recip_ready"], b + 1)
                        shape = [S, HEADS, KC]
                        r = (recip[:, par, :].unsqueeze(1) if over_heads else recip[:, par, :].unsqueeze(2)).to_broadcast(shape)
                        nc.gpsimd.tensor_tensor(e[:, par, :, :], e[:, par, :, :], r, ALU.mult).then_inc(s["probs_ready"], 1)

                pipeline(pool, step)

            @block.scalar
            def _(act):
                act.wait_ge(s["var_ready"], 1)
                nc.scalar.activation(m.sd[:, :], m.var[:, :], ACT.Sqrt, bias=m.eps[:, 0:1]).then_inc(s["sd_ready"], 1)

                def step(b, par, front, middle, back):
                    nxt = 1 - par
                    if front:
                        wait(act, s["xt_in_psum"], b + 2)
                        wait(act, s["proj_in_psum"], b)
                        nc.scalar.copy(xt[:, nxt, :], m.psum[:, 6, 0:S]).then_inc(s["xt_ready"], 1)
                    if back:
                        for n, g in enumerate((0, 2)):
                            wait(act, s["pt_in_psum"], (b - 1) * NG + g + 1)
                            wait(act, s["heads_done"], b - 1)
                            nc.scalar.copy(pt[:, g * HG:(g + 1) * HG, :],
                                           m.psum[0:KC, 4, :].rearrange("p (h s) -> p h s", s=S)).then_inc(s["pt_by_act"], 1)
                    if middle:
                        wait(act, s["shifted"], b + 1)
                        wait(act, s["pt_in_psum"], (b - 1) * NG)
                        nc.scalar.activation(e[:, par, :, :].rearrange("p (j h) k -> p j (h k)", h=HG),
                                             m.psum[:, 0:NG, 0:HG * KC], ACT.Exp, scale=DK ** -0.5).then_inc(s["exp_ready"], 1)
                    if back:
                        wait(act, s["heads_done"], b)
                        wait(act, s["y_done"], b - 2)
                        if layer == 0:
                            nc.scalar.activation(ot[:, nxt, :], m.psum[:, 7, 0:S], ACT.Identity,
                                                 bias=m.bias_columns[:, 2:3]).then_inc(s["heads_ready"], 1)
                        else:
                            nc.scalar.copy(ot[:, nxt, :], m.psum[:, 7, 0:S]).then_inc(s["heads_ready"], 1)
                    if front:
                        wait(act, s["proj_in_psum"], b + 2)
                        wait(act, s["scores_done"], b)
                        if layer == 0:
                            nc.scalar.activation(qt[:, nxt, :], m.psum[:, 6, S:2 * S], ACT.Identity,
                                                 bias=m.bias_columns[:, 0:1]).then_inc(s["q_ready"], 1)
                        else:
                            nc.scalar.copy(qt[:, nxt, :], m.psum[:, 6, S:2 * S]).then_inc(s["q_ready"], 1)
                        if isinstance(b, int) and b == -1:
                            act.wait_ge(s["zeroed"], 2)
                        nc.scalar.copy(vpad[:, nxt, :, 0:DK], m.psum[0:KC, 6, 3 * S:4 * S].rearrange("p (h d) -> p h d", d=DK))\
                            .then_inc(s["v_ready"], 1)

                pipeline(act, step)

            @block.vector
            def _(dve):
                variance_of_x(nc, m, dve, s["parts_ready"], s["var_ready"])
                rstd_of_x(nc, m, dve, s["sd_ready"], s["rstd_ready"], s["shift_ready"])

                def step(b, par, front, middle, back):
                    nxt = 1 - par
                    if front:
                        wait(dve, s["xt_in_psum"], b)
                        nc.vector.tensor_scalar(xn[:, nxt, :], m.x[:, b + 1, :], m.rstd[:, bass.ds(b + 1, 1)],
                                                m.shift[:, bass.ds(b + 1, 1)], ALU.mult, ALU.add).then_inc(s["xn_ready"], 1)
                    if middle:
                        wait(dve, s["scores_done"], b + 1)
                        wait(dve, s["shifted"], b - 1)
                        nc.vector.tensor_reduce(per_row(negmax, par), scores_view(), AX.XY if over_heads else AX.X,
                                                ALU.max, negate=True).then_inc(s["negmax_ready"], 1)
                    if back:
                        for n, g in enumerate((1, 3)):
                            wait(dve, s["pt_in_psum"], (b - 1) * NG + g + 1)
                            wait(dve, s["heads_done"], b - 1)
                            nc.vector.tensor_copy(pt[:, g * HG:(g + 1) * HG, :],
                                                  m.psum[0:KC, 5, :].rearrange("p (h s) -> p h s", s=S)).then_inc(s["pt_by_dve"], 1)
                    if middle:
                        wait(dve, s["exp_ready"], b + 1)
                        ev = e[:, par, :, :]
                        nc.vector.tensor_reduce(total[:, par, :], ev.rearrange("p h k -> p k h") if over_heads else ev,
                                                AX.X, ALU.add).then_inc(s["sum_ready"], 1)
                        wait(dve, s["sum_ready"], b + 1)
                        wait(dve, s["probs_ready"], b - 1)
                        nc.vector.reciprocal(recip[:, par, :], total[:, par, :]).then_inc(s["recip_ready"], 1)
                    if back:
                        wait(dve, s["y_done"], b)
                        if layer == 0:
                            wait(dve, s["bias_added"], b)
                        nc.vector.scalar_tensor_tensor(m.x[:, b - 1, :], m.psum[:, 7, S:2 * S], gate, m.x[:, b - 1, :],
                                                       ALU.mult, ALU.add).then_inc(s["x_done"], 1)
                        wait(dve, s["x_done"], b)
                    if front:
                        wait(dve, s["v_ready"], b + 2)
                        kin = m.psum[:, 6, 2 * S:2 * S + KC].unsqueeze(1).to_broadcast([D, HG, KC])
                        mask = m.group_mask[:, :].unsqueeze(2).to_broadcast([D, HG, KC])
                        nc.vector.scalar_tensor_tensor(ktm[:, nxt, :, :], kin, m.bias_columns[:, 1:2] if layer == 0 else 0.0,
                                                       mask, ALU.add, ALU.mult).then_inc(s["k_ready"], 1)
                    if back:
                        nc.vector.bn_stats(m.moments[:, b - 1, :], m.x[:, b - 1, :])

                pipeline(dve, step)

            @block.tensor
            def _(pe):
                def step(b, par, front, middle, back):
                    nxt = 1 - par
                    if middle:
                        wait(pe, s["q_ready"], b + 1)
                        wait(pe, s["k_ready"], b + 1)
                        wait(pe, s["exp_ready"], b)
                        for j in range(NG):
                            rows = slice(32 * j, 32 * j + 32)
                            last = nc.tensor.matmul(m.psum[:, j, 0:HG * KC], qt[rows, par, :],
                                                    ktm[rows, par, :, :].rearrange("p h k -> p (h k)"), start=True, stop=True)
                        last.then_inc(s["scores_done"], 1)
                    if front:
                        wait(pe, s["xn_ready"], b + 2)
                        wait(pe, s["q_ready"], b + 1)
                        wait(pe, s["k_ready"], b + 1)
                        nc.tensor.transpose(m.psum[:, 6, 0:S], xn[:, nxt, :], m.ident[:, :]).then_inc(s["xt_in_psum"], 1)
                    if back:
                        wait(pe, s["probs_ready"], b)
                        for g in range(NG):
                            if g % 2 == 0:
                                wait(pe, s["pt_by_act"], (b - 1) * 2 + g // 2)
                            else:
                                wait(pe, s["pt_by_dve"], (b - 1) * 2 + g // 2)
                            for h in range(HG):
                                last = nc.tensor.transpose(m.psum[0:KC, 4 + g % 2, h * S:(h + 1) * S],
                                                           e[:, nxt, g * HG + h, :], m.ident[:, :])
                            last.then_inc(s["pt_in_psum"], 1)
                    if middle:
                        wait(pe, s["negmax_ready"], b + 1)
                        for j in range(NG):
                            nm = negmax[:, par, :]
                            nm = nm.unsqueeze(1) if over_heads else nm[:, j * HG:(j + 1) * HG].unsqueeze(2)
                            last = nc.tensor.matmul(m.psum[:, j, 0:HG * KC].rearrange("p (h k) -> p h k", k=KC), m.ident_bf[:, :],
                                                    nm.to_broadcast([S, HG, KC]), start=False, stop=True, skip_group_check=True)
                        last.then_inc(s["shifted"], 1)
                    if back:
                        wait(pe, s["pt_by_act"], b * 2)
                        wait(pe, s["pt_by_dve"], b * 2)
                        wait(pe, s["x_done"], b - 1)
                        for h in range(HG):
                            for g in range(NG):
                                at = (g * HG + h) * VPAD - h * DK
                                lhs = vpad[:, nxt, :, :].rearrange("p h c -> p (h c)")[:, at:at + 32]
                                last = nc.tensor.matmul(m.psum[32 * g:32 * g + 32, 7, 0:S], lhs, pt[:, g * HG + h, :],
                                                        start=(h == 0), stop=(h == HG - 1), skip_group_check=True)
                        last.then_inc(s["heads_done"], 1)
                    if front:
                        wait(pe, s["xt_ready"], b + 2)
                        nc.tensor.matmul(m.psum[:, 6, S:2 * S], wq[:, :], xt[:, nxt, :], start=True, stop=True)
                        wait(pe, s["ct_ready"], b + 2)
                        ct = cts[:, nxt, :]
                        nc.tensor.matmul(m.psum[:, 6, 2 * S:2 * S + KC], wk[:, :], ct, start=True, stop=True)
                        nc.tensor.matmul(m.psum[0:KC, 6, 3 * S:4 * S], ct, wv[:, :], start=True, stop=True).then_inc(s["proj_in_psum"], 1)
                    if back:
                        wait(pe, s["heads_ready"], b)
                        nc.tensor.matmul(m.psum[:, 7, S:2 * S], ot[:, nxt, :], wo[:, :], start=True, stop=True).then_inc(s["y_done"], 1)

                pipeline(pe, step)


def transpose_groups(nc, m, s, xn, xts, xt_all, engines, router=None):
    nc_engines = engines
    which, eng = nc_engines

    def step(g, par, front, middle, back):
        nxt = 1 - par
        if which == "vector":
            if front:
                wait(eng, s["xt_in_psum"], g)
                for t in range(GB):
                    at = (g + 1) * GB + t
                    last = nc.vector.tensor_scalar(xn[:, nxt, t, :], m.x[:, at, :], m.rstd[:, bass.ds(at, 1)],
                                                   m.shift[:, bass.ds(at, 1)], ALU.mult, ALU.add)
                last.then_inc(s["xn_ready"], 1)
            if middle:
                wait(eng, s["logits_in_psum"], g + 1)
                nc.vector.tensor_copy(router[1][:, bass.ds(g * GB, GB), :],
                                      m.psum[:, 2 + par, 0:GB * E0].rearrange("p (t e) -> p t e", e=E0)).then_inc(s["logits_ready"], 1)
        if which == "scalar" and front:
            wait(eng, s["xt_in_psum"], g + 2)
            wait(eng, s["logits_in_psum"], g)
            wait(eng, s["xt_copied"], g)
            nc.scalar.copy(xts[:, nxt, :], m.psum[:, nxt, :]).then_inc(s["xts_ready"], 1)
        if which == "gpsimd" and front:
            wait(eng, s["xts_ready"], g + 2)
            nc.gpsimd.tensor_copy(xt_all[:, bass.ds((g + 1) * GT, GT)], xts[:, nxt, :]).then_inc(s["xt_copied"], 1)
        if which == "tensor":
            if front:
                wait(eng, s["xn_ready"], g + 2)
                wait(eng, s["xts_ready"], g)
                for t in range(GB):
                    last = nc.tensor.transpose(m.psum[:, nxt, t * S:(t + 1) * S], xn[:, nxt, t, :], m.ident[:, :])
                last.then_inc(s["xt_in_psum"], 1)
            if middle:
                wait(eng, s["xts_ready"], g + 1)
                wait(eng, s["logits_ready"], g - 1)
                for t in range(GB):
                    last = nc.tensor.matmul(m.psum[:, 2 + par, t * E0:(t + 1) * E0], xts[:, par, t * S:(t + 1) * S],
                                            router[0][:, :], start=True, stop=True)
                last.then_inc(s["logits_in_psum"], 1)

    pipeline(eng, step, NGB)


def top_two(nc, m, link, p, work, m1, m2, pick1, pick2):
    wide = [S, B, E0]
    down = m.down[:, 0:E0].unsqueeze(1).to_broadcast(wide)

    def spread(t):
        return t[:, :].unsqueeze(2).to_broadcast(wide)

    for value, pick, first in ((m1, pick1, True), (m2, pick2, False)):
        link(nc.vector.tensor_reduce(value[:, :], p[:, :, :], AX.X, ALU.max))
        link(nc.vector.tensor_tensor(pick[:, :, :], p[:, :, :], spread(value), ALU.is_ge))
        link(nc.vector.tensor_tensor(pick[:, :, :], pick[:, :, :], down, ALU.mult))
        link(nc.vector.tensor_reduce(work[:, :], pick[:, :, :], AX.X, ALU.max))
        link(nc.vector.tensor_tensor(pick[:, :, :], pick[:, :, :], spread(work), ALU.is_equal))
        if first:
            link(nc.vector.scalar_tensor_tensor(p[:, :, :], pick[:, :, :], -4.0, p[:, :, :], ALU.mult, ALU.add))


def experts(nc, m, sem, layer, router_t, w_up, w_gate, w_down, n_exp, shared, clear):
    hidden = F0 if layer == 0 else F3
    chunks = hidden // 128
    names = ("parts_ready var_ready sd_ready rstd_ready shift_ready xn_ready xt_in_psum xts_ready xt_copied "
             "logits_in_psum logits_ready link exp_wanted exp_ready weights_ready shared_ready hidden_in_psum silu_ready up_read "
             "hidden_ready y_done_a y_done_b y_read_a y_read_b w_loaded_a w_loaded_b stats_done")
    s = {n: sem(f"{n}_ffn{layer}") for n in names.split()}
    gate = m.gate[:, 4 + layer:5 + layer]
    y_done, y_read = (s["y_done_a"], s["y_done_b"]), (s["y_read_a"], s["y_read_b"])
    w_loaded = (s["w_loaded_a"], s["w_loaded_b"])
    loads = 2 if layer == 0 else 3
    with ExitStack() as ctx:
        def sb(name, shape, dtype=F32):
            return ctx.enter_context(nc.sbuf_tensor(f"{name}_ffn{layer}", shape, dtype))

        xn = sb("xn", [S, 2, GB, D])
        xts = sb("xt_slot", [D, 2, GT])
        xt_all = sb("xt_all", [D, B * S])
        logits = sb("logits", [S, B, E0])
        m1, m2, work, rec = (sb(n, [S, B]) for n in ("top1", "top2", "pick_code", "weight_recip"))
        pick1, pick2 = sb("pick1", [S, B, E0]), sb("pick2", [S, B, E0])
        weight = sb("expert_weight", [S, n_exp, B])
        up = sb("w_up", [D, 2, hidden])
        down = sb("w_down", [128, 2, chunks, D])
        side = sb("w_gate", [D, 2, hidden]) if layer == 3 else None
        silu = sb("silu", [128, 2, GT]) if layer == 3 else None
        hid = sb("hidden", [128, 2, chunks, GT])

        def all_experts(eng, block_of):
            block_of(0, 0, False)
            with eng.Fori(0, 3) as i:
                block_of(i * 2 + 1, 1, False)
                block_of(i * 2 + 2, 0, False)
            for e in range(7, n_exp):
                block_of(e, e % 2, e == n_exp - 1)

        with nc.Block() as block:
            @block.sync
            def _(sync):
                for e in range(n_exp):
                    slot = e % 2
                    if e >= 2:
                        sync.wait_ge(y_done[1], (e - 1) * (NGB // 2))
                    sync.dma_start(up[:, slot, :], w_up(e)).then_inc(w_loaded[slot], 16)
                    if layer == 3:
                        sync.dma_start(side[:, slot, :], w_gate(e)).then_inc(w_loaded[slot], 16)
                    sync.dma_start(down[:, slot, :, :], w_down(e).rearrange("(c f) d -> f c d", f=128)).then_inc(w_loaded[slot], 16)

            @block.gpsimd
            def _(pool):
                clear(pool)
                transpose_groups(nc, m, s, xn, xts, xt_all, ("gpsimd", pool))

            @block.scalar
            def _(act):
                act.wait_ge(s["var_ready"], 1)
                nc.scalar.activation(m.sd[:, :], m.var[:, :], ACT.Sqrt, bias=m.eps[:, 0:1]).then_inc(s["sd_ready"], 1)
                transpose_groups(nc, m, s, xn, xts, xt_all, ("scalar", act))
                act.wait_ge(s["exp_wanted"], 1)
                nc.scalar.activation(logits[:, :, :], logits[:, :, :], ACT.Exp,
                                     scale=1.0 if layer == 0 else -1.0).then_inc(s["exp_ready"], 1)
                if layer == 0:
                    act.wait_ge(s["logits_ready"], NGB)
                    act.sem_inc(s["hidden_ready"], chunks)

                def unit(e, g, u):
                    n = e * NGB + g
                    for c in range(chunks):
                        if layer == 0:
                            wait(act, s["hidden_in_psum"], n * chunks + c + 1)
                            if c == 0:
                                wait(act, y_done[u], e * (NGB // 2) + g_pair(g, u))
                            nc.scalar.activation(hid[:, u, c, :], m.psum[:, c, :], ACT.Gelu).then_inc(s["hidden_ready"], 1)
                        else:
                            wait(act, s["hidden_in_psum"], n * chunks + c + 1)
                            wait(act, s["hidden_ready"], n * chunks + c + 1)
                            nc.scalar.activation(silu[:, c, :], m.psum[:, c, :], ACT.Silu).then_inc(s["silu_ready"], 1)

                def block_of(e, slot, last):
                    with act.Fori(0, NGB // 2) as i:
                        pair[0] = i
                        unit(e, i * 2, 0)
                        unit(e, i * 2 + 1, 1)

                pair = [None]

                def g_pair(g, u):
                    return pair[0]

                all_experts(act, block_of)

            @block.vector
            def _(dve):
                variance_of_x(nc, m, dve, s["parts_ready"], s["var_ready"])
                rstd_of_x(nc, m, dve, s["sd_ready"], s["rstd_ready"], s["shift_ready"])
                transpose_groups(nc, m, s, xn, xts, xt_all, ("vector", dve), (router_t, logits))
                count = [0]

                def link(ins):
                    count[0] += 1
                    ins.then_inc(s["link"], 1)
                    dve.wait_ge(s["link"], count[0])

                wide = [S, B, E0]

                def spread(t):
                    return t[:, :].unsqueeze(2).to_broadcast(wide)

                dve.wait_ge(s["logits_ready"], NGB)
                if layer == 0:
                    link(nc.vector.tensor_reduce(work[:, :], logits[:, :, :], AX.X, ALU.max))
                    nc.vector.tensor_tensor(logits[:, :, :], logits[:, :, :], spread(work), ALU.subtract).then_inc(s["exp_wanted"], 1)
                    dve.wait_ge(s["exp_ready"], 1)
                    link(nc.vector.tensor_reduce(work[:, :], logits[:, :, :], AX.X, ALU.add))
                    link(nc.vector.reciprocal(rec[:, :], work[:, :]))
                    link(nc.vector.tensor_tensor(logits[:, :, :], logits[:, :, :], spread(rec), ALU.mult))
                else:
                    dve.sem_inc(s["exp_wanted"], 1)
                    dve.wait_ge(s["exp_ready"], 1)
                    link(nc.vector.tensor_scalar(logits[:, :, :], logits[:, :, :], 1.0, None, ALU.add))
                    link(nc.vector.reciprocal(logits[:, :, :], logits[:, :, :]))
                top_two(nc, m, link, logits, work, m1, m2, pick1, pick2)
                link(nc.vector.scalar_tensor_tensor(work[:, :], m1[:, :], 1e-9 if layer == 0 else 0.0, m2[:, :], ALU.add, ALU.add))
                link(nc.vector.reciprocal(rec[:, :], work[:, :]))
                link(nc.vector.tensor_scalar(rec[:, :], rec[:, :], gate, 1.0 if layer == 0 else 1.0 / 3.0, ALU.mult, ALU.mult))
                link(nc.vector.tensor_tensor(pick1[:, :, :], pick1[:, :, :], spread(m1), ALU.mult))
                link(nc.vector.tensor_tensor(pick2[:, :, :], pick2[:, :, :], spread(m2), ALU.mult))
                link(nc.vector.tensor_tensor(pick1[:, :, :], pick1[:, :, :], pick2[:, :, :], ALU.add))
                link(nc.vector.tensor_tensor(weight[:, shared:shared + E0, :].rearrange("p e b -> p b e"), pick1[:, :, :],
                                             spread(rec), ALU.mult))
                if shared:
                    link(nc.vector.memset(weight[:, 0, :], 1.0 / 3.0))
                    link(nc.vector.tensor_scalar(weight[:, 0, :], weight[:, 0, :], gate, None, ALU.mult))
                if layer == 3:
                    dve.sem_inc(s["hidden_ready"], chunks)

                def multiply(e, g, u, p):
                    n = e * NGB + g
                    for c in range(chunks):
                        wait(dve, s["silu_ready"], n * chunks + c + 1)
                        if c == 0:
                            wait(dve, y_done[u], e * (NGB // 2) + p)
                        nc.vector.tensor_tensor(hid[:, u, c, :], silu[:, c, :], m.psum[:, 2 + c, :], ALU.mult)\
                            .then_inc(s["hidden_ready"], 1)

                def update(e, g, u, p, last):
                    wait(dve, y_done[u], e * (NGB // 2) + p + 1)
                    for t in range(GB):
                        at = g * GB + t
                        ins = nc.vector.scalar_tensor_tensor(m.x[:, at, :], m.psum[:, 4 + u, t * D:(t + 1) * D],
                                                             weight[:, e, bass.ds(at, 1)], m.x[:, at, :], ALU.mult, ALU.add)
                    ins.then_inc(y_read[u], 1)

                def stats(g):
                    for t in range(GB):
                        nc.vector.bn_stats(m.moments[:, g * GB + t, :], m.x[:, g * GB + t, :])

                def block_of(e, slot, last):
                    with dve.Fori(0, NGB // 2) as i:
                        if layer == 3:
                            multiply(e, i * 2, 0, i)
                            multiply(e, i * 2 + 1, 1, i)
                        update(e, i * 2, 0, i, last)
                        update(e, i * 2 + 1, 1, i, last)

                all_experts(dve, block_of)
                dve.wait_ge(y_read[0], n_exp * NGB // 2)
                dve.wait_ge(y_read[1], n_exp * NGB // 2)
                for b in range(B):
                    nc.vector.bn_stats(m.moments[:, b, :], m.x[:, b, :])

            @block.tensor
            def _(pe):
                transpose_groups(nc, m, s, xn, xts, xt_all, ("tensor", pe), (router_t, logits))
                pe.wait_ge(s["xt_copied"], NGB)
                pe.wait_ge(s["xts_ready"], NGB)
                pe.wait_ge(s["logits_ready"], NGB)

                def block_of(e, slot, last):
                    with pe.Fori(0, NGB // 2) as i:
                        wait(pe, w_loaded[slot], (e + 2 - slot) * 8 * loads)
                        for u in range(2):
                            n = e * NGB + i * 2 + u
                            for c in range(chunks):
                                wait(pe, s["hidden_ready"], n * chunks + c + 1)
                                cols = slice(c * 128, (c + 1) * 128)
                                moving = xt_all[:, bass.ds((i * 2 + u) * GT, GT)]
                                last_mm = nc.tensor.matmul(m.psum[:, c, :], up[:, slot, cols], moving, start=True, stop=True)
                                if layer == 3:
                                    last_mm = nc.tensor.matmul(m.psum[:, 2 + c, :], side[:, slot, cols], moving, start=True, stop=True)
                                last_mm.then_inc(s["hidden_in_psum"], 1)
                        for u in range(2):
                            n = e * NGB + i * 2 + u
                            wait(pe, s["hidden_ready"], (n + 2) * chunks)
                            wait(pe, y_read[u], e * (NGB // 2) + i)
                            for t in range(GB):
                                for c in range(chunks):
                                    last_mm = nc.tensor.matmul(m.psum[:, 4 + u, t * D:(t + 1) * D], hid[:, u, c, t * S:(t + 1) * S],
                                                               down[:, slot, c, :], start=(c == 0), stop=(c == chunks - 1))
                            last_mm.then_inc(y_done[u], 1)

                all_experts(pe, block_of)


def chain(eng, sem, done, length):
    count = [0]

    def link(ins):
        count[0] += 1
        assert count[0] <= length
        ins.then_inc(sem, 1)
        wait(eng, sem, done * length + count[0])

    return link


def competitive_attention(nc, m, sem, clear):
    names = ("parts_ready var_ready sd_ready rstd_ready shift_ready loaded neg_ready ones_ready xn_used xn_ready xt_in_psum xt_ready "
             "z_in_psum exp_ready sim_ready simt_in_psum simt_ready agg_in_psum rows_ready y_done x_done mid_link back_link")
    s = {n: sem(f"{n}_1") for n in names.split()}
    gate = m.gate[:, 1:2]
    MID, BACK = 6, 3
    with ExitStack() as ctx:
        def sb(name, shape, dtype=F32):
            return ctx.enter_context(nc.sbuf_tensor(f"{name}_xattn1", shape, dtype))

        xn = sb("xn", [S, 2, GB, D])
        xt = sb("xt", [D, 2, GT])
        alpha_beta = sb("alpha_beta", [S, 2])
        sim = sb("sim", [S, 2, GB, KC])
        pick = sb("pick", [S, 2, GB, KC])
        best = sb("best_sim", [S, GB])
        code = sb("pick_code", [S, GB])
        weighted = sb("weighted_tokens", [S, 2, GB, D + 1])
        simt = sb("sim_transposed", [KC, GT])
        rows = sb("context_out", [KC, GB, D])
        tally = sb("token_count", [KC, 2, 2])
        with nc.Block() as block:
            @block.gpsimd
            def _(pool):
                clear(pool)
                nc.gpsimd.memset(weighted[:, :, :, :], 1.0).then_inc(s["ones_ready"], 1)

            @block.sync
            def _(sync):
                sync.dma_start(alpha_beta[:, 0:1], row_of(m.a["L1_xattn_sim_alpha"])).then_inc(s["loaded"], 16)
                sync.dma_start(alpha_beta[:, 1:2], row_of(m.a["L1_xattn_sim_beta"])).then_inc(s["loaded"], 16)

            @block.scalar
            def _(act):
                act.wait_ge(s["var_ready"], 1)
                nc.scalar.activation(m.sd[:, :], m.var[:, :], ACT.Sqrt, bias=m.eps[:, 0:1]).then_inc(s["sd_ready"], 1)
                act.wait_ge(s["neg_ready"], 1)

                def step(g, par, front, middle, back):
                    nxt = 1 - par
                    if middle:
                        wait(act, s["z_in_psum"], g + 1)
                        wait(act, s["simt_in_psum"], g - 1)
                        nc.scalar.activation(sim[:, par, :, :].rearrange("p b k -> p (b k)"), m.psum[:, 1, 0:GB * KC], ACT.Exp,
                                             scale=alpha_beta[:, 0:1], bias=alpha_beta[:, 1:2]).then_inc(s["exp_ready"], 1)
                    if back:
                        wait(act, s["simt_in_psum"], g)
                        wait(act, s["y_done"], g - 1)
                        nc.scalar.copy(simt[:, :], m.psum[0:KC, 2, :]).then_inc(s["simt_ready"], 1)
                    if front:
                        wait(act, s["xt_in_psum"], g + 2)
                        wait(act, s["z_in_psum"], g)
                        nc.scalar.copy(xt[:, nxt, :], m.psum[:, 0, :]).then_inc(s["xt_ready"], 1)

                pipeline(act, step, NGB)

            @block.vector
            def _(dve):
                dve.wait_ge(s["loaded"], 32)
                nc.vector.tensor_scalar(alpha_beta[:, :], alpha_beta[:, :], -1.0, None, ALU.mult).then_inc(s["neg_ready"], 1)
                variance_of_x(nc, m, dve, s["parts_ready"], s["var_ready"])
                rstd_of_x(nc, m, dve, s["sd_ready"], s["rstd_ready"], s["shift_ready"])
                dve.wait_ge(s["ones_ready"], 1)
                wide = [S, GB, KC]

                def step(g, par, front, middle, back):
                    nxt = 1 - par
                    if front:
                        wait(dve, s["xt_in_psum"], g)
                        wait(dve, s["xn_used"], g)
                        for t in range(GB):
                            at = (g + 1) * GB + t
                            ins = nc.vector.tensor_scalar(xn[:, nxt, t, :], m.x[:, at, :], m.rstd[:, bass.ds(at, 1)],
                                                          m.shift[:, bass.ds(at, 1)], ALU.mult, ALU.add)
                        ins.then_inc(s["xn_ready"], 1)
                    if back:
                        link = chain(dve, s["back_link"], g - 1, BACK)
                        wait(dve, s["agg_in_psum"], g)
                        wait(dve, s["y_done"], g - 1)
                        agg = m.psum[0:KC, 3:5, 0:2 * (D + 1)].rearrange("p j (u c) -> p j u c", u=2)
                        nc.vector.tensor_scalar(tally[:, :, :].unsqueeze(3), agg[:, :, :, D:D + 1], 1.0, None, ALU.add)
                        link(nc.vector.tensor_tensor(rows[:, :, :].rearrange("p (j u) d -> p j u d", u=2), agg[:, :, :, 0:D],
                                                     m.ctx[:, bass.ds((g - 1) * GB, GB), :].rearrange("p (j u) d -> p j u d", u=2), ALU.add))
                        tl = tally[:, :, :].rearrange("p j u -> p (j u)")
                        link(nc.vector.reciprocal(tl, tl))
                        link(nc.vector.tensor_tensor(rows[:, :, :], rows[:, :, :], tl.unsqueeze(2).to_broadcast([KC, GB, D]), ALU.mult))
                    if middle:
                        link = chain(dve, s["mid_link"], g, MID)
                        wait(dve, s["exp_ready"], g + 1)
                        wait(dve, s["agg_in_psum"], g - 1)
                        sv, pv = sim[:, par, :, :], pick[:, par, :, :]
                        link(nc.vector.tensor_scalar(sv, sv, 1.0, None, ALU.add))
                        link(nc.vector.reciprocal(sv, sv))
                        link(nc.vector.tensor_reduce(best[:, :], sv, AX.X, ALU.max))
                        link(nc.vector.tensor_tensor(pv, sv, best[:, :].unsqueeze(2).to_broadcast(wide), ALU.is_ge))
                        link(nc.vector.tensor_tensor(pv, pv, m.down[:, 0:KC].unsqueeze(1).to_broadcast(wide), ALU.mult))
                        link(nc.vector.tensor_reduce(code[:, :], pv, AX.X, ALU.max))
                        nc.vector.tensor_tensor(pv, pv, code[:, :].unsqueeze(2).to_broadcast(wide), ALU.is_equal)
                        for t in range(GB):
                            ins = nc.vector.tensor_scalar(weighted[:, par, t, 0:D], xn[:, par, t, :], best[:, t:t + 1], None, ALU.mult)
                        ins.then_inc(s["sim_ready"], 1)
                        xg = m.x[:, bass.ds(g * GB, GB), :].rearrange("p b d -> p (b d)")
                        nc.vector.scalar_tensor_tensor(xg, xn[:, par, :, :].rearrange("p b d -> p (b d)"), gate, xg,
                                                       ALU.mult, ALU.add).then_inc(s["xn_used"], 1)
                    if back:
                        wait(dve, s["y_done"], g)
                        xg = m.x[:, bass.ds((g - 1) * GB, GB), :].rearrange("p b d -> p (b d)")
                        nc.vector.scalar_tensor_tensor(xg, m.psum[:, 5, :], gate, xg, ALU.mult, ALU.add).then_inc(s["x_done"], 1)

                pipeline(dve, step, NGB)
                dve.wait_ge(s["x_done"], NGB)
                for b in range(B):
                    nc.vector.bn_stats(m.moments[:, b, :], m.x[:, b, :])

            @block.tensor
            def _(pe):
                def step(g, par, front, middle, back):
                    nxt = 1 - par
                    if middle:
                        wait(pe, s["xt_ready"], g + 1)
                        wait(pe, s["exp_ready"], g)
                        for t in range(GB):
                            mm = nc.tensor.matmul(m.psum[:, 1, t * KC:(t + 1) * KC], xt[:, par, t * S:(t + 1) * S],
                                                  m.ctx_t[:, bass.ds((g * GB + t) * KC, KC)], start=True, stop=True)
                        mm.then_inc(s["z_in_psum"], 1)
                    if back:
                        wait(pe, s["sim_ready"], g)
                        wait(pe, s["simt_ready"], g - 1)
                        for t in range(GB):
                            mm = nc.tensor.transpose(m.psum[0:KC, 2, t * S:(t + 1) * S], sim[:, nxt, t, :], m.ident[:, :])
                        mm.then_inc(s["simt_in_psum"], 1)
                        wait(pe, s["back_link"], (g - 1) * BACK)
                        for t in range(GB):
                            mm = nc.tensor.matmul(m.psum[0:KC, 3 + t // 2, (t % 2) * (D + 1):(t % 2 + 1) * (D + 1)], pick[:, nxt, t, :],
                                                  weighted[:, nxt, t, :], start=True, stop=True)
                        mm.then_inc(s["agg_in_psum"], 1)
                    if front:
                        wait(pe, s["xn_ready"], g + 2)
                        wait(pe, s["xt_ready"], g + 1)
                        for t in range(GB):
                            mm = nc.tensor.transpose(m.psum[:, 0, t * S:(t + 1) * S], xn[:, nxt, t, :], m.ident[:, :])
                        mm.then_inc(s["xt_in_psum"], 1)
                    if back:
                        wait(pe, s["back_link"], g * BACK)
                        wait(pe, s["simt_ready"], g)
                        wait(pe, s["x_done"], g - 1)
                        for t in range(GB):
                            mm = nc.tensor.matmul(m.psum[:, 5, t * D:(t + 1) * D], simt[:, t * S:(t + 1) * S], rows[:, t, :],
                                                  start=True, stop=True)
                        mm.then_inc(s["y_done"], 1)

                pipeline(pe, step, NGB)


def dense_feed_forward(nc, m, sem, clear):
    names = ("parts_ready var_ready sd_ready rstd_ready shift_ready loaded rows_ready xn_ready xt_in_psum xt_ready base_ready "
             "hidden_in_psum hidden_ready y_done z_ready z_var_ready z_sd_ready zn_ready scaled moved x_done link w_transposed")
    s = {n: sem(f"{n}_ffn1") for n in names.split()}
    chunks = F0 // 128
    LINKS = 6
    a = m.a
    with ExitStack() as ctx:
        def sb(name, shape, dtype=F32):
            return ctx.enter_context(nc.sbuf_tensor(f"{name}_ffn1", shape, dtype))

        xn = sb("xn", [S, 2, GB, D])
        xt = sb("xt", [D, 2, GT])
        base = sb("xn_and_bias", [S, 2, GB, D])
        up, down = sb("w_up", [D, F0]), sb("w_down", [128, chunks, D])
        b1 = sb("b1_columns", [128, chunks])
        row_b2, row_gamma, row_beta = (sb(n, [S, D]) for n in ("b2_row", "gamma_row", "beta_row"))
        hid = sb("hidden", [128, 2, chunks, GT])
        z = sb("z", [S, 2, GB, D])
        zst = sb("z_stats", [S, GB, 6])
        mean2, halves, var, sd, rstd, shift = (sb(n, [S, GB]) for n in ("z_mean2", "z_halves", "z_var", "z_sd", "z_rstd", "z_shift"))
        with nc.Block() as block:
            @block.sync
            def _(sync):
                for to, of in ((up[:, :], a["L1_ffn_w1"][0]), (down[:, :, :], a["L1_ffn_w2"][0].rearrange("(c f) d -> f c d", f=128)),
                               *((b1[:, c:c + 1], column_of(a["L1_ffn_b1"][0, c * 128:(c + 1) * 128])) for c in range(chunks)), (row_b2[:, :], row_of(a["L1_ffn_b2"][0])),
                               (row_gamma[:, :], row_of(a["L1_ffn_gamma"])), (row_beta[:, :], row_of(a["L1_ffn_beta"]))):
                    sync.dma_start(to, of).then_inc(s["loaded"], 16)

            @block.gpsimd
            def _(pool):
                clear(pool)
                pool.wait_ge(s["rows_ready"], 2)

                def step(g, par, front, middle, back):
                    nxt = 1 - par
                    wide = [S, GB, D]
                    if front:
                        wait(pool, s["xn_ready"], g + 2)
                        wait(pool, s["z_ready"], g)
                        nc.gpsimd.tensor_tensor(base[:, nxt, :, :], xn[:, nxt, :, :], row_b2[:, :].unsqueeze(1).to_broadcast(wide),
                                                ALU.add).then_inc(s["base_ready"], 1)
                    if back:
                        zv, xv = z[:, nxt, :, :], m.x[:, bass.ds((g - 1) * GB, GB), :]
                        wait(pool, s["zn_ready"], g)
                        nc.gpsimd.tensor_tensor(zv, zv, row_gamma[:, :].unsqueeze(1).to_broadcast(wide), ALU.mult).then_inc(s["scaled"], 1)
                        wait(pool, s["scaled"], g)
                        nc.gpsimd.tensor_tensor(zv, zv, row_beta[:, :].unsqueeze(1).to_broadcast(wide), ALU.add).then_inc(s["moved"], 1)
                        wait(pool, s["moved"], g)
                        nc.gpsimd.tensor_tensor(xv, xv, zv, ALU.add).then_inc(s["x_done"], 1)

                pipeline(pool, step, NGB)

            @block.scalar
            def _(act):
                act.wait_ge(s["var_ready"], 1)
                nc.scalar.activation(m.sd[:, :], m.var[:, :], ACT.Sqrt, bias=m.eps[:, 0:1]).then_inc(s["sd_ready"], 1)
                act.wait_ge(s["loaded"], 16 * 9)

                def step(g, par, front, middle, back):
                    nxt = 1 - par
                    if middle:
                        wait(act, s["y_done"], g - 1)
                        for c in range(chunks):
                            wait(act, s["hidden_in_psum"], g * chunks + c + 1)
                            nc.scalar.activation(hid[:, par, c, :], m.psum[:, c, :], ACT.Relu, bias=b1[:, c:c + 1]).then_inc(s["hidden_ready"], 1)
                    if front:
                        wait(act, s["xt_in_psum"], g + 2)
                        nc.scalar.copy(xt[:, nxt, :], m.psum[:, 5, :]).then_inc(s["xt_ready"], 1)
                    if back:
                        wait(act, s["z_var_ready"], g)
                        nc.scalar.activation(sd[:, :], var[:, :], ACT.Sqrt, bias=m.eps[:, 0:1]).then_inc(s["z_sd_ready"], 1)

                pipeline(act, step, NGB)

            @block.vector
            def _(dve):
                variance_of_x(nc, m, dve, s["parts_ready"], s["var_ready"])
                dve.wait_ge(s["loaded"], 16 * 9)
                gate = m.gate[:, 5:6]
                nc.vector.tensor_scalar(row_gamma[:, :], row_gamma[:, :], gate, None, ALU.mult).then_inc(s["rows_ready"], 1)
                nc.vector.tensor_scalar(row_beta[:, :], row_beta[:, :], gate, None, ALU.mult).then_inc(s["rows_ready"], 1)
                rstd_of_x(nc, m, dve, s["sd_ready"], s["rstd_ready"], s["shift_ready"])

                def step(g, par, front, middle, back):
                    nxt = 1 - par
                    if front:
                        wait(dve, s["xt_in_psum"], g)
                        wait(dve, s["base_ready"], g)
                        for t in range(GB):
                            at = (g + 1) * GB + t
                            ins = nc.vector.tensor_scalar(xn[:, nxt, t, :], m.x[:, at, :], m.rstd[:, bass.ds(at, 1)],
                                                          m.shift[:, bass.ds(at, 1)], ALU.mult, ALU.add)
                        ins.then_inc(s["xn_ready"], 1)
                    if back:
                        link = chain(dve, s["link"], g - 1, LINKS)
                        wait(dve, s["y_done"], g)
                        wait(dve, s["base_ready"], g)
                        wait(dve, s["x_done"], g - 2)
                        zv = z[:, nxt, :, :]
                        nc.vector.tensor_tensor(zv, m.psum[:, 4, :].rearrange("p (t d) -> p t d", d=D), base[:, nxt, :, :],
                                                ALU.add).then_inc(s["z_ready"], 1)
                        wait(dve, s["z_ready"], g)
                        for t in range(GB):
                            ins = nc.vector.bn_stats(zst[:, t, :], zv[:, t, :])
                        link(ins)
                        me, qe, mo, qo = (zst[:, :, c] for c in (1, 2, 4, 5))
                        nc.vector.tensor_tensor(mean2[:, :], me, mo, ALU.add)
                        link(nc.vector.tensor_tensor(halves[:, :], me, mo, ALU.subtract))
                        link(nc.vector.tensor_tensor(var[:, :], qe, qo, ALU.add))
                        link(nc.vector.scalar_tensor_tensor(halves[:, :], halves[:, :], 0.25, halves[:, :], ALU.mult, ALU.mult))
                        nc.vector.scalar_tensor_tensor(var[:, :], var[:, :], 1.0 / D, halves[:, :], ALU.mult, ALU.add)\
                            .then_inc(s["z_var_ready"], 1)
                        wait(dve, s["z_sd_ready"], g)
                        link(nc.vector.reciprocal(rstd[:, :], sd[:, :]))
                        link(nc.vector.scalar_tensor_tensor(shift[:, :], mean2[:, :], -0.5, rstd[:, :], ALU.mult, ALU.mult))
                        for t in range(GB):
                            ins = nc.vector.tensor_scalar(zv[:, t, :], zv[:, t, :], rstd[:, t:t + 1], shift[:, t:t + 1], ALU.mult, ALU.add)
                        ins.then_inc(s["zn_ready"], 1)

                pipeline(dve, step, NGB)
                dve.wait_ge(s["x_done"], NGB)
                for b in range(B):
                    nc.vector.bn_stats(m.moments[:, b, :], m.x[:, b, :])

            @block.tensor
            def _(pe):
                pe.wait_ge(s["loaded"], 16 * 9)

                def step(g, par, front, middle, back):
                    nxt = 1 - par
                    if middle:
                        wait(pe, s["xt_ready"], g + 1)
                        wait(pe, s["hidden_ready"], g * chunks)
                        for c in range(chunks):
                            nc.tensor.matmul(m.psum[:, c, :], up[:, c * 128:(c + 1) * 128], xt[:, par, :], start=True, stop=True)\
                                .then_inc(s["hidden_in_psum"], 1)
                    if back:
                        wait(pe, s["hidden_ready"], g * chunks)
                        wait(pe, s["z_ready"], g - 1)
                        for t in range(GB):
                            for c in range(chunks):
                                mm = nc.tensor.matmul(m.psum[:, 4, t * D:(t + 1) * D], hid[:, nxt, c, t * S:(t + 1) * S], down[:, c, :],
                                                      start=(c == 0), stop=(c == chunks - 1))
                        mm.then_inc(s["y_done"], 1)
                    if front:
                        wait(pe, s["xn_ready"], g + 2)
                        wait(pe, s["xt_ready"], g + 1)
                        for t in range(GB):
                            mm = nc.tensor.transpose(m.psum[:, 5, t * S:(t + 1) * S], xn[:, nxt, t, :], m.ident[:, :])
                        mm.then_inc(s["xt_in_psum"], 1)

                pipeline(pe, step, NGB)


def controller_feed_forward(nc, m, sem, clear):
    names = ("parts_ready var_ready sd_ready rstd_ready shift_ready loaded ones_ready row_ready xn_ready xt_in_psum xt_ready "
             "low_in_psum low_ready logits_in_psum bias_added picked_ready coded full_read rt_in_psum rt_ready y_done x_done link")
    s = {n: sem(f"{n}_ffn2") for n in names.split()}
    gate = m.gate[:, 6:7]
    a = m.a
    LINKS = 3
    HID = MX * MY
    CH = HID // 128
    with ExitStack() as ctx:
        def sb(name, shape, dtype=F32):
            return ctx.enter_context(nc.sbuf_tensor(f"{name}_ffn2", shape, dtype))

        xn = sb("xn", [S, 2, D])
        xt = sb("xt", [D, 2, S])
        low = sb("low_rank", [ML + 1, 2, S])
        m1, m2 = sb("m1", [D, ML]), sb("m2_and_mb", [ML + 1, HID])
        w1, w2 = sb("w1", [D, HID]), sb("w2", [128, CH, D])
        row_b2 = sb("b2_row", [S, D])
        top = sb("top_logit", [S, MX])
        code = sb("pick_code", [S, MX])
        pick = sb("pick", [S, 2, MX, MY])
        rt = sb("picked_transposed", [128, CH * S])
        with nc.Block() as block:
            @block.sync
            def _(sync):
                loads = [(m1[:, :], a["L2_ffn_m1"]), (m2[0:ML, :], a["L2_ffn_m2"].rearrange("l x y -> l (x y)")),
                         (m2[ML:ML + 1, :], a["L2_ffn_mb"].rearrange("(o x) y -> o (x y)", o=1)),
                         (w1[:, :], a["L2_ffn_w1"].rearrange("d x y -> d (x y)")), (row_b2[:, :], row_of(a["L2_ffn_b2"]))]
                w2_blocks = a["L2_ffn_w2"].rearrange("y (c i) d -> i y c d", i=2)
                loads += [(w2[i * MY:(i + 1) * MY, :, :], w2_blocks[i]) for i in range(2)]
                for to, of in loads:
                    sync.dma_start(to, of).then_inc(s["loaded"], 16)

            @block.gpsimd
            def _(pool):
                clear(pool)
                nc.gpsimd.memset(low[ML:ML + 1, :, :], 1.0).then_inc(s["ones_ready"], 1)
                pool.wait_ge(s["ones_ready"], 1)
                pool.wait_ge(s["row_ready"], 1)

                def step(b, par, front, middle, back):
                    if front:
                        wait(pool, s["xn_ready"], b + 2)
                        nc.gpsimd.tensor_tensor(m.x[:, b + 1, :], m.x[:, b + 1, :], row_b2[:, :], ALU.add).then_inc(s["bias_added"], 1)
                    if middle:
                        wait(pool, s["picked_ready"], b + 1)
                        pv = pick[:, par, :, :]
                        nc.gpsimd.tensor_tensor(pv, pv, m.down[:, 0:MY].unsqueeze(1).to_broadcast([S, MX, MY]), ALU.mult).then_inc(s["coded"], 1)

                pipeline(pool, step)

            @block.scalar
            def _(act):
                act.wait_ge(s["var_ready"], 1)
                nc.scalar.activation(m.sd[:, :], m.var[:, :], ACT.Sqrt, bias=m.eps[:, 0:1]).then_inc(s["sd_ready"], 1)

                def step(b, par, front, middle, back):
                    nxt = 1 - par
                    if front:
                        wait(act, s["xt_in_psum"], b + 2)
                        wait(act, s["logits_in_psum"], b)
                        nc.scalar.copy(xt[:, nxt, :], m.psum[:, 0, 0:S]).then_inc(s["xt_ready"], 1)
                        wait(act, s["low_in_psum"], b + 2)
                        nc.scalar.copy(low[0:ML, nxt, :], m.psum[0:ML, 0, S:2 * S]).then_inc(s["low_ready"], 1)
                    if back:
                        wait(act, s["rt_in_psum"], b)
                        wait(act, s["y_done"], b - 1)
                        nc.scalar.copy(rt[:, :], m.psum[:, 5, :]).then_inc(s["rt_ready"], 1)

                pipeline(act, step)

            @block.vector
            def _(dve):
                variance_of_x(nc, m, dve, s["parts_ready"], s["var_ready"])
                rstd_of_x(nc, m, dve, s["sd_ready"], s["rstd_ready"], s["shift_ready"])
                dve.wait_ge(s["loaded"], 16 * 7)
                nc.vector.tensor_scalar(row_b2[:, :], row_b2[:, :], gate, None, ALU.mult).then_inc(s["row_ready"], 1)
                wide = [S, MX, MY]

                def step(b, par, front, middle, back):
                    nxt = 1 - par
                    link = chain(dve, s["link"], b, LINKS)
                    pv = pick[:, par, :, :]
                    if front:
                        wait(dve, s["xt_in_psum"], b)
                        nc.vector.tensor_scalar(xn[:, nxt, :], m.x[:, b + 1, :], m.rstd[:, bass.ds(b + 1, 1)],
                                                m.shift[:, bass.ds(b + 1, 1)], ALU.mult, ALU.add).then_inc(s["xn_ready"], 1)
                    if middle:
                        wait(dve, s["logits_in_psum"], b + 1)
                        logits = m.psum[:, 1 + par, :].rearrange("p (x y) -> p x y", y=MY)
                        link(nc.vector.tensor_reduce(top[:, :], logits, AX.X, ALU.max))
                        wait(dve, s["rt_in_psum"], b - 1)
                        nc.vector.tensor_tensor(pv, logits, top[:, :].unsqueeze(2).to_broadcast(wide), ALU.is_ge).then_inc(s["picked_ready"], 1)
                    if back:
                        wait(dve, s["y_done"], b)
                        wait(dve, s["bias_added"], b)
                        nc.vector.scalar_tensor_tensor(m.x[:, b - 1, :], m.psum[:, 6, 0:D], gate, m.x[:, b - 1, :],
                                                       ALU.mult, ALU.add).then_inc(s["x_done"], 1)
                    if middle:
                        wait(dve, s["coded"], b + 1)
                        if back:
                            wait(dve, s["x_done"], b)
                        link(nc.vector.tensor_reduce(code[:, :], pv, AX.X, ALU.max))
                        link(nc.vector.tensor_tensor(pv, pv, code[:, :].unsqueeze(2).to_broadcast(wide), ALU.is_equal))
                        nc.vector.scalar_tensor_tensor(pv.rearrange("p x y -> p (x y)"), m.psum[:, 3 + par, :], 0.0,
                                                       pv.rearrange("p x y -> p (x y)"), ALU.max, ALU.mult).then_inc(s["full_read"], 1)
                    if back:
                        if not middle:
                            wait(dve, s["x_done"], b)
                        nc.vector.bn_stats(m.moments[:, b - 1, :], m.x[:, b - 1, :])

                pipeline(dve, step)

            @block.tensor
            def _(pe):
                pe.wait_ge(s["loaded"], 16 * 7)
                pe.wait_ge(s["ones_ready"], 1)

                def step(b, par, front, middle, back):
                    nxt = 1 - par
                    if front:
                        wait(pe, s["xn_ready"], b + 2)
                        wait(pe, s["low_ready"], b + 1)
                        nc.tensor.transpose(m.psum[:, 0, 0:S], xn[:, nxt, :], m.ident[:, :]).then_inc(s["xt_in_psum"], 1)
                    if middle:
                        wait(pe, s["low_ready"], b + 1)
                        wait(pe, s["full_read"], b - 1)
                        nc.tensor.matmul(m.psum[:, 1 + par, :], low[:, par, :], m2[:, :], start=True, stop=True)
                        nc.tensor.matmul(m.psum[:, 3 + par, :], xt[:, par, :], w1[:, :], start=True, stop=True).then_inc(s["logits_in_psum"], 1)
                    if front:
                        wait(pe, s["xt_ready"], b + 2)
                        nc.tensor.matmul(m.psum[0:ML, 0, S:2 * S], m1[:, :], xt[:, nxt, :], start=True, stop=True).then_inc(s["low_in_psum"], 1)
                    if back:
                        wait(pe, s["full_read"], b)
                        wait(pe, s["rt_ready"], b - 1)
                        for c in range(CH):
                            mm = nc.tensor.transpose(m.psum[:, 5, c * S:(c + 1) * S],
                                                     pick[:, nxt, :, :].rearrange("p x y -> p (x y)")[:, c * 128:(c + 1) * 128], m.ident[:, :])
                        mm.then_inc(s["rt_in_psum"], 1)
                        wait(pe, s["rt_ready"], b)
                        wait(pe, s["x_done"], b - 1)
                        for c in range(CH):
                            mm = nc.tensor.matmul(m.psum[:, 6, 0:D], rt[:, c * S:(c + 1) * S], w2[:, c, :], start=(c == 0), stop=(c == CH - 1))
                        mm.then_inc(s["y_done"], 1)

                pipeline(pe, step)


def latent_attention(nc, m, sem, clear):
    names = ("parts_ready var_ready sd_ready rstd_ready shift_ready loaded ctx_parts ctx_var ctx_sd ctx_rstd ctx_shift "
             "lat_var lat_sd lat_rstd lat_scale lat_shift "
             "prep_psum prep_read rows_ready cn_raw cn_scaled cn_ready ln_raw ln_scaled ln_ready kvt_in_psum kvt_ready "
             "q_in_psum q_ready scores_done negmax_ready shifted exp_ready sum_ready recip_ready probs_ready pt_in_psum "
             "pt_read_act pt_read_dve c_in_psum c_ready y_done x_done bias_added w_ready kept")
    s = {n: sem(f"{n}_3") for n in names.split()}
    gate = m.gate[:, 3:4]
    a = m.a
    SCALE = D ** -0.5
    with ExitStack() as ctx:
        def sb(name, shape, dtype=F32):
            return ctx.enter_context(nc.sbuf_tensor(f"{name}_xattn3", shape, dtype))

        wq, wkv, wo = sb("wq", [D, H3 * D]), sb("wkv", [D, 2, H3 * D]), sb("wo", [D, H3, D])
        b_rows = sb("bias_rows", [H3, 2, D])
        b_cols = sb("bias_columns", [D, 2, H3])
        bv_wide = sb("bv_wide", [D, H3, S])
        w_t = sb("weights_transposed", [D, 3, H3, D])
        w_qk, w_vo = sb("w_qk", [D, H3, D]), sb("w_vo", [D, H3, D])
        t0 = sb("key_weights_times_bq", [D, H3])
        row_out = sb("output_bias_row", [S, D])
        rows = sb("norm_rows", [S, 4, D])
        c_moments = sb("context_moments", [KC, B, 6])
        c_mean2, c_half, c_var, c_sd, c_rstd, c_shift = (sb(f"context_{n}", [KC, B]) for n in ("mean2", "half", "var", "sd", "rstd", "shift"))
        l_var, l_sd, l_scale, l_shift = (sb(f"latent_{n}", [S, B]) for n in ("var", "sd", "scale", "shift"))
        kn = sb("kv_before_beta", [S, 2, 2, D])
        kv = sb("kv", [S, 2, 2, D])
        kept = sb("kv_kept", [S, 2, 2, D])
        kvt = sb("kv_transposed", [D, 2, KV])
        q = sb("queries", [D, 2, H3, S])
        e = sb("exp_scores", [S, 2, H3, KV])
        negmax = sb("negated_max", [S, 2, H3], BF16)
        total, recip = sb("softmax_sum", [S, 2, H3]), sb("softmax_recip", [S, 2, H3])
        ptc, ptl = sb("probs_t_context", [KC, H3 * S]), sb("probs_t_latents", [S, H3 * S])
        c = sb("heads_out", [D, H3, S])
        HB = 2
        HH = 4
        PREP = 3 * H3 // 4 + 1
        with nc.Block() as block:
            @block.sync
            def _(sync):
                loads = [(wq[:, :], a["L3_xattn_Wq"]), (wkv[:, :, :], a["L3_xattn_Wkv"].rearrange("d (t n) -> d t n", t=2)),
                         (wo[:, :, :], a["L3_xattn_Wo"].rearrange("(h c) d -> c h d", c=D)),
                         (b_rows[:, 0, :], a["L3_xattn_bq"].rearrange("(h c) -> h c", c=D)),
                         (b_rows[:, 1, :], a["L3_xattn_bkv"][H3 * D:2 * H3 * D].rearrange("(h c) -> h c", c=D)),
                         (row_out[:, :], row_of(a["L3_xattn_bo"]))]
                loads += [(rows[:, i, :], row_of(a[f"L3_xattn_{n}"])) for i, n in enumerate(("gamma_media", "beta_media", "gamma_lat", "beta_lat"))]
                for to, of in loads:
                    sync.dma_start(to, of).then_inc(s["loaded"], 16)

            LOADED = 16 * 10

            @block.gpsimd
            def _(pool):
                clear(pool)
                pool.wait_ge(s["loaded"], LOADED)
                pool.wait_ge(s["rows_ready"], 1)

                def step(b, par, front, middle, back):
                    nxt = 1 - par
                    if front:
                        for part, raw, scaled, ready, n in ((0, "cn_raw", "cn_scaled", "cn_ready", KC), (1, "ln_raw", "ln_scaled", "ln_ready", S)):
                            t = kn[0:n, nxt, part, :]
                            wait(pool, s[raw], b + 2)
                            nc.gpsimd.tensor_tensor(t, t, rows[0:n, 2 * part, :], ALU.mult).then_inc(s[scaled], 1)
                            wait(pool, s[scaled], b + 2)
                            nc.gpsimd.tensor_tensor(kv[0:n, nxt, part, :], t, rows[0:n, 2 * part + 1, :], ALU.add).then_inc(s[ready], 1)
                        nc.gpsimd.tensor_tensor(m.x[:, b + 1, :], m.x[:, b + 1, :], row_out[:, :], ALU.add).then_inc(s["bias_added"], 1)
                    if middle:
                        wait(pool, s["c_in_psum"], (b - 1) * 2)
                        nc.gpsimd.tensor_tensor(kept[0:KC, par, 0, :], kn[0:KC, par, 0, :], rows[0:KC, 1, :], ALU.add).then_inc(s["kept"], 1)
                        nc.gpsimd.tensor_tensor(kept[:, par, 1, :], kn[:, par, 1, :], rows[:, 3, :], ALU.add).then_inc(s["kept"], 1)
                        wait(pool, s["recip_ready"], b + 1)
                        ev = e[:, par, :, :]
                        nc.gpsimd.tensor_tensor(ev, ev, recip[:, par, :].unsqueeze(2).to_broadcast([S, H3, KV]), ALU.mult).then_inc(s["probs_ready"], 1)

                pipeline(pool, step)

            @block.scalar
            def _(act):
                act.wait_ge(s["var_ready"], 1)
                nc.scalar.activation(m.sd[:, :], m.var[:, :], ACT.Sqrt, bias=m.eps[:, 0:1]).then_inc(s["sd_ready"], 1)
                act.wait_ge(s["lat_var"], 1)
                nc.scalar.activation(l_sd[:, :], l_var[:, :], ACT.Sqrt, bias=m.eps[:, 0:1]).then_inc(s["lat_sd"], 1)
                act.wait_ge(s["ctx_var"], 1)
                nc.scalar.activation(c_sd[:, :], c_var[:, :], ACT.Sqrt, bias=m.eps[0:KC, 0:1]).then_inc(s["ctx_sd"], 1)
                for n in range(PREP - 1):
                    act.wait_ge(s["prep_psum"], n + 1)
                    nc.scalar.copy(w_t[:, n // 2, HH * (n % 2):HH * (n % 2) + HH, :].rearrange("p h c -> p (h c)"), m.psum[:, n, :]).then_inc(s["prep_read"], 1)
                act.wait_ge(s["prep_psum"], PREP + 1)
                nc.scalar.copy(w_qk[:, :, :].rearrange("p (n h) c -> p n (h c)", n=2), m.psum[:, 0:2, :]).then_inc(s["w_ready"], 1)
                act.wait_ge(s["prep_psum"], PREP + 2)
                nc.scalar.copy(w_vo[:, :, :].rearrange("p (n h) c -> p n (h c)", n=2), m.psum[:, 2:4, :]).then_inc(s["w_ready"], 1)

                def step(b, par, front, middle, back):
                    nxt = 1 - par
                    if front:
                        wait(act, s["kvt_in_psum"], b + 2)
                        wait(act, s["scores_done"], b)
                        nc.scalar.copy(kvt[:, nxt, :], m.psum[:, 7, 0:KV]).then_inc(s["kvt_ready"], 1)
                    if back:
                        wait(act, s["c_in_psum"], (b - 1) * 2)
                        wait(act, s["pt_in_psum"], (b - 1) * 4 + 1)
                        nc.scalar.copy(ptc[:, 0:512], m.psum[0:KC, 6, :]).then_inc(s["pt_read_act"], 1)
                        wait(act, s["pt_in_psum"], (b - 1) * 4 + 3)
                        nc.scalar.copy(ptl[:, 0:512], m.psum[:, 5, :]).then_inc(s["pt_read_act"], 1)
                    if middle:
                        wait(act, s["shifted"], b + 1)
                        wait(act, s["pt_in_psum"], (b - 1) * 4)
                        nc.scalar.activation(e[:, par, :, :].rearrange("p (n h) k -> p n (h k)", h=HB), m.psum[:, 0:4, 0:HB * KV],
                                             ACT.Exp, scale=SCALE).then_inc(s["exp_ready"], 1)
                    if back:
                        for n in range(2):
                            wait(act, s["y_done"], b - 1)
                            wait(act, s["c_in_psum"], (b - 1) * 2 + n + 1)
                            nc.scalar.copy(c[:, n * HH:(n + 1) * HH, :].rearrange("p h t -> p (h t)"), m.psum[:, 4 + n, :]).then_inc(s["c_ready"], 1)

                pipeline(act, step)

            @block.vector
            def _(dve):
                variance_of_x(nc, m, dve, s["parts_ready"], s["var_ready"])
                for b in range(B):
                    nc.vector.bn_stats(c_moments[:, b, :], m.ctx[:, b, :])
                rstd_of_x(nc, m, dve, s["sd_ready"], s["rstd_ready"], s["shift_ready"])
                nc.vector.tensor_tensor(l_var[:, :], m.rstd[:, :], m.rstd[:, :], ALU.mult).then_inc(s["lat_scale"], 1)
                dve.wait_ge(s["lat_scale"], 1)
                nc.vector.tensor_tensor(l_var[:, :], l_var[:, :], m.var[:, :], ALU.mult).then_inc(s["lat_var"], 1)
                me, qe, mo, qo = (c_moments[:, :, k] for k in (1, 2, 4, 5))
                dve.wait_ge(s["lat_var"], 1)
                nc.vector.tensor_tensor(c_mean2[:, :], me, mo, ALU.add).then_inc(s["ctx_parts"], 1)
                nc.vector.tensor_tensor(c_half[:, :], me, mo, ALU.subtract).then_inc(s["ctx_parts"], 1)
                nc.vector.tensor_tensor(c_var[:, :], qe, qo, ALU.add).then_inc(s["ctx_parts"], 1)
                dve.wait_ge(s["ctx_parts"], 3)
                nc.vector.scalar_tensor_tensor(c_half[:, :], c_half[:, :], 0.25, c_half[:, :], ALU.mult, ALU.mult).then_inc(s["ctx_parts"], 1)
                dve.wait_ge(s["ctx_parts"], 4)
                nc.vector.scalar_tensor_tensor(c_var[:, :], c_var[:, :], 1.0 / D, c_half[:, :], ALU.mult, ALU.add).then_inc(s["ctx_var"], 1)
                dve.wait_ge(s["lat_sd"], 1)
                nc.vector.reciprocal(l_scale[:, :], l_sd[:, :]).then_inc(s["lat_rstd"], 1)
                dve.wait_ge(s["lat_rstd"], 1)
                nc.vector.tensor_tensor(l_shift[:, :], l_scale[:, :], m.shift[:, :], ALU.mult).then_inc(s["lat_shift"], 1)
                nc.vector.tensor_tensor(l_scale[:, :], l_scale[:, :], m.rstd[:, :], ALU.mult).then_inc(s["lat_shift"], 1)
                dve.wait_ge(s["ctx_sd"], 1)
                nc.vector.reciprocal(c_rstd[:, :], c_sd[:, :]).then_inc(s["ctx_rstd"], 1)
                dve.wait_ge(s["ctx_rstd"], 1)
                nc.vector.scalar_tensor_tensor(c_shift[:, :], c_mean2[:, :], -0.5, c_rstd[:, :], ALU.mult, ALU.mult).then_inc(s["ctx_shift"], 1)
                dve.wait_ge(s["ctx_shift"], 1)
                dve.wait_ge(s["lat_shift"], 2)
                dve.wait_ge(s["prep_psum"], PREP)
                nc.vector.tensor_copy(b_cols[:, :, :].rearrange("p t h -> p (t h)"), m.psum[:, 6, 0:2 * H3]).then_inc(s["prep_read"], 1)
                dve.wait_ge(s["prep_read"], PREP)
                nc.vector.tensor_copy(bv_wide[:, :, :], b_cols[:, 1, :].unsqueeze(2).to_broadcast([D, H3, S])).then_inc(s["prep_read"], 1)
                dve.wait_ge(s["prep_psum"], PREP + 3)
                nc.vector.tensor_copy(t0[:, :], m.psum[:, 4, 0:H3]).then_inc(s["w_ready"], 1)
                nc.vector.tensor_tensor(row_out[:, :], row_out[:, :], m.psum[:, 5, 0:D], ALU.add).then_inc(s["w_ready"], 1)
                dve.wait_ge(s["w_ready"], 4)
                nc.vector.tensor_scalar(row_out[:, :], row_out[:, :], gate, None, ALU.mult).then_inc(s["rows_ready"], 1)

                def step(b, par, front, middle, back):
                    nxt = 1 - par
                    if front:
                        wait(dve, s["kvt_in_psum"], b)
                        wait(dve, s["kept"], b * 2)
                        nc.vector.tensor_scalar(kn[0:KC, nxt, 0, :], m.ctx[:, b + 1, :], c_rstd[:, bass.ds(b + 1, 1)],
                                                c_shift[:, bass.ds(b + 1, 1)], ALU.mult, ALU.add).then_inc(s["cn_raw"], 1)
                        nc.vector.tensor_scalar(kn[:, nxt, 1, :], m.x[:, b + 1, :], l_scale[:, bass.ds(b + 1, 1)],
                                                l_shift[:, bass.ds(b + 1, 1)], ALU.mult, ALU.add).then_inc(s["ln_raw"], 1)

                def middle_one(b, par):
                    wait(dve, s["scores_done"], b + 1)
                    wait(dve, s["shifted"], b - 1)
                    sv = m.psum[:, 0:4, 0:HB * KV].rearrange("p n (h k) -> p n h k", h=HB)
                    nc.vector.tensor_reduce(negmax[:, par, :].rearrange("p (n h) -> p n h", h=HB), sv, AX.X, ALU.max, negate=True).then_inc(s["negmax_ready"], 1)

                def full(b, par, front, middle, back):
                    nxt = 1 - par
                    step(b, par, front, middle, back)
                    if middle:
                        middle_one(b, par)
                    if back:
                        wait(dve, s["c_in_psum"], (b - 1) * 2)
                        wait(dve, s["pt_in_psum"], (b - 1) * 4 + 2)
                        nc.vector.tensor_copy(ptc[:, 512:1024], m.psum[0:KC, 4, :]).then_inc(s["pt_read_dve"], 1)
                        wait(dve, s["pt_in_psum"], (b - 1) * 4 + 4)
                        nc.vector.tensor_copy(ptl[:, 512:1024], m.psum[:, 6, :]).then_inc(s["pt_read_dve"], 1)
                    if middle:
                        wait(dve, s["exp_ready"], b + 1)
                        nc.vector.tensor_reduce(total[:, par, :], e[:, par, :, :], AX.X, ALU.add).then_inc(s["sum_ready"], 1)
                        wait(dve, s["sum_ready"], b + 1)
                        wait(dve, s["probs_ready"], b - 1)
                        nc.vector.reciprocal(recip[:, par, :], total[:, par, :]).then_inc(s["recip_ready"], 1)
                    if front:
                        for n in range(2):
                            wait(dve, s["q_in_psum"], (b + 1) * 2 + n + 1)
                            wait(dve, s["scores_done"], b)
                            nc.vector.tensor_tensor(q[:, nxt, n * HH:(n + 1) * HH, :], m.psum[:, 4 + n, :].rearrange("p (h t) -> p h t", h=HH),
                                                    t0[:, n * HH:(n + 1) * HH].unsqueeze(2).to_broadcast([D, HH, S]), ALU.add).then_inc(s["q_ready"], 1)
                    if back:
                        wait(dve, s["y_done"], b)
                        wait(dve, s["bias_added"], b)
                        nc.vector.scalar_tensor_tensor(m.x[:, b - 1, :], m.psum[:, 7, 256:256 + D], gate, m.x[:, b - 1, :],
                                                       ALU.mult, ALU.add).then_inc(s["x_done"], 1)

                pipeline(dve, full)
                dve.wait_ge(s["x_done"], B)
                for b in range(B):
                    nc.vector.bn_stats(m.moments[:, b, :], m.x[:, b, :])

            @block.tensor
            def _(pe):
                pe.wait_ge(s["loaded"], LOADED)
                for n in range(PREP - 1):
                    for h in range(HH):
                        head = HH * (n % 2) + h
                        w = wq[:, head * D:(head + 1) * D] if n < 2 else wkv[:, n // 2 - 1, head * D:(head + 1) * D]
                        mm = nc.tensor.transpose(m.psum[:, n, h * D:(h + 1) * D], w, m.ident[:, :])
                    mm.then_inc(s["prep_psum"], 1)
                for t in range(2):
                    mm = nc.tensor.transpose(m.psum[:, 6, t * H3:(t + 1) * H3], b_rows[:, t, :], m.ident[0:H3, 0:H3])
                mm.then_inc(s["prep_psum"], 1)
                pe.wait_ge(s["prep_read"], PREP + 1)
                for h in range(H3):
                    mm = nc.tensor.matmul(m.psum[:, h // HH, (h % HH) * D:(h % HH + 1) * D], w_t[:, 0, h, :], w_t[:, 1, h, :], start=True, stop=True)
                mm.then_inc(s["prep_psum"], 1)
                for h in range(H3):
                    mm = nc.tensor.matmul(m.psum[:, 2 + h // HH, (h % HH) * D:(h % HH + 1) * D], w_t[:, 2, h, :], wo[:, h, :], start=True, stop=True)
                mm.then_inc(s["prep_psum"], 1)
                for h in range(H3):
                    nc.tensor.matmul(m.psum[:, 4, h:h + 1], w_t[:, 1, h, :], b_cols[:, 0, h:h + 1], start=True, stop=True)
                for h in range(H3):
                    mm = nc.tensor.matmul(m.psum[:, 5, 0:D], bv_wide[:, h, :], wo[:, h, :], start=(h == 0), stop=(h == H3 - 1))
                mm.then_inc(s["prep_psum"], 1)
                pe.wait_ge(s["w_ready"], 4)

                def step(b, par, front, middle, back):
                    nxt = 1 - par
                    if middle:
                        wait(pe, s["q_ready"], (b + 1) * 2)
                        wait(pe, s["exp_ready"], b)
                        for h in range(H3):
                            mm = nc.tensor.matmul(m.psum[:, h // HB, (h % HB) * KV:(h % HB + 1) * KV], q[:, par, h, :], kvt[:, par, :],
                                                  start=(h % HB == 0), stop=True, skip_group_check=True)
                        mm.then_inc(s["scores_done"], 1)
                    if front:
                        wait(pe, s["cn_ready"], b + 2)
                        wait(pe, s["ln_ready"], b + 2)
                        wait(pe, s["kvt_ready"], b + 1)
                        wait(pe, s["x_done"], b - 1)
                        nc.tensor.transpose(m.psum[:, 7, 0:KC], kv[0:KC, nxt, 0, :], m.ident[0:KC, 0:KC])
                        nc.tensor.transpose(m.psum[:, 7, KC:KV], kv[:, nxt, 1, :], m.ident[:, :]).then_inc(s["kvt_in_psum"], 1)
                    if back:
                        wait(pe, s["probs_ready"], b)
                        wait(pe, s["q_ready"], b * 2) if not middle else None
                        wait(pe, s["c_ready"], (b - 1) * 2)
                        for n, (bank, keys, half) in enumerate(((6, 0, 0), (4, 0, 1), (5, 1, 0), (6, 1, 1))):
                            k0, k1 = (0, KC) if keys == 0 else (KC, KV)
                            if n == 0:
                                wait(pe, s["pt_read_dve"], (b - 1) * 2)
                            if n == 3:
                                wait(pe, s["pt_read_act"], (b - 1) * 2 + 1)
                            for h in range(HH):
                                mm = nc.tensor.transpose(m.psum[0:k1 - k0, bank, h * S:(h + 1) * S], e[:, nxt, half * HH + h, k0:k1], m.ident[:, :])
                            mm.then_inc(s["pt_in_psum"], 1)
                    if middle:
                        wait(pe, s["negmax_ready"], b + 1)
                        for n in range(4):
                            mm = nc.tensor.matmul(m.psum[:, n, 0:HB * KV].rearrange("p (h k) -> p h k", k=KV), m.ident_bf[:, :],
                                                  negmax[:, par, n * HB:(n + 1) * HB].unsqueeze(2).to_broadcast([S, HB, KV]),
                                                  start=False, stop=True, skip_group_check=True)
                        mm.then_inc(s["shifted"], 1)
                    if back:
                        wait(pe, s["pt_read_act"], b * 2)
                        wait(pe, s["pt_read_dve"], b * 2)
                        wait(pe, s["kept"], b * 2)
                        for half in range(2):
                            cols = slice(half * 512, (half + 1) * 512)
                            nc.tensor.matmul(m.psum[:, 4 + half, :], kept[0:KC, nxt, 0, :], ptc[:, cols], start=True, stop=False)
                            nc.tensor.matmul(m.psum[:, 4 + half, :], kept[:, nxt, 1, :], ptl[:, cols], start=False, stop=True).then_inc(s["c_in_psum"], 1)
                        wait(pe, s["c_ready"], b * 2)
                        wait(pe, s["kvt_ready"], b + 2) if front else None
                        for h in range(H3):
                            mm = nc.tensor.matmul(m.psum[:, 7, 256:256 + D], c[:, h, :], w_vo[:, h, :], start=(h == 0), stop=(h == H3 - 1))
                        mm.then_inc(s["y_done"], 1)
                    if front:
                        wait(pe, s["kvt_ready"], b + 2)
                        for n in range(2):
                            for h in range(HH):
                                mm = nc.tensor.matmul(m.psum[:, 4 + n, h * S:(h + 1) * S], w_qk[:, n * HH + h, :], kvt[:, nxt, KC:KV], start=True, stop=True)
                            mm.then_inc(s["q_in_psum"], 1)

                pipeline(pe, step)


def store(nc, m, a, sem):
    stored = sem("stored")
    with nc.Block() as block:
        @block.sync
        def _(sync):
            sync.dma_start(a["out"].rearrange("b s d -> s b d"), m.x[:, :, :]).then_inc(stored, 16)
            sync.wait_ge(stored, 16)


def program(nc, a, last_phase=99, first_phase=0):
    with ExitStack() as ctx:
        m = allocate(nc, ctx)
        m.a = a
        previous = []

        def phase(build, *args):
            held = []

            def sem(name):
                held.append(nc.alloc_semaphore(name))
                return held[-1]

            def clear(pool):
                for old in previous:
                    pool.sem_clear(old)

            build(nc, m, sem, *args, clear)
            for old in previous:
                nc.release_semaphore(old)
            previous[:] = held

        prepare(nc, ctx, m, a)
        if first_phase < 1 <= last_phase:
            phase(head_attention, 0, (m.wq0, m.wk0, m.wv0, m.wo0))
        if first_phase < 2 <= last_phase:
            phase(experts, 0, m.router_t, lambda e: a["L0_ffn_w1"][e], None, lambda e: a["L0_ffn_w2"][e], E0, 0)
        if first_phase < 3 <= last_phase:
            phase(competitive_attention)
        if first_phase < 4 <= last_phase:
            phase(dense_feed_forward)
        if first_phase < 5 <= last_phase:
            phase(head_attention, 2, (m.wq2, m.wk2, m.wv2, m.wo2))
        if first_phase < 6 <= last_phase:
            phase(controller_feed_forward)
        if first_phase < 7 <= last_phase:
            phase(latent_attention)
        if first_phase < 8 <= last_phase:
            phase(experts, 3, m.wg3, lambda e: a["L3_ffn_Ws1"] if isinstance(e, int) and e == 0 else a["L3_ffn_We1"][e - 1],
                  lambda e: a["L3_ffn_Ws3"] if isinstance(e, int) and e == 0 else a["L3_ffn_We3"][e - 1],
                  lambda e: a["L3_ffn_Ws2"] if isinstance(e, int) and e == 0 else a["L3_ffn_We2"][e - 1], E3 + 1, 1)
        store(nc, m, a, lambda n: ctx.enter_context(nc.semaphore(n)))


_OUTS = [((B, S, D), "float32")]


def kernel(**inputs):
    import numpy as _np
    import concourse.bacc as _bacc
    from concourse import mybir as _mybir
    from concourse.bass_utils import run_bass_kernel_spmd as _run

    nc = _bacc.Bacc("TRN2", target_bir_lowering=False, num_devices=1)
    arrays, args = {}, {}
    for name in inputs:
        v = _np.ascontiguousarray(inputs[name])
        arrays[f"in_{name}_dram"] = v
        args[name] = nc.dram_tensor(f"in_{name}_dram", v.shape, _mybir.dt.from_np(v.dtype), kind="ExternalInput").ap()
    for i, (shape, dtype) in enumerate(_OUTS):
        args["out"] = nc.dram_tensor(f"out_{i}_dram", shape, _mybir.dt.from_np(_np.dtype(dtype)), kind="ExternalOutput").ap()
    program(nc, args)
    r = _run(nc, [arrays], core_ids=[0])
    return r.results[0]["out_0_dram"]
```

```python
from contextlib import ExitStack

import concourse.bass as bass
from concourse import mybir

ALU = mybir.AluOpType
ACT = mybir.ActivationFunctionType
AX = mybir.AxisListType
F32 = mybir.dt.float32
BF16 = mybir.dt.bfloat16
F32R = mybir.dt.float32r

B = 32
S = 128
D = 128
KC = 77
HEADS = 16
DK = D // HEADS
HG = 4
NG = HEADS // HG
GB = 4
NGB = B // GB
GT = GB * S
E0, F0 = 8, 512
MX, MY, ML = 8, 64, 64
E3, F3 = 8, 256
H3 = 8
KV = KC + S
EPS = 1e-5
VPAD = D // HG + DK


def wait(eng, sem, value):
    if isinstance(value, int) and value <= 0:
        return
    eng.wait_ge(sem, value)


def pipeline(eng, step, n=B):
    step(-1, 1, True, False, False)
    step(0, 0, True, True, False)
    step(1, 1, True, True, True)
    with eng.Fori(0, (n - 4) // 2) as i:
        step(i * 2 + 2, 0, True, True, True)
        step(i * 2 + 3, 1, True, True, True)
    step(n - 2, 0, True, True, True)
    step(n - 1, 1, False, True, True)
    step(n, 0, False, False, True)


def pipeline4(eng, step, n=B):
    for i in range(-1, 4):
        step(i, i % 2, True, i >= 0, i >= 1, i >= 2)
    with eng.Fori(0, (n - 6) // 2) as i:
        step(i * 2 + 4, 0, True, True, True, True)
        step(i * 2 + 5, 1, True, True, True, True)
    for i in range(n - 2, n + 2):
        step(i, i % 2, i < n - 1, i < n, i <= n, True)


class Memory:
    pass


def row_of(ap):
    return ap.partition_broadcast(128)


def column_of(ap):
    return ap.rearrange("(p a) -> p a", a=1)


def allocate(nc, ctx):
    def sb(name, shape, dtype=F32):
        return ctx.enter_context(nc.sbuf_tensor(name, shape, dtype))

    m = Memory()
    m.x = sb("x_residual", [S, B, D])
    m.ctx = sb("context_rows", [KC, B, D])
    m.ctx_t = sb("context_transposed", [D, B * KC])
    m.moments = sb("x_moments", [S, B, 6])
    m.mean2 = sb("x_mean_doubled", [S, B])
    m.halves = sb("x_halves_difference", [S, B])
    m.var = sb("x_variance", [S, B])
    m.sd = sb("x_deviation", [S, B])
    m.rstd = sb("x_rstd", [S, B])
    m.shift = sb("x_shift", [S, B])
    m.eps = sb("layernorm_eps", [128, 1])
    m.ident = sb("identity", [128, 128])
    m.ident_bf = sb("identity_bf16", [128, 128], BF16)
    m.group_mask = sb("head_in_group_mask", [128, HG])
    m.gate = sb("tanh_gates", [128, 8])
    m.down = sb("descending_count", [128, 128])
    m.psum = ctx.enter_context(nc.psum_tensor("psum", [128, 8, 512], F32))
    m.wq0, m.wk0, m.wv0, m.wo0 = (sb(f"L0_w{c}", [D, D]) for c in "qkvo")
    m.wq2, m.wk2, m.wv2, m.wo2 = (sb(f"L2_w{c}_transposed", [D, D]) for c in "qkvo")
    m.w2_raw = sb("L2_weights_raw", [D, 4, D])
    m.bias_columns = sb("L0_bias_columns", [D, 3])
    m.row_bo0 = sb("L0_bo_row", [128, D])
    m.router_raw = sb("L0_router_raw", [E0, D])
    m.router_t = sb("L0_router_transposed", [D, E0])
    m.wg3 = sb("L3_router", [D, E3])
    return m


def prepare(nc, ctx, m, a):
    def sem(name):
        return ctx.enter_context(nc.semaphore(name))

    x_loaded, ctx_loaded, small_loaded, w_loaded = (sem(n) for n in ("x_loaded", "ctx_loaded", "small_loaded", "w_loaded"))
    blank, ident_ready, mask_ready, down_ready = (sem(n) for n in ("blank", "ident_ready", "mask_ready", "down_ready"))
    identb_ready, tanh_done = sem("identb_ready"), sem("tanh_done")
    tr_done, tr_read = sem("tr_done"), sem("tr_read")
    gated = sem("gated")
    NT = B // GB
    LOADS_X = 4
    with nc.Block() as block:
        @block.sync
        def _(sync):
            for q in range(LOADS_X):
                rows = slice(q * B // LOADS_X, (q + 1) * B // LOADS_X)
                sync.dma_start(m.x[:, rows, :], a["x"][rows].rearrange("b s d -> s b d")).then_inc(x_loaded, 16)
            sync.dma_start(m.w2_raw[:, :, :][:, 0, :], a["L2_xattn_Wq"]).then_inc(w_loaded, 16)
            sync.dma_start(m.w2_raw[:, 1, :], a["L2_xattn_Wk"]).then_inc(w_loaded, 16)
            sync.dma_start(m.w2_raw[:, 2, :], a["L2_xattn_Wv"]).then_inc(w_loaded, 16)
            sync.dma_start(m.w2_raw[:, 3, :], a["L2_xattn_Wo"]).then_inc(w_loaded, 16)
            sync.dma_start(m.router_raw[:, :], a["L0_ffn_router_w"]).then_inc(w_loaded, 16)
            sync.wait_ge(small_loaded, 16 * 11)
            sync.wait_ge(ctx_loaded, 16)

        @block.scalar
        def _(act):
            act.dma_start(m.ctx[:, :, :], a["ctx_1024"].rearrange("b k d -> k b d")).then_inc(ctx_loaded, 16)
            act.dma_start(m.gate[:, 0:4], row_of(a["g_xattn"])).then_inc(small_loaded, 16)
            act.dma_start(m.gate[:, 4:8], row_of(a["g_ffn"])).then_inc(small_loaded, 16)
            act.dma_start(m.wq0[:, :], a["L0_xattn_Wq"]).then_inc(small_loaded, 16)
            act.dma_start(m.wk0[:, :], a["L0_xattn_Wk"]).then_inc(small_loaded, 16)
            act.dma_start(m.wv0[:, :], a["L0_xattn_Wv"]).then_inc(small_loaded, 16)
            act.dma_start(m.wo0[:, :], a["L0_xattn_Wo"]).then_inc(small_loaded, 16)
            act.dma_start(m.wg3[:, :], a["L3_ffn_Wg"]).then_inc(small_loaded, 16)
            act.dma_start(m.bias_columns[:, 0:1], column_of(a["L0_xattn_bq"])).then_inc(small_loaded, 16)
            act.dma_start(m.bias_columns[:, 1:2], column_of(a["L0_xattn_bk"])).then_inc(small_loaded, 16)
            act.dma_start(m.bias_columns[:, 2:3], column_of(a["L0_xattn_bv"])).then_inc(small_loaded, 16)
            act.dma_start(m.row_bo0[:, :], row_of(a["L0_xattn_bo"])).then_inc(small_loaded, 16)
            act.wait_ge(small_loaded, 16 * 11)
            nc.scalar.activation(m.gate[:, :], m.gate[:, :], ACT.Tanh).then_inc(tanh_done, 1)
            for t in range(1, NT, 2):
                act.wait_ge(tr_done, t + 1)
                nc.scalar.copy(m.ctx_t[:, t * GB * KC:(t + 1) * GB * KC],
                               m.psum[:, t % 8, 0:GB * KC]).then_inc(tr_read, 1)
            act.wait_ge(tr_done, NT + 2)
            nc.scalar.copy(m.router_t[:, :], m.psum[:, 1, 0:E0]).then_inc(tr_read, 1)

        @block.gpsimd
        def _(pool):
            nc.gpsimd.memset(m.ident[:, :], 0.0).then_inc(blank, 1)
            nc.gpsimd.memset(m.eps[:, :], EPS).then_inc(blank, 1)
            nc.gpsimd.iota(m.down[:, :], [[-1, 128]], base=128, channel_multiplier=0,
                           allow_small_or_imprecise_dtypes=True).then_inc(down_ready, 1)
            pool.wait_ge(blank, 2)
            nc.gpsimd.affine_select(out=m.ident[:, :], in_=m.ident[:, :], compare_op=ALU.not_equal, fill=1.0,
                                    base=0, pattern=[[-1, 128]], channel_multiplier=1).then_inc(ident_ready, 1)

        @block.tensor
        def _(pe):
            pe.wait_ge(ident_ready, 1)
            pe.wait_ge(ctx_loaded, 16)
            for t in range(NT):
                for u in range(GB):
                    last = nc.tensor.transpose(m.psum[:, t % 8, u * KC:(u + 1) * KC], m.ctx[:, t * GB + u, :],
                                               m.ident[0:KC, 0:KC])
                last.then_inc(tr_done, 1)
            pe.wait_ge(w_loaded, 16 * 5)
            pe.wait_ge(tr_read, NT)
            for u in range(4):
                last = nc.tensor.transpose(m.psum[:, 0, u * D:(u + 1) * D], m.w2_raw[:, u, :], m.ident[:, :])
            last.then_inc(tr_done, 1)
            nc.tensor.transpose(m.psum[:, 1, 0:E0], m.router_raw[:, :], m.ident[0:E0, 0:E0]).then_inc(tr_done, 1)

        @block.vector
        def _(dve):
            dve.wait_ge(ident_ready, 1)
            nc.vector.tensor_copy(m.ident_bf[:, :], m.ident[:, :]).then_inc(identb_ready, 1)
            nc.vector.tensor_reduce(m.group_mask[:, :], m.ident[:, :].rearrange("p (j h d) -> p h j d", h=HG, d=DK),
                                    AX.XY, ALU.add).then_inc(mask_ready, 1)
            for t in range(0, NT, 2):
                dve.wait_ge(tr_done, t + 1)
                nc.vector.tensor_copy(m.ctx_t[:, t * GB * KC:(t + 1) * GB * KC],
                                      m.psum[:, t % 8, 0:GB * KC]).then_inc(tr_read, 1)
            dve.wait_ge(tr_done, NT + 1)
            for u, w in enumerate((m.wq2, m.wk2, m.wv2, m.wo2)):
                nc.vector.tensor_copy(w[:, :], m.psum[:, 0, u * D:(u + 1) * D]).then_inc(tr_read, 1)
            dve.wait_ge(x_loaded, 16 * LOADS_X)
            dve.wait_ge(tanh_done, 1)
            nc.vector.tensor_scalar(m.row_bo0[:, :], m.row_bo0[:, :], m.gate[:, 0:1], None, ALU.mult).then_inc(gated, 1)
            for b in range(B):
                nc.vector.bn_stats(m.moments[:, b, :], m.x[:, b, :])


def variance_of_x(nc, m, dve, parts_ready, var_ready):
    even_mean, even_m2, odd_mean, odd_m2 = (m.moments[:, :, c] for c in (1, 2, 4, 5))
    nc.vector.tensor_tensor(m.mean2[:, :], even_mean, odd_mean, ALU.add).then_inc(parts_ready, 1)
    nc.vector.tensor_tensor(m.halves[:, :], even_mean, odd_mean, ALU.subtract).then_inc(parts_ready, 1)
    nc.vector.tensor_tensor(m.var[:, :], even_m2, odd_m2, ALU.add).then_inc(parts_ready, 1)
    dve.wait_ge(parts_ready, 3)
    nc.vector.scalar_tensor_tensor(m.halves[:, :], m.halves[:, :], 0.25, m.halves[:, :], ALU.mult, ALU.mult).then_inc(parts_ready, 1)
    dve.wait_ge(parts_ready, 4)
    nc.vector.scalar_tensor_tensor(m.var[:, :], m.var[:, :], 1.0 / D, m.halves[:, :], ALU.mult, ALU.add).then_inc(var_ready, 1)


def rstd_of_x(nc, m, dve, sd_ready, rstd_ready, shift_ready):
    dve.wait_ge(sd_ready, 1)
    nc.vector.reciprocal(m.rstd[:, :], m.sd[:, :]).then_inc(rstd_ready, 1)
    dve.wait_ge(rstd_ready, 1)
    nc.vector.scalar_tensor_tensor(m.shift[:, :], m.mean2[:, :], -0.5, m.rstd[:, :], ALU.mult, ALU.mult).then_inc(shift_ready, 1)
    dve.wait_ge(shift_ready, 1)


def head_attention(nc, m, sem, layer, w, clear):
    over_heads = layer == 2
    wq, wk, wv, wo = w
    n_rec = KC if over_heads else HEADS
    names = ("sd_ready rstd_ready shift_ready xn_ready xt_in_psum xt_ready proj_in_psum q_ready k_ready "
             "parts_ready var_ready scores_done negmax_ready shifted exp_ready sum_ready recip_ready probs_ready pt_in_psum "
             "ct_ready v_in_psum ot_in_psum ot_ready v_ready y_done x_done bias_added zeroed "
             "pt_read_0 pt_read_1 pt_read_2 pt_read_3")
    s = {n: sem(f"{n}_{layer}") for n in names.split()}
    pt_read = [s[f"pt_read_{g}"] for g in range(NG)]
    gate = m.gate[:, layer:layer + 1]
    with ExitStack() as ctx:
        def sb(name, shape, dtype=F32):
            return ctx.enter_context(nc.sbuf_tensor(f"{name}_{layer}", shape, dtype))

        xn = sb("xn", [S, 2, D])
        xt = sb("xt", [D, 2, S])
        qt = sb("qt", [D, 2, S])
        ktm = sb("kt_masked", [D, 2, HG, KC])
        vpad = sb("v_padded", [KC, 2, HEADS, VPAD])
        e = sb("exp_scores", [S, 2, HEADS, KC])
        negmax = sb("negated_max", [S, 2, n_rec], BF16)
        total = sb("softmax_sum", [S, 2, n_rec])
        recip = sb("softmax_recip", [S, 2, n_rec])
        pt = sb("probs_transposed", [KC, HEADS, S])
        ot = sb("heads_out", [D, S])
        cts = sb("context_slot", [D, 2, KC])

        def scores_view():
            t = m.psum[:, 0:NG, 0:HG * KC]
            return t.rearrange("p j (h k) -> p k j h", k=KC) if over_heads else t.rearrange("p j (h k) -> p j h k", k=KC)

        def per_row(t, par):
            return t[:, par, :] if over_heads else t[:, par, :].rearrange("p (j h) -> p j h", h=HG)

        with nc.Block() as block:
            @block.gpsimd
            def _(pool):
                clear(pool)
                nc.gpsimd.memset(vpad[:, :, :, :], 0.0).then_inc(s["zeroed"], 1)

                def step(b, par, front, middle, back, tail):
                    if front:
                        wait(pool, s["v_in_psum"], b)
                        nc.gpsimd.tensor_copy(cts[:, 1 - par, :], m.ctx_t[:, bass.ds((b + 1) * KC, KC)]).then_inc(s["ct_ready"], 1)
                    if front and layer == 0:
                        wait(pool, s["xn_ready"], b + 2)
                        nc.gpsimd.tensor_tensor(m.x[:, b + 1, :], m.x[:, b + 1, :], m.row_bo0[:, :],
                                                ALU.add).then_inc(s["bias_added"], 1)
                    if middle:
                        wait(pool, s["recip_ready"], b + 1)
                        for half in range(2):
                            heads = slice(half * HEADS // 2, (half + 1) * HEADS // 2)
                            rec = recip[:, par, :].unsqueeze(1) if over_heads else recip[:, par, heads].unsqueeze(2)
                            nc.gpsimd.tensor_tensor(e[:, par, heads, :], e[:, par, heads, :], rec.to_broadcast([S, HEADS // 2, KC]),
                                                    ALU.mult).then_inc(s["probs_ready"], 1)

                pipeline4(pool, step)

            @block.scalar
            def _(act):
                act.wait_ge(s["var_ready"], 1)
                nc.scalar.activation(m.sd[:, :], m.var[:, :], ACT.Sqrt, bias=m.eps[:, 0:1]).then_inc(s["sd_ready"], 1)

                def copy_group(b, g):
                    wait(act, s["pt_in_psum"], (b - 1) * NG + g + 1)
                    wait(act, s["ot_in_psum"], b - 1)
                    nc.scalar.copy(pt[:, g * HG:(g + 1) * HG, :],
                                   m.psum[0:KC, 4 + g % 2, :].rearrange("p (h s) -> p h s", s=S)).then_inc(pt_read[g], 1)

                def step(b, par, front, middle, back, tail):
                    nxt = 1 - par
                    if tail:
                        wait(act, s["ot_in_psum"], b - 1)
                        wait(act, s["y_done"], b - 2)
                        if layer == 0:
                            nc.scalar.activation(ot[:, :], m.psum[:, 7, 0:S], ACT.Identity,
                                                 bias=m.bias_columns[:, 2:3]).then_inc(s["ot_ready"], 1)
                        else:
                            nc.scalar.copy(ot[:, :], m.psum[:, 7, 0:S]).then_inc(s["ot_ready"], 1)
                    if front:
                        wait(act, s["xt_in_psum"], b + 2)
                        wait(act, s["proj_in_psum"], b)
                        nc.scalar.copy(xt[:, nxt, :], m.psum[:, 6, 0:S]).then_inc(s["xt_ready"], 1)
                    if back:
                        copy_group(b, 0)
                        copy_group(b, 1)
                    if front:
                        wait(act, s["proj_in_psum"], b + 2)
                        wait(act, s["scores_done"], b)
                        if layer == 0:
                            nc.scalar.activation(qt[:, nxt, :], m.psum[:, 6, S:2 * S], ACT.Identity,
                                                 bias=m.bias_columns[:, 0:1]).then_inc(s["q_ready"], 1)
                        else:
                            nc.scalar.copy(qt[:, nxt, :], m.psum[:, 6, S:2 * S]).then_inc(s["q_ready"], 1)
                    if middle:
                        if isinstance(b, int) and b == 0:
                            act.wait_ge(s["zeroed"], 1)
                        wait(act, s["v_in_psum"], b + 1)
                        wait(act, s["ot_in_psum"], b - 1)
                        nc.scalar.copy(vpad[:, par, :, 0:DK], m.psum[0:KC, 6, 3 * S:4 * S].rearrange("p (h d) -> p h d", d=DK))\
                            .then_inc(s["v_ready"], 1)
                        wait(act, s["shifted"], b + 1)
                        wait(act, s["pt_in_psum"], (b - 1) * NG)
                        nc.scalar.activation(e[:, par, :, :].rearrange("p (j h) k -> p j (h k)", h=HG),
                                             m.psum[:, 0:NG, 0:HG * KC], ACT.Exp, scale=DK ** -0.5).then_inc(s["exp_ready"], 1)
                    if back:
                        copy_group(b, 3)

                pipeline4(act, step)

            @block.vector
            def _(dve):
                variance_of_x(nc, m, dve, s["parts_ready"], s["var_ready"])
                rstd_of_x(nc, m, dve, s["sd_ready"], s["rstd_ready"], s["shift_ready"])

                def step(b, par, front, middle, back, tail):
                    nxt = 1 - par
                    if front:
                        wait(dve, s["xt_in_psum"], b)
                        nc.vector.tensor_scalar(xn[:, nxt, :], m.x[:, b + 1, :], m.rstd[:, bass.ds(b + 1, 1)],
                                                m.shift[:, bass.ds(b + 1, 1)], ALU.mult, ALU.add).then_inc(s["xn_ready"], 1)
                    if middle:
                        wait(dve, s["scores_done"], b + 1)
                        wait(dve, s["shifted"], b - 1)
                        nc.vector.tensor_reduce(per_row(negmax, par), scores_view(), AX.XY if over_heads else AX.X,
                                                ALU.max, negate=True).then_inc(s["negmax_ready"], 1)
                    if tail:
                        wait(dve, s["y_done"], b - 1)
                        if layer == 0:
                            wait(dve, s["bias_added"], b - 1)
                        nc.vector.scalar_tensor_tensor(m.x[:, b - 2, :], m.psum[:, 7, S:2 * S], gate, m.x[:, b - 2, :],
                                                       ALU.mult, ALU.add).then_inc(s["x_done"], 1)
                    if back:
                        wait(dve, s["pt_in_psum"], (b - 1) * NG + 3)
                        wait(dve, s["ot_in_psum"], b - 1)
                        nc.vector.tensor_copy(pt[:, 2 * HG:3 * HG, :], m.psum[0:KC, 4, :].rearrange("p (h s) -> p h s", s=S)).then_inc(pt_read[2], 1)
                    if front:
                        wait(dve, s["q_ready"], b + 2)
                        wait(dve, s["v_ready"], b + 1)
                        kin = m.psum[:, 6, 2 * S:2 * S + KC].unsqueeze(1).to_broadcast([D, HG, KC])
                        mask = m.group_mask[:, :].unsqueeze(2).to_broadcast([D, HG, KC])
                        nc.vector.scalar_tensor_tensor(ktm[:, nxt, :, :], kin, m.bias_columns[:, 1:2] if layer == 0 else 0.0,
                                                       mask, ALU.add, ALU.mult).then_inc(s["k_ready"], 1)
                    if middle:
                        wait(dve, s["exp_ready"], b + 1)
                        nc.vector.tensor_reduce(total[:, par, :], e[:, par, :, :].rearrange("p h k -> p k h") if over_heads else e[:, par, :, :],
                                                AX.X, ALU.add).then_inc(s["sum_ready"], 1)
                        wait(dve, s["sum_ready"], b + 1)
                        wait(dve, s["probs_ready"], (b - 1) * 2)
                        nc.vector.reciprocal(recip[:, par, :], total[:, par, :]).then_inc(s["recip_ready"], 1)
                    if tail:
                        wait(dve, s["x_done"], b - 1)
                        nc.vector.bn_stats(m.moments[:, b - 2, :], m.x[:, b - 2, :])

                pipeline4(dve, step)

            @block.tensor
            def _(pe):
                def transposes(b, nxt, g):
                    if g >= 2:
                        wait(pe, pt_read[g - 2], b)
                    else:
                        wait(pe, pt_read[g + 2], b - 1)
                    for h in range(HG):
                        last = nc.tensor.transpose(m.psum[0:KC, 4 + g % 2, h * S:(h + 1) * S], e[:, nxt, g * HG + h, :], m.ident[:, :])
                    last.then_inc(s["pt_in_psum"], 1)

                def step(b, par, front, middle, back, tail):
                    nxt = 1 - par
                    if middle:
                        wait(pe, s["q_ready"], b + 1)
                        wait(pe, s["k_ready"], b + 1)
                        wait(pe, s["exp_ready"], b)
                        for j in range(NG):
                            rows = slice(32 * j, 32 * j + 32)
                            last = nc.tensor.matmul(m.psum[:, j, 0:HG * KC], qt[rows, par, :],
                                                    ktm[rows, par, :, :].rearrange("p h k -> p (h k)"), start=True, stop=True)
                        last.then_inc(s["scores_done"], 1)
                    if front:
                        wait(pe, s["xn_ready"], b + 2)
                        wait(pe, s["q_ready"], b + 1)
                        wait(pe, s["k_ready"], b + 1)
                        wait(pe, s["v_ready"], b)
                        nc.tensor.transpose(m.psum[:, 6, 0:S], xn[:, nxt, :], m.ident[:, :]).then_inc(s["xt_in_psum"], 1)
                    if tail:
                        wait(pe, s["ot_ready"], b - 1)
                        nc.tensor.matmul(m.psum[:, 7, S:2 * S], ot[:, :], wo[:, :], start=True, stop=True).then_inc(s["y_done"], 1)
                    if back:
                        wait(pe, s["probs_ready"], b * 2 - 1)
                        transposes(b, nxt, 0)
                        transposes(b, nxt, 1)
                    if front:
                        wait(pe, s["xt_ready"], b + 2)
                    if middle:
                        wait(pe, s["ct_ready"], b + 1)
                        if not front:
                            wait(pe, s["k_ready"], b + 1)
                            wait(pe, s["v_ready"], b)
                        nc.tensor.matmul(m.psum[0:KC, 6, 3 * S:4 * S], cts[:, par, :], wv[:, :], start=True, stop=True).then_inc(s["v_in_psum"], 1)
                    if front:
                        nc.tensor.matmul(m.psum[:, 6, S:2 * S], wq[:, :], xt[:, nxt, :], start=True, stop=True)
                        wait(pe, s["ct_ready"], b + 2)
                        nc.tensor.matmul(m.psum[:, 6, 2 * S:2 * S + KC], wk[:, :], cts[:, nxt, :], start=True, stop=True)\
                            .then_inc(s["proj_in_psum"], 1)
                    if middle:
                        wait(pe, s["negmax_ready"], b + 1)
                        for j in range(NG):
                            nm = negmax[:, par, :]
                            nm = nm.unsqueeze(1) if over_heads else nm[:, j * HG:(j + 1) * HG].unsqueeze(2)
                            last = nc.tensor.matmul(m.psum[:, j, 0:HG * KC].rearrange("p (h k) -> p h k", k=KC), m.ident_bf[:, :],
                                                    nm.to_broadcast([S, HG, KC]), start=False, stop=True, skip_group_check=True)
                        last.then_inc(s["shifted"], 1)
                    if back:
                        wait(pe, s["probs_ready"], b * 2)
                        transposes(b, nxt, 2)
                        transposes(b, nxt, 3)
                        wait(pe, s["v_ready"], b)
                        wait(pe, s["x_done"], b - 1)
                        wait(pe, s["ot_ready"], b - 1)
                        for pair in ((0, 1), (2, 3)):
                            for g in pair:
                                wait(pe, pt_read[g], b)
                            for h in range(HG):
                                for g in pair:
                                    at = (g * HG + h) * VPAD - h * DK
                                    lhs = vpad[:, nxt, :, :].rearrange("p h c -> p (h c)")[:, at:at + 32]
                                    last = nc.tensor.matmul(m.psum[32 * g:32 * g + 32, 7, 0:S], lhs, pt[:, g * HG + h, :],
                                                            start=(h == 0), stop=(h == HG - 1), skip_group_check=True)
                        last.then_inc(s["ot_in_psum"], 1)

                pipeline4(pe, step)


def transpose_groups(nc, m, s, xn, xts, xt_high, xt_low, engines, router=None):
    nc_engines = engines
    which, eng = nc_engines

    def step(g, par, front, middle, back):
        nxt = 1 - par
        if which == "vector":
            if front:
                wait(eng, s["xt_in_psum"], g)
                for t in range(GB):
                    at = (g + 1) * GB + t
                    last = nc.vector.tensor_scalar(xn[:, nxt, t, :], m.x[:, at, :], m.rstd[:, bass.ds(at, 1)],
                                                   m.shift[:, bass.ds(at, 1)], ALU.mult, ALU.add)
                last.then_inc(s["xn_ready"], 1)
            if middle:
                wait(eng, s["logits_in_psum"], g + 1)
                nc.vector.tensor_copy(router[1][:, bass.ds(g * GB, GB), :],
                                      m.psum[:, 2 + par, 0:GB * E0].rearrange("p (t e) -> p t e", e=E0)).then_inc(s["logits_ready"], 1)
        if which == "scalar" and front:
            wait(eng, s["xt_in_psum"], g + 2)
            wait(eng, s["logits_in_psum"], g)
            wait(eng, s["xt_low_ready"], g)
            nc.scalar.copy(xts[:, nxt, :], m.psum[:, nxt, :]).then_inc(s["xts_ready"], 1)
            nc.scalar.copy(xt_high[:, bass.ds((g + 1) * GT, GT)], m.psum[:, nxt, :]).then_inc(s["xt_high_ready"], 1)
        if which == "gpsimd" and front:
            wait(eng, s["xt_high_ready"], g + 2)
            nc.gpsimd.tensor_tensor(xt_low[:, bass.ds((g + 1) * GT, GT)], xts[:, nxt, :], xt_high[:, bass.ds((g + 1) * GT, GT)],
                                    ALU.subtract).then_inc(s["xt_low_ready"], 1)
        if which == "tensor":
            if front:
                wait(eng, s["xn_ready"], g + 2)
                wait(eng, s["xt_high_ready"], g)
                for t in range(GB):
                    last = nc.tensor.transpose(m.psum[:, nxt, t * S:(t + 1) * S], xn[:, nxt, t, :], m.ident[:, :])
                last.then_inc(s["xt_in_psum"], 1)
            if middle:
                wait(eng, s["xts_ready"], g + 1)
                wait(eng, s["logits_ready"], g - 1)
                for t in range(GB):
                    last = nc.tensor.matmul(m.psum[:, 2 + par, t * E0:(t + 1) * E0], xts[:, par, t * S:(t + 1) * S],
                                            router[0][:, :], start=True, stop=True)
                last.then_inc(s["logits_in_psum"], 1)

    pipeline(eng, step, NGB)


def top_two(nc, m, link, p, work, m1, m2, pick1, pick2):
    wide = [S, B, E0]
    down = m.down[:, 0:E0].unsqueeze(1).to_broadcast(wide)

    def spread(t):
        return t[:, :].unsqueeze(2).to_broadcast(wide)

    for value, pick, first in ((m1, pick1, True), (m2, pick2, False)):
        link(nc.vector.tensor_reduce(value[:, :], p[:, :, :], AX.X, ALU.max))
        link(nc.vector.tensor_tensor(pick[:, :, :], p[:, :, :], spread(value), ALU.is_ge))
        link(nc.vector.tensor_tensor(pick[:, :, :], pick[:, :, :], down, ALU.mult))
        link(nc.vector.tensor_reduce(work[:, :], pick[:, :, :], AX.X, ALU.max))
        link(nc.vector.tensor_tensor(pick[:, :, :], pick[:, :, :], spread(work), ALU.is_equal))
        if first:
            link(nc.vector.scalar_tensor_tensor(p[:, :, :], pick[:, :, :], -4.0, p[:, :, :], ALU.mult, ALU.add))


def experts(nc, m, sem, layer, router_t, w_up, w_gate, w_down, n_exp, shared, clear):
    hidden = F0 if layer == 0 else F3
    chunks = hidden // 128
    names = ("parts_ready var_ready sd_ready rstd_ready shift_ready xn_ready xt_in_psum xts_ready xt_high_ready xt_low_ready "
             "logits_in_psum logits_ready link exp_wanted exp_ready weights_ready shared_ready hidden_in_psum silu_ready up_read "
             "hidden_ready y_done_a y_done_b y_read_a y_read_b w_loaded_a w_loaded_b w_split")
    s = {n: sem(f"{n}_ffn{layer}") for n in names.split()}
    gate = m.gate[:, 4 + layer:5 + layer]
    y_done, y_read = (s["y_done_a"], s["y_done_b"]), (s["y_read_a"], s["y_read_b"])
    w_loaded = (s["w_loaded_a"], s["w_loaded_b"])
    loads = 2 if layer == 0 else 3
    with ExitStack() as ctx:
        def sb(name, shape, dtype=F32):
            return ctx.enter_context(nc.sbuf_tensor(f"{name}_ffn{layer}", shape, dtype))

        xn = sb("xn", [S, 2, GB, D])
        xts = sb("xt_slot", [D, 2, GT])
        xt_high, xt_low = sb("xt_high", [D, B * S], F32R), sb("xt_low", [D, B * S], F32R)
        logits = sb("logits", [S, B, E0])
        m1, m2, work, rec = (sb(n, [S, B]) for n in ("top1", "top2", "pick_code", "weight_recip"))
        pick1, pick2 = sb("pick1", [S, B, E0]), sb("pick2", [S, B, E0])
        weight = sb("expert_weight", [S, n_exp, B])
        raw = sb("w_up_raw", [D, 2, loads - 1, hidden])
        high, low = sb("w_up_high", [D, 2, loads - 1, hidden], F32R), sb("w_up_low", [D, 2, loads - 1, hidden], F32R)
        down = sb("w_down", [128, 2, chunks, D])
        silu = sb("silu", [128, 2, GT]) if layer == 3 else None
        hid = sb("hidden", [128, 2, chunks, GT])

        def all_experts(eng, block_of):
            block_of(0, 0, False)
            with eng.Fori(0, 3) as i:
                block_of(i * 2 + 1, 1, False)
                block_of(i * 2 + 2, 0, False)
            for e in range(7, n_exp):
                block_of(e, e % 2, e == n_exp - 1)

        with nc.Block() as block:
            @block.sync
            def _(sync):
                for e in range(n_exp):
                    slot = e % 2
                    if e >= 2:
                        sync.wait_ge(y_done[1], (e - 1) * (NGB // 2))
                        sync.wait_ge(s["w_split"], 2 * (e - 1))
                    sync.dma_start(raw[:, slot, 0, :], w_up(e)).then_inc(w_loaded[slot], 16)
                    if layer == 3:
                        sync.dma_start(raw[:, slot, 1, :], w_gate(e)).then_inc(w_loaded[slot], 16)
                    sync.dma_start(down[:, slot, :, :], w_down(e).rearrange("(c f) d -> f c d", f=128)).then_inc(w_loaded[slot], 16)

            @block.gpsimd
            def _(pool):
                clear(pool)

                def split(e, slot):
                    if e >= 2:
                        pool.wait_ge(y_done[1], (e - 1) * (NGB // 2))
                    pool.wait_ge(w_loaded[slot], (e // 2 + 1) * 16 * loads)
                    nc.gpsimd.tensor_copy(high[:, slot, :, :], raw[:, slot, :, :]).then_inc(s["w_split"], 1)
                    pool.wait_ge(s["w_split"], 2 * e + 1)
                    nc.gpsimd.tensor_tensor(low[:, slot, :, :], raw[:, slot, :, :], high[:, slot, :, :], ALU.subtract).then_inc(s["w_split"], 1)

                split(0, 0)
                transpose_groups(nc, m, s, xn, xts, xt_high, xt_low, ("gpsimd", pool))
                for e in range(1, n_exp):
                    split(e, e % 2)

            @block.scalar
            def _(act):
                act.wait_ge(s["var_ready"], 1)
                nc.scalar.activation(m.sd[:, :], m.var[:, :], ACT.Sqrt, bias=m.eps[:, 0:1]).then_inc(s["sd_ready"], 1)
                transpose_groups(nc, m, s, xn, xts, xt_high, xt_low, ("scalar", act))
                act.wait_ge(s["exp_wanted"], 1)
                nc.scalar.activation(logits[:, :, :], logits[:, :, :], ACT.Exp,
                                     scale=1.0 if layer == 0 else -1.0).then_inc(s["exp_ready"], 1)
                if layer == 0:
                    act.wait_ge(s["logits_ready"], NGB)
                    act.sem_inc(s["hidden_ready"], chunks)

                def unit(e, g, u):
                    n = e * NGB + g
                    for c in range(chunks):
                        if layer == 0:
                            wait(act, s["hidden_in_psum"], n * chunks + c + 1)
                            if c == 0:
                                wait(act, y_done[u], e * (NGB // 2) + g_pair(g, u))
                            nc.scalar.activation(hid[:, u, c, :], m.psum[:, c, :], ACT.Gelu).then_inc(s["hidden_ready"], 1)
                        else:
                            wait(act, s["hidden_in_psum"], n * chunks + c + 1)
                            wait(act, s["hidden_ready"], n * chunks + c + 1)
                            nc.scalar.activation(silu[:, c, :], m.psum[:, c, :], ACT.Silu).then_inc(s["silu_ready"], 1)

                def block_of(e, slot, last):
                    with act.Fori(0, NGB // 2) as i:
                        pair[0] = i
                        unit(e, i * 2, 0)
                        unit(e, i * 2 + 1, 1)

                pair = [None]

                def g_pair(g, u):
                    return pair[0]

                all_experts(act, block_of)

            @block.vector
            def _(dve):
                variance_of_x(nc, m, dve, s["parts_ready"], s["var_ready"])
                rstd_of_x(nc, m, dve, s["sd_ready"], s["rstd_ready"], s["shift_ready"])
                transpose_groups(nc, m, s, xn, xts, xt_high, xt_low, ("vector", dve), (router_t, logits))
                count = [0]

                def link(ins):
                    count[0] += 1
                    ins.then_inc(s["link"], 1)
                    dve.wait_ge(s["link"], count[0])

                wide = [S, B, E0]

                def spread(t):
                    return t[:, :].unsqueeze(2).to_broadcast(wide)

                dve.wait_ge(s["logits_ready"], NGB)
                if layer == 0:
                    link(nc.vector.tensor_reduce(work[:, :], logits[:, :, :], AX.X, ALU.max))
                    nc.vector.tensor_tensor(logits[:, :, :], logits[:, :, :], spread(work), ALU.subtract).then_inc(s["exp_wanted"], 1)
                    dve.wait_ge(s["exp_ready"], 1)
                    link(nc.vector.tensor_reduce(work[:, :], logits[:, :, :], AX.X, ALU.add))
                    link(nc.vector.reciprocal(rec[:, :], work[:, :]))
                    link(nc.vector.tensor_tensor(logits[:, :, :], logits[:, :, :], spread(rec), ALU.mult))
                else:
                    dve.sem_inc(s["exp_wanted"], 1)
                    dve.wait_ge(s["exp_ready"], 1)
                    link(nc.vector.tensor_scalar(logits[:, :, :], logits[:, :, :], 1.0, None, ALU.add))
                    link(nc.vector.reciprocal(logits[:, :, :], logits[:, :, :]))
                top_two(nc, m, link, logits, work, m1, m2, pick1, pick2)
                link(nc.vector.scalar_tensor_tensor(work[:, :], m1[:, :], 1e-9 if layer == 0 else 0.0, m2[:, :], ALU.add, ALU.add))
                link(nc.vector.reciprocal(rec[:, :], work[:, :]))
                link(nc.vector.tensor_scalar(rec[:, :], rec[:, :], gate, 1.0 if layer == 0 else 1.0 / 3.0, ALU.mult, ALU.mult))
                link(nc.vector.tensor_tensor(pick1[:, :, :], pick1[:, :, :], spread(m1), ALU.mult))
                link(nc.vector.tensor_tensor(pick2[:, :, :], pick2[:, :, :], spread(m2), ALU.mult))
                link(nc.vector.tensor_tensor(pick1[:, :, :], pick1[:, :, :], pick2[:, :, :], ALU.add))
                link(nc.vector.tensor_tensor(weight[:, shared:shared + E0, :].rearrange("p e b -> p b e"), pick1[:, :, :],
                                             spread(rec), ALU.mult))
                if shared:
                    link(nc.vector.memset(weight[:, 0, :], 1.0 / 3.0))
                    link(nc.vector.tensor_scalar(weight[:, 0, :], weight[:, 0, :], gate, None, ALU.mult))
                if layer == 3:
                    dve.sem_inc(s["hidden_ready"], chunks)

                def multiply(e, g, u, p):
                    n = e * NGB + g
                    for c in range(chunks):
                        wait(dve, s["silu_ready"], n * chunks + c + 1)
                        if c == 0:
                            wait(dve, y_done[u], e * (NGB // 2) + p)
                        nc.vector.tensor_tensor(hid[:, u, c, :], silu[:, c, :], m.psum[:, 2 + c, :], ALU.mult)\
                            .then_inc(s["hidden_ready"], 1)

                def update(e, g, u, p, last):
                    wait(dve, y_done[u], e * (NGB // 2) + p + 1)
                    for t in range(GB):
                        at = g * GB + t
                        ins = nc.vector.scalar_tensor_tensor(m.x[:, at, :], m.psum[:, 4 + u, t * D:(t + 1) * D],
                                                             weight[:, e, bass.ds(at, 1)], m.x[:, at, :], ALU.mult, ALU.add)
                    ins.then_inc(y_read[u], 1)

                def stats(g):
                    for t in range(GB):
                        nc.vector.bn_stats(m.moments[:, g * GB + t, :], m.x[:, g * GB + t, :])

                def block_of(e, slot, last):
                    with dve.Fori(0, NGB // 2) as i:
                        if layer == 3:
                            multiply(e, i * 2, 0, i)
                            multiply(e, i * 2 + 1, 1, i)
                        update(e, i * 2, 0, i, last)
                        update(e, i * 2 + 1, 1, i, last)

                all_experts(dve, block_of)
                dve.wait_ge(y_read[0], n_exp * NGB // 2)
                dve.wait_ge(y_read[1], n_exp * NGB // 2)
                for b in range(B):
                    nc.vector.bn_stats(m.moments[:, b, :], m.x[:, b, :])

            @block.tensor
            def _(pe):
                transpose_groups(nc, m, s, xn, xts, xt_high, xt_low, ("tensor", pe), (router_t, logits))
                pe.wait_ge(s["xt_low_ready"], NGB)
                pe.wait_ge(s["xts_ready"], NGB)
                pe.wait_ge(s["logits_ready"], NGB)

                def up_project(e, slot, side, c, g):
                    cols = slice(c * 128, (c + 1) * 128)
                    terms = ((low, xt_high), (high, xt_low), (high, xt_high))
                    for n, (weights, moving) in enumerate(terms):
                        mm = nc.tensor.matmul(m.psum[:, 2 * side + c, :], weights[:, slot, side, cols], moving[:, bass.ds(g * GT, GT)],
                                              start=(n == 0), stop=(n == len(terms) - 1))
                    return mm

                def block_of(e, slot, last):
                    with pe.Fori(0, NGB // 2) as i:
                        wait(pe, s["w_split"], e * 2 + 2)
                        for u in range(2):
                            n = e * NGB + i * 2 + u
                            for c in range(chunks):
                                wait(pe, s["hidden_ready"], n * chunks + c + 1)
                                for side in range(loads - 1):
                                    last_mm = up_project(e, slot, side, c, i * 2 + u)
                                last_mm.then_inc(s["hidden_in_psum"], 1)
                        wait(pe, w_loaded[slot], (e + 2 - slot) * 8 * loads)
                        for u in range(2):
                            n = e * NGB + i * 2 + u
                            wait(pe, s["hidden_ready"], (n + 2) * chunks)
                            wait(pe, y_read[u], e * (NGB // 2) + i)
                            for t in range(GB):
                                for c in range(chunks):
                                    last_mm = nc.tensor.matmul(m.psum[:, 4 + u, t * D:(t + 1) * D], hid[:, u, c, t * S:(t + 1) * S],
                                                               down[:, slot, c, :], start=(c == 0), stop=(c == chunks - 1))
                            last_mm.then_inc(y_done[u], 1)

                all_experts(pe, block_of)


def chain(eng, sem, done, length):
    count = [0]

    def link(ins):
        count[0] += 1
        assert count[0] <= length
        ins.then_inc(sem, 1)
        wait(eng, sem, done * length + count[0])

    return link


def competitive_attention(nc, m, sem, clear):
    names = ("parts_ready var_ready sd_ready rstd_ready shift_ready loaded neg_ready ones_ready xn_used xn_ready xt_in_psum xt_ready "
             "z_in_psum exp_ready sim_ready simt_in_psum simt_ready agg_in_psum rows_ready y_done x_done mid_link back_link")
    s = {n: sem(f"{n}_1") for n in names.split()}
    gate = m.gate[:, 1:2]
    MID, BACK = 6, 3
    with ExitStack() as ctx:
        def sb(name, shape, dtype=F32):
            return ctx.enter_context(nc.sbuf_tensor(f"{name}_xattn1", shape, dtype))

        xn = sb("xn", [S, 2, GB, D])
        xt = sb("xt", [D, 2, GT])
        alpha_beta = sb("alpha_beta", [S, 2])
        sim = sb("sim", [S, 2, GB, KC])
        pick = sb("pick", [S, 2, GB, KC])
        best = sb("best_sim", [S, GB])
        code = sb("pick_code", [S, GB])
        weighted = sb("weighted_tokens", [S, 2, GB, D + 1])
        simt = sb("sim_transposed", [KC, GT])
        rows = sb("context_out", [KC, GB, D])
        tally = sb("token_count", [KC, 2, 2])
        with nc.Block() as block:
            @block.gpsimd
            def _(pool):
                clear(pool)
                nc.gpsimd.memset(weighted[:, :, :, :], 1.0).then_inc(s["ones_ready"], 1)

            @block.sync
            def _(sync):
                sync.dma_start(alpha_beta[:, 0:1], row_of(m.a["L1_xattn_sim_alpha"])).then_inc(s["loaded"], 16)
                sync.dma_start(alpha_beta[:, 1:2], row_of(m.a["L1_xattn_sim_beta"])).then_inc(s["loaded"], 16)

            @block.scalar
            def _(act):
                act.wait_ge(s["var_ready"], 1)
                nc.scalar.activation(m.sd[:, :], m.var[:, :], ACT.Sqrt, bias=m.eps[:, 0:1]).then_inc(s["sd_ready"], 1)
                act.wait_ge(s["neg_ready"], 1)

                def step(g, par, front, middle, back):
                    nxt = 1 - par
                    if middle:
                        wait(act, s["z_in_psum"], g + 1)
                        wait(act, s["simt_in_psum"], g - 1)
                        nc.scalar.activation(sim[:, par, :, :].rearrange("p b k -> p (b k)"), m.psum[:, 1, 0:GB * KC], ACT.Exp,
                                             scale=alpha_beta[:, 0:1], bias=alpha_beta[:, 1:2]).then_inc(s["exp_ready"], 1)
                    if back:
                        wait(act, s["simt_in_psum"], g)
                        wait(act, s["y_done"], g - 1)
                        nc.scalar.copy(simt[:, :], m.psum[0:KC, 2, :]).then_inc(s["simt_ready"], 1)
                    if front:
                        wait(act, s["xt_in_psum"], g + 2)
                        wait(act, s["z_in_psum"], g)
                        nc.scalar.copy(xt[:, nxt, :], m.psum[:, 0, :]).then_inc(s["xt_ready"], 1)

                pipeline(act, step, NGB)

            @block.vector
            def _(dve):
                dve.wait_ge(s["loaded"], 32)
                nc.vector.tensor_scalar(alpha_beta[:, :], alpha_beta[:, :], -1.0, None, ALU.mult).then_inc(s["neg_ready"], 1)
                variance_of_x(nc, m, dve, s["parts_ready"], s["var_ready"])
                rstd_of_x(nc, m, dve, s["sd_ready"], s["rstd_ready"], s["shift_ready"])
                dve.wait_ge(s["ones_ready"], 1)
                wide = [S, GB, KC]

                def step(g, par, front, middle, back):
                    nxt = 1 - par
                    if front:
                        wait(dve, s["xt_in_psum"], g)
                        wait(dve, s["xn_used"], g)
                        for t in range(GB):
                            at = (g + 1) * GB + t
                            ins = nc.vector.tensor_scalar(xn[:, nxt, t, :], m.x[:, at, :], m.rstd[:, bass.ds(at, 1)],
                                                          m.shift[:, bass.ds(at, 1)], ALU.mult, ALU.add)
                        ins.then_inc(s["xn_ready"], 1)
                    if back:
                        link = chain(dve, s["back_link"], g - 1, BACK)
                        wait(dve, s["agg_in_psum"], g)
                        wait(dve, s["y_done"], g - 1)
                        agg = m.psum[0:KC, 3:5, 0:2 * (D + 1)].rearrange("p j (u c) -> p j u c", u=2)
                        nc.vector.tensor_scalar(tally[:, :, :].unsqueeze(3), agg[:, :, :, D:D + 1], 1.0, None, ALU.add)
                        link(nc.vector.tensor_tensor(rows[:, :, :].rearrange("p (j u) d -> p j u d", u=2), agg[:, :, :, 0:D],
                                                     m.ctx[:, bass.ds((g - 1) * GB, GB), :].rearrange("p (j u) d -> p j u d", u=2), ALU.add))
                        tl = tally[:, :, :].rearrange("p j u -> p (j u)")
                        link(nc.vector.reciprocal(tl, tl))
                        link(nc.vector.tensor_tensor(rows[:, :, :], rows[:, :, :], tl.unsqueeze(2).to_broadcast([KC, GB, D]), ALU.mult))
                    if middle:
                        link = chain(dve, s["mid_link"], g, MID)
                        wait(dve, s["exp_ready"], g + 1)
                        wait(dve, s["agg_in_psum"], g - 1)
                        sv, pv = sim[:, par, :, :], pick[:, par, :, :]
                        link(nc.vector.tensor_scalar(sv, sv, 1.0, None, ALU.add))
                        link(nc.vector.reciprocal(sv, sv))
                        link(nc.vector.tensor_reduce(best[:, :], sv, AX.X, ALU.max))
                        link(nc.vector.tensor_tensor(pv, sv, best[:, :].unsqueeze(2).to_broadcast(wide), ALU.is_ge))
                        link(nc.vector.tensor_tensor(pv, pv, m.down[:, 0:KC].unsqueeze(1).to_broadcast(wide), ALU.mult))
                        link(nc.vector.tensor_reduce(code[:, :], pv, AX.X, ALU.max))
                        nc.vector.tensor_tensor(pv, pv, code[:, :].unsqueeze(2).to_broadcast(wide), ALU.is_equal)
                        for t in range(GB):
                            ins = nc.vector.tensor_scalar(weighted[:, par, t, 0:D], xn[:, par, t, :], best[:, t:t + 1], None, ALU.mult)
                        ins.then_inc(s["sim_ready"], 1)
                        xg = m.x[:, bass.ds(g * GB, GB), :].rearrange("p b d -> p (b d)")
                        nc.vector.scalar_tensor_tensor(xg, xn[:, par, :, :].rearrange("p b d -> p (b d)"), gate, xg,
                                                       ALU.mult, ALU.add).then_inc(s["xn_used"], 1)
                    if back:
                        wait(dve, s["y_done"], g)
                        xg = m.x[:, bass.ds((g - 1) * GB, GB), :].rearrange("p b d -> p (b d)")
                        nc.vector.scalar_tensor_tensor(xg, m.psum[:, 5, :], gate, xg, ALU.mult, ALU.add).then_inc(s["x_done"], 1)

                pipeline(dve, step, NGB)
                dve.wait_ge(s["x_done"], NGB)
                for b in range(B):
                    nc.vector.bn_stats(m.moments[:, b, :], m.x[:, b, :])

            @block.tensor
            def _(pe):
                def step(g, par, front, middle, back):
                    nxt = 1 - par
                    if middle:
                        wait(pe, s["xt_ready"], g + 1)
                        wait(pe, s["exp_ready"], g)
                        for t in range(GB):
                            mm = nc.tensor.matmul(m.psum[:, 1, t * KC:(t + 1) * KC], xt[:, par, t * S:(t + 1) * S],
                                                  m.ctx_t[:, bass.ds((g * GB + t) * KC, KC)], start=True, stop=True)
                        mm.then_inc(s["z_in_psum"], 1)
                    if back:
                        wait(pe, s["sim_ready"], g)
                        wait(pe, s["simt_ready"], g - 1)
                        for t in range(GB):
                            mm = nc.tensor.transpose(m.psum[0:KC, 2, t * S:(t + 1) * S], sim[:, nxt, t, :], m.ident[:, :])
                        mm.then_inc(s["simt_in_psum"], 1)
                        wait(pe, s["back_link"], (g - 1) * BACK)
                        for t in range(GB):
                            mm = nc.tensor.matmul(m.psum[0:KC, 3 + t // 2, (t % 2) * (D + 1):(t % 2 + 1) * (D + 1)], pick[:, nxt, t, :],
                                                  weighted[:, nxt, t, :], start=True, stop=True)
                        mm.then_inc(s["agg_in_psum"], 1)
                    if front:
                        wait(pe, s["xn_ready"], g + 2)
                        wait(pe, s["xt_ready"], g + 1)
                        for t in range(GB):
                            mm = nc.tensor.transpose(m.psum[:, 0, t * S:(t + 1) * S], xn[:, nxt, t, :], m.ident[:, :])
                        mm.then_inc(s["xt_in_psum"], 1)
                    if back:
                        wait(pe, s["back_link"], g * BACK)
                        wait(pe, s["simt_ready"], g)
                        wait(pe, s["x_done"], g - 1)
                        for t in range(GB):
                            mm = nc.tensor.matmul(m.psum[:, 5, t * D:(t + 1) * D], simt[:, t * S:(t + 1) * S], rows[:, t, :],
                                                  start=True, stop=True)
                        mm.then_inc(s["y_done"], 1)

                pipeline(pe, step, NGB)


def dense_feed_forward(nc, m, sem, clear):
    names = ("parts_ready var_ready sd_ready rstd_ready shift_ready loaded rows_ready xn_ready xt_in_psum xt_ready base_ready "
             "hidden_in_psum hidden_ready y_done z_ready z_var_ready z_sd_ready zn_ready scaled moved x_done link w_transposed")
    s = {n: sem(f"{n}_ffn1") for n in names.split()}
    chunks = F0 // 128
    LINKS = 6
    a = m.a
    with ExitStack() as ctx:
        def sb(name, shape, dtype=F32):
            return ctx.enter_context(nc.sbuf_tensor(f"{name}_ffn1", shape, dtype))

        xn = sb("xn", [S, 2, GB, D])
        xt = sb("xt", [D, 2, GT])
        base = sb("xn_and_bias", [S, 2, GB, D])
        up, down = sb("w_up", [D, F0]), sb("w_down", [128, chunks, D])
        b1 = sb("b1_columns", [128, chunks])
        row_b2, row_gamma, row_beta = (sb(n, [S, D]) for n in ("b2_row", "gamma_row", "beta_row"))
        hid = sb("hidden", [128, 2, chunks, GT])
        z = sb("z", [S, 2, GB, D])
        zst = sb("z_stats", [S, GB, 6])
        mean2, halves, var, sd, rstd, shift = (sb(n, [S, GB]) for n in ("z_mean2", "z_halves", "z_var", "z_sd", "z_rstd", "z_shift"))
        with nc.Block() as block:
            @block.sync
            def _(sync):
                for to, of in ((up[:, :], a["L1_ffn_w1"][0]), (down[:, :, :], a["L1_ffn_w2"][0].rearrange("(c f) d -> f c d", f=128)),
                               *((b1[:, c:c + 1], column_of(a["L1_ffn_b1"][0, c * 128:(c + 1) * 128])) for c in range(chunks)), (row_b2[:, :], row_of(a["L1_ffn_b2"][0])),
                               (row_gamma[:, :], row_of(a["L1_ffn_gamma"])), (row_beta[:, :], row_of(a["L1_ffn_beta"]))):
                    sync.dma_start(to, of).then_inc(s["loaded"], 16)

            @block.gpsimd
            def _(pool):
                clear(pool)
                pool.wait_ge(s["rows_ready"], 2)

                def step(g, par, front, middle, back):
                    nxt = 1 - par
                    wide = [S, GB, D]
                    if front:
                        wait(pool, s["xn_ready"], g + 2)
                        wait(pool, s["z_ready"], g)
                        nc.gpsimd.tensor_tensor(base[:, nxt, :, :], xn[:, nxt, :, :], row_b2[:, :].unsqueeze(1).to_broadcast(wide),
                                                ALU.add).then_inc(s["base_ready"], 1)
                    if back:
                        zv, xv = z[:, nxt, :, :], m.x[:, bass.ds((g - 1) * GB, GB), :]
                        wait(pool, s["zn_ready"], g)
                        nc.gpsimd.tensor_tensor(zv, zv, row_gamma[:, :].unsqueeze(1).to_broadcast(wide), ALU.mult).then_inc(s["scaled"], 1)
                        wait(pool, s["scaled"], g)
                        nc.gpsimd.tensor_tensor(zv, zv, row_beta[:, :].unsqueeze(1).to_broadcast(wide), ALU.add).then_inc(s["moved"], 1)
                        wait(pool, s["moved"], g)
                        nc.gpsimd.tensor_tensor(xv, xv, zv, ALU.add).then_inc(s["x_done"], 1)

                pipeline(pool, step, NGB)

            @block.scalar
            def _(act):
                act.wait_ge(s["var_ready"], 1)
                nc.scalar.activation(m.sd[:, :], m.var[:, :], ACT.Sqrt, bias=m.eps[:, 0:1]).then_inc(s["sd_ready"], 1)
                act.wait_ge(s["loaded"], 16 * 9)

                def step(g, par, front, middle, back):
                    nxt = 1 - par
                    if middle:
                        wait(act, s["y_done"], g - 1)
                        for c in range(chunks):
                            wait(act, s["hidden_in_psum"], g * chunks + c + 1)
                            nc.scalar.activation(hid[:, par, c, :], m.psum[:, c, :], ACT.Relu, bias=b1[:, c:c + 1]).then_inc(s["hidden_ready"], 1)
                    if front:
                        wait(act, s["xt_in_psum"], g + 2)
                        nc.scalar.copy(xt[:, nxt, :], m.psum[:, 5, :]).then_inc(s["xt_ready"], 1)
                    if back:
                        wait(act, s["z_var_ready"], g)
                        nc.scalar.activation(sd[:, :], var[:, :], ACT.Sqrt, bias=m.eps[:, 0:1]).then_inc(s["z_sd_ready"], 1)

                pipeline(act, step, NGB)

            @block.vector
            def _(dve):
                variance_of_x(nc, m, dve, s["parts_ready"], s["var_ready"])
                dve.wait_ge(s["loaded"], 16 * 9)
                gate = m.gate[:, 5:6]
                nc.vector.tensor_scalar(row_gamma[:, :], row_gamma[:, :], gate, None, ALU.mult).then_inc(s["rows_ready"], 1)
                nc.vector.tensor_scalar(row_beta[:, :], row_beta[:, :], gate, None, ALU.mult).then_inc(s["rows_ready"], 1)
                rstd_of_x(nc, m, dve, s["sd_ready"], s["rstd_ready"], s["shift_ready"])

                def step(g, par, front, middle, back):
                    nxt = 1 - par
                    if front:
                        wait(dve, s["xt_in_psum"], g)
                        wait(dve, s["base_ready"], g)
                        for t in range(GB):
                            at = (g + 1) * GB + t
                            ins = nc.vector.tensor_scalar(xn[:, nxt, t, :], m.x[:, at, :], m.rstd[:, bass.ds(at, 1)],
                                                          m.shift[:, bass.ds(at, 1)], ALU.mult, ALU.add)
                        ins.then_inc(s["xn_ready"], 1)
                    if back:
                        link = chain(dve, s["link"], g - 1, LINKS)
                        wait(dve, s["y_done"], g)
                        wait(dve, s["base_ready"], g)
                        wait(dve, s["x_done"], g - 2)
                        zv = z[:, nxt, :, :]
                        nc.vector.tensor_tensor(zv, m.psum[:, 4, :].rearrange("p (t d) -> p t d", d=D), base[:, nxt, :, :],
                                                ALU.add).then_inc(s["z_ready"], 1)
                        wait(dve, s["z_ready"], g)
                        for t in range(GB):
                            ins = nc.vector.bn_stats(zst[:, t, :], zv[:, t, :])
                        link(ins)
                        me, qe, mo, qo = (zst[:, :, c] for c in (1, 2, 4, 5))
                        nc.vector.tensor_tensor(mean2[:, :], me, mo, ALU.add)
                        link(nc.vector.tensor_tensor(halves[:, :], me, mo, ALU.subtract))
                        link(nc.vector.tensor_tensor(var[:, :], qe, qo, ALU.add))
                        link(nc.vector.scalar_tensor_tensor(halves[:, :], halves[:, :], 0.25, halves[:, :], ALU.mult, ALU.mult))
                        nc.vector.scalar_tensor_tensor(var[:, :], var[:, :], 1.0 / D, halves[:, :], ALU.mult, ALU.add)\
                            .then_inc(s["z_var_ready"], 1)
                        wait(dve, s["z_sd_ready"], g)
                        link(nc.vector.reciprocal(rstd[:, :], sd[:, :]))
                        link(nc.vector.scalar_tensor_tensor(shift[:, :], mean2[:, :], -0.5, rstd[:, :], ALU.mult, ALU.mult))
                        for t in range(GB):
                            ins = nc.vector.tensor_scalar(zv[:, t, :], zv[:, t, :], rstd[:, t:t + 1], shift[:, t:t + 1], ALU.mult, ALU.add)
                        ins.then_inc(s["zn_ready"], 1)

                pipeline(dve, step, NGB)
                dve.wait_ge(s["x_done"], NGB)
                for b in range(B):
                    nc.vector.bn_stats(m.moments[:, b, :], m.x[:, b, :])

            @block.tensor
            def _(pe):
                pe.wait_ge(s["loaded"], 16 * 9)

                def step(g, par, front, middle, back):
                    nxt = 1 - par
                    if middle:
                        wait(pe, s["xt_ready"], g + 1)
                        wait(pe, s["hidden_ready"], g * chunks)
                        for c in range(chunks):
                            nc.tensor.matmul(m.psum[:, c, :], up[:, c * 128:(c + 1) * 128], xt[:, par, :], start=True, stop=True)\
                                .then_inc(s["hidden_in_psum"], 1)
                    if back:
                        wait(pe, s["hidden_ready"], g * chunks)
                        wait(pe, s["z_ready"], g - 1)
                        for t in range(GB):
                            for c in range(chunks):
                                mm = nc.tensor.matmul(m.psum[:, 4, t * D:(t + 1) * D], hid[:, nxt, c, t * S:(t + 1) * S], down[:, c, :],
                                                      start=(c == 0), stop=(c == chunks - 1))
                        mm.then_inc(s["y_done"], 1)
                    if front:
                        wait(pe, s["xn_ready"], g + 2)
                        wait(pe, s["xt_ready"], g + 1)
                        for t in range(GB):
                            mm = nc.tensor.transpose(m.psum[:, 5, t * S:(t + 1) * S], xn[:, nxt, t, :], m.ident[:, :])
                        mm.then_inc(s["xt_in_psum"], 1)

                pipeline(pe, step, NGB)


def controller_feed_forward(nc, m, sem, clear):
    names = ("parts_ready var_ready sd_ready rstd_ready shift_ready loaded ones_ready row_ready xn_ready xt_in_psum xt_ready "
             "low_in_psum low_ready logits_in_psum full_in_psum bias_added top_ready ge_ready coded code_ready first_ready full_ready picked_ready "
             "rt_in_psum rt_ready y_done x_done")
    s = {n: sem(f"{n}_ffn2") for n in names.split()}
    gate = m.gate[:, 6:7]
    a = m.a
    HID = MX * MY
    CH = HID // 128
    with ExitStack() as ctx:
        def sb(name, shape, dtype=F32):
            return ctx.enter_context(nc.sbuf_tensor(f"{name}_ffn2", shape, dtype))

        xn = sb("xn", [S, 2, D])
        xt = sb("xt", [D, 2, S])
        low = sb("low_rank", [ML + 1, 2, S])
        m1, m2 = sb("m1", [D, ML]), sb("m2_and_mb", [ML + 1, HID])
        w1, w2 = sb("w1", [D, HID]), sb("w2", [128, CH, D])
        row_b2 = sb("b2_row", [S, D])
        full = sb("all_hidden", [S, 2, HID])
        top = sb("top_logit", [S, MX])
        code = sb("pick_code", [S, MX])
        pick = sb("pick", [S, 2, MX, MY])
        rt = sb("picked_transposed", [128, CH * S])
        with nc.Block() as block:
            @block.sync
            def _(sync):
                loads = [(m1[:, :], a["L2_ffn_m1"]), (m2[0:ML, :], a["L2_ffn_m2"].rearrange("l x y -> l (x y)")),
                         (m2[ML:ML + 1, :], a["L2_ffn_mb"].rearrange("(o x) y -> o (x y)", o=1)),
                         (w1[:, :], a["L2_ffn_w1"].rearrange("d x y -> d (x y)")), (row_b2[:, :], row_of(a["L2_ffn_b2"]))]
                w2_blocks = a["L2_ffn_w2"].rearrange("y (c i) d -> i y c d", i=2)
                loads += [(w2[i * MY:(i + 1) * MY, :, :], w2_blocks[i]) for i in range(2)]
                for to, of in loads:
                    sync.dma_start(to, of).then_inc(s["loaded"], 16)

            @block.gpsimd
            def _(pool):
                clear(pool)
                nc.gpsimd.memset(low[ML:ML + 1, :, :], 1.0).then_inc(s["ones_ready"], 1)
                pool.wait_ge(s["ones_ready"], 1)
                pool.wait_ge(s["row_ready"], 1)

                def step(b, par, front, middle, back, tail):
                    if front:
                        wait(pool, s["xn_ready"], b + 2)
                        nc.gpsimd.tensor_tensor(m.x[:, b + 1, :], m.x[:, b + 1, :], row_b2[:, :], ALU.add).then_inc(s["bias_added"], 1)
                    if middle:
                        wait(pool, s["ge_ready"], b + 1)
                        pv = pick[:, par, :, :]
                        nc.gpsimd.tensor_tensor(pv, pv, m.down[:, 0:MY].unsqueeze(1).to_broadcast([S, MX, MY]), ALU.mult).then_inc(s["coded"], 1)

                pipeline4(pool, step)

            @block.scalar
            def _(act):
                act.wait_ge(s["var_ready"], 1)
                nc.scalar.activation(m.sd[:, :], m.var[:, :], ACT.Sqrt, bias=m.eps[:, 0:1]).then_inc(s["sd_ready"], 1)

                def step(b, par, front, middle, back, tail):
                    nxt = 1 - par
                    if front:
                        wait(act, s["xt_in_psum"], b + 2)
                        wait(act, s["full_in_psum"], b)
                        nc.scalar.copy(xt[:, nxt, :], m.psum[:, 0, 0:S]).then_inc(s["xt_ready"], 1)
                        wait(act, s["low_in_psum"], b + 2)
                        wait(act, s["logits_in_psum"], b)
                        nc.scalar.copy(low[0:ML, nxt, :], m.psum[0:ML, 0, S:2 * S]).then_inc(s["low_ready"], 1)
                    if back:
                        wait(act, s["rt_in_psum"], b)
                        wait(act, s["y_done"], b - 1)
                        nc.scalar.copy(rt[:, :], m.psum[:, 5, :]).then_inc(s["rt_ready"], 1)
                    if middle:
                        wait(act, s["full_in_psum"], b + 1)
                        wait(act, s["picked_ready"], b - 1)
                        nc.scalar.activation(full[:, par, :], m.psum[:, 3 + par, :], ACT.Relu).then_inc(s["full_ready"], 1)

                pipeline4(act, step)

            @block.vector
            def _(dve):
                variance_of_x(nc, m, dve, s["parts_ready"], s["var_ready"])
                rstd_of_x(nc, m, dve, s["sd_ready"], s["rstd_ready"], s["shift_ready"])
                dve.wait_ge(s["loaded"], 16 * 7)
                nc.vector.tensor_scalar(row_b2[:, :], row_b2[:, :], gate, None, ALU.mult).then_inc(s["row_ready"], 1)
                wide = [S, MX, MY]

                def step(b, par, front, middle, back, tail):
                    nxt = 1 - par
                    if front:
                        wait(dve, s["xt_in_psum"], b)
                        nc.vector.tensor_scalar(xn[:, nxt, :], m.x[:, b + 1, :], m.rstd[:, bass.ds(b + 1, 1)],
                                                m.shift[:, bass.ds(b + 1, 1)], ALU.mult, ALU.add).then_inc(s["xn_ready"], 1)
                    if back:
                        pv = pick[:, nxt, :, :]
                        wait(dve, s["coded"], b)
                        nc.vector.tensor_reduce(code[:, :], pv, AX.X, ALU.max).then_inc(s["code_ready"], 1)
                    if back:
                        wait(dve, s["code_ready"], b)
                        nc.vector.tensor_tensor(pv, pv, code[:, :].unsqueeze(2).to_broadcast(wide), ALU.is_equal).then_inc(s["first_ready"], 1)
                    if tail:
                        wait(dve, s["y_done"], b - 1)
                        wait(dve, s["bias_added"], b - 1)
                        nc.vector.scalar_tensor_tensor(m.x[:, b - 2, :], m.psum[:, 6, 0:D], gate, m.x[:, b - 2, :],
                                                       ALU.mult, ALU.add).then_inc(s["x_done"], 1)
                    if middle:
                        wait(dve, s["logits_in_psum"], b + 1)
                        logits = m.psum[:, 1 + par, :].rearrange("p (x y) -> p x y", y=MY)
                        nc.vector.tensor_reduce(top[:, :], logits, AX.X, ALU.max).then_inc(s["top_ready"], 1)
                    if back:
                        wait(dve, s["first_ready"], b)
                        wait(dve, s["full_ready"], b)
                        pf = pv.rearrange("p x y -> p (x y)")
                        nc.vector.tensor_tensor(pf, pf, full[:, nxt, :], ALU.mult).then_inc(s["picked_ready"], 1)
                    if middle:
                        wait(dve, s["top_ready"], b + 1)
                        wait(dve, s["rt_in_psum"], b - 1)
                        nc.vector.tensor_tensor(pick[:, par, :, :], logits, top[:, :].unsqueeze(2).to_broadcast(wide),
                                                ALU.is_ge).then_inc(s["ge_ready"], 1)
                    if tail:
                        wait(dve, s["x_done"], b - 1)
                        nc.vector.bn_stats(m.moments[:, b - 2, :], m.x[:, b - 2, :])

                pipeline4(dve, step)

            @block.tensor
            def _(pe):
                pe.wait_ge(s["loaded"], 16 * 7)
                pe.wait_ge(s["ones_ready"], 1)

                def step(b, par, front, middle, back, tail):
                    nxt = 1 - par
                    if front:
                        wait(pe, s["xn_ready"], b + 2)
                        wait(pe, s["low_ready"], b + 1)
                        nc.tensor.transpose(m.psum[:, 0, 0:S], xn[:, nxt, :], m.ident[:, :]).then_inc(s["xt_in_psum"], 1)
                    if tail:
                        wait(pe, s["rt_ready"], b - 1)
                        wait(pe, s["x_done"], b - 2)
                        for c in range(CH):
                            mm = nc.tensor.matmul(m.psum[:, 6, 0:D], rt[:, c * S:(c + 1) * S], w2[:, c, :], start=(c == 0), stop=(c == CH - 1))
                        mm.then_inc(s["y_done"], 1)
                    if middle:
                        wait(pe, s["low_ready"], b + 1)
                        wait(pe, s["ge_ready"], b - 1)
                        nc.tensor.matmul(m.psum[:, 1 + par, :], low[:, par, :], m2[:, :], start=True, stop=True).then_inc(s["logits_in_psum"], 1)
                    if front:
                        wait(pe, s["xt_ready"], b + 2)
                        nc.tensor.matmul(m.psum[0:ML, 0, S:2 * S], m1[:, :], xt[:, nxt, :], start=True, stop=True).then_inc(s["low_in_psum"], 1)
                    if middle:
                        wait(pe, s["full_ready"], b - 1)
                        nc.tensor.matmul(m.psum[:, 3 + par, :], xt[:, par, :], w1[:, :], start=True, stop=True).then_inc(s["full_in_psum"], 1)
                    if back:
                        wait(pe, s["picked_ready"], b)
                        wait(pe, s["rt_ready"], b - 1)
                        for c in range(CH):
                            mm = nc.tensor.transpose(m.psum[:, 5, c * S:(c + 1) * S],
                                                     pick[:, nxt, :, :].rearrange("p x y -> p (x y)")[:, c * 128:(c + 1) * 128], m.ident[:, :])
                        mm.then_inc(s["rt_in_psum"], 1)

                pipeline4(pe, step)


def latent_attention(nc, m, sem, clear):
    names = ("parts_ready var_ready sd_ready rstd_ready shift_ready loaded ctx_parts ctx_var ctx_sd ctx_rstd ctx_shift "
             "lat_var lat_sd lat_rstd lat_scale lat_shift "
             "prep_psum prep_read rows_ready cn_raw cn_scaled cn_ready ln_raw ln_scaled ln_ready kvt_in_psum kvt_ready "
             "q_in_psum q_ready scores_done negmax_ready shifted exp_ready sum_ready recip_ready probs_ready pt_in_psum "
             "pt_read_act pt_read_dve c_in_psum c_ready y_done x_done bias_added w_ready kept")
    s = {n: sem(f"{n}_3") for n in names.split()}
    gate = m.gate[:, 3:4]
    a = m.a
    SCALE = D ** -0.5
    with ExitStack() as ctx:
        def sb(name, shape, dtype=F32):
            return ctx.enter_context(nc.sbuf_tensor(f"{name}_xattn3", shape, dtype))

        wq, wkv, wo = sb("wq", [D, H3 * D]), sb("wkv", [D, 2, H3 * D]), sb("wo", [D, H3, D])
        b_rows = sb("bias_rows", [H3, 2, D])
        b_cols = sb("bias_columns", [D, 2, H3])
        bv_wide = sb("bv_wide", [D, H3, S])
        w_t = sb("weights_transposed", [D, 3, H3, D])
        w_qk, w_vo = sb("w_qk", [D, H3, D]), sb("w_vo", [D, H3, D])
        t0 = sb("key_weights_times_bq", [D, H3])
        row_out = sb("output_bias_row", [S, D])
        rows = sb("norm_rows", [S, 4, D])
        c_moments = sb("context_moments", [KC, B, 6])
        c_mean2, c_half, c_var, c_sd, c_rstd, c_shift = (sb(f"context_{n}", [KC, B]) for n in ("mean2", "half", "var", "sd", "rstd", "shift"))
        l_var, l_sd, l_scale, l_shift = (sb(f"latent_{n}", [S, B]) for n in ("var", "sd", "scale", "shift"))
        kn = sb("kv_before_beta", [S, 2, 2, D])
        kv = sb("kv", [S, 2, 2, D])
        kept = sb("kv_kept", [S, 2, 2, D])
        kvt = sb("kv_transposed", [D, 2, KV])
        q = sb("queries", [D, 2, H3, S])
        e = sb("exp_scores", [S, 2, H3, KV])
        negmax = sb("negated_max", [S, 2, H3], BF16)
        total, recip = sb("softmax_sum", [S, 2, H3]), sb("softmax_recip", [S, 2, H3])
        ptc, ptl = sb("probs_t_context", [KC, H3 * S]), sb("probs_t_latents", [S, H3 * S])
        c = sb("heads_out", [D, H3, S])
        HB = 2
        HH = 4
        Q_BANKS = (6, 4)
        PREP = 3 * H3 // 4 + 1
        with nc.Block() as block:
            @block.sync
            def _(sync):
                loads = [(wq[:, :], a["L3_xattn_Wq"]), (wkv[:, :, :], a["L3_xattn_Wkv"].rearrange("d (t n) -> d t n", t=2)),
                         (wo[:, :, :], a["L3_xattn_Wo"].rearrange("(h c) d -> c h d", c=D)),
                         (b_rows[:, 0, :], a["L3_xattn_bq"].rearrange("(h c) -> h c", c=D)),
                         (b_rows[:, 1, :], a["L3_xattn_bkv"][H3 * D:2 * H3 * D].rearrange("(h c) -> h c", c=D)),
                         (row_out[:, :], row_of(a["L3_xattn_bo"]))]
                loads += [(rows[:, i, :], row_of(a[f"L3_xattn_{n}"])) for i, n in enumerate(("gamma_media", "beta_media", "gamma_lat", "beta_lat"))]
                for to, of in loads:
                    sync.dma_start(to, of).then_inc(s["loaded"], 16)

            LOADED = 16 * 10

            @block.gpsimd
            def _(pool):
                clear(pool)
                pool.wait_ge(s["loaded"], LOADED)
                pool.wait_ge(s["rows_ready"], 1)

                def step(b, par, front, middle, back):
                    nxt = 1 - par
                    if front:
                        for part, raw, scaled, ready, n in ((0, "cn_raw", "cn_scaled", "cn_ready", KC), (1, "ln_raw", "ln_scaled", "ln_ready", S)):
                            t = kn[0:n, nxt, part, :]
                            wait(pool, s[raw], b + 2)
                            nc.gpsimd.tensor_tensor(t, t, rows[0:n, 2 * part, :], ALU.mult).then_inc(s[scaled], 1)
                            wait(pool, s[scaled], b + 2)
                            nc.gpsimd.tensor_tensor(kv[0:n, nxt, part, :], t, rows[0:n, 2 * part + 1, :], ALU.add).then_inc(s[ready], 1)
                        nc.gpsimd.tensor_tensor(m.x[:, b + 1, :], m.x[:, b + 1, :], row_out[:, :], ALU.add).then_inc(s["bias_added"], 1)
                    if middle:
                        wait(pool, s["c_in_psum"], (b - 1) * 2)
                        nc.gpsimd.tensor_tensor(kept[0:KC, par, 0, :], kn[0:KC, par, 0, :], rows[0:KC, 1, :], ALU.add).then_inc(s["kept"], 1)
                        nc.gpsimd.tensor_tensor(kept[:, par, 1, :], kn[:, par, 1, :], rows[:, 3, :], ALU.add).then_inc(s["kept"], 1)
                        wait(pool, s["recip_ready"], b + 1)
                        ev = e[:, par, :, :]
                        nc.gpsimd.tensor_tensor(ev, ev, recip[:, par, :].unsqueeze(2).to_broadcast([S, H3, KV]), ALU.mult).then_inc(s["probs_ready"], 1)

                pipeline(pool, step)

            @block.scalar
            def _(act):
                act.wait_ge(s["var_ready"], 1)
                nc.scalar.activation(m.sd[:, :], m.var[:, :], ACT.Sqrt, bias=m.eps[:, 0:1]).then_inc(s["sd_ready"], 1)
                act.wait_ge(s["lat_var"], 1)
                nc.scalar.activation(l_sd[:, :], l_var[:, :], ACT.Sqrt, bias=m.eps[:, 0:1]).then_inc(s["lat_sd"], 1)
                act.wait_ge(s["ctx_var"], 1)
                nc.scalar.activation(c_sd[:, :], c_var[:, :], ACT.Sqrt, bias=m.eps[0:KC, 0:1]).then_inc(s["ctx_sd"], 1)
                for n in range(PREP - 1):
                    act.wait_ge(s["prep_psum"], n + 1)
                    nc.scalar.copy(w_t[:, n // 2, HH * (n % 2):HH * (n % 2) + HH, :].rearrange("p h c -> p (h c)"), m.psum[:, n, :]).then_inc(s["prep_read"], 1)
                act.wait_ge(s["prep_psum"], PREP + 1)
                nc.scalar.copy(w_qk[:, :, :].rearrange("p (n h) c -> p n (h c)", n=2), m.psum[:, 0:2, :]).then_inc(s["w_ready"], 1)
                act.wait_ge(s["prep_psum"], PREP + 2)
                nc.scalar.copy(w_vo[:, :, :].rearrange("p (n h) c -> p n (h c)", n=2), m.psum[:, 2:4, :]).then_inc(s["w_ready"], 1)

                def step(b, par, front, middle, back):
                    nxt = 1 - par
                    if front:
                        wait(act, s["kvt_in_psum"], b + 2)
                        wait(act, s["scores_done"], b)
                        nc.scalar.copy(kvt[:, nxt, :], m.psum[:, 7, 0:KV]).then_inc(s["kvt_ready"], 1)
                    if back:
                        wait(act, s["c_in_psum"], (b - 1) * 2)
                        wait(act, s["pt_in_psum"], (b - 1) * 4 + 1)
                        nc.scalar.copy(ptc[:, 0:512], m.psum[0:KC, 6, :]).then_inc(s["pt_read_act"], 1)
                        wait(act, s["pt_in_psum"], (b - 1) * 4 + 3)
                        nc.scalar.copy(ptl[:, 0:512], m.psum[:, 5, :]).then_inc(s["pt_read_act"], 1)
                    if middle:
                        wait(act, s["shifted"], b + 1)
                        wait(act, s["pt_in_psum"], (b - 1) * 4)
                        nc.scalar.activation(e[:, par, :, :].rearrange("p (n h) k -> p n (h k)", h=HB), m.psum[:, 0:4, 0:HB * KV],
                                             ACT.Exp, scale=SCALE).then_inc(s["exp_ready"], 1)
                    if back:
                        for n in range(2):
                            wait(act, s["y_done"], b - 1)
                            wait(act, s["c_in_psum"], (b - 1) * 2 + n + 1)
                            nc.scalar.copy(c[:, n * HH:(n + 1) * HH, :].rearrange("p h t -> p (h t)"), m.psum[:, 4 + n, :]).then_inc(s["c_ready"], 1)

                pipeline(act, step)

            @block.vector
            def _(dve):
                variance_of_x(nc, m, dve, s["parts_ready"], s["var_ready"])
                for b in range(B):
                    nc.vector.bn_stats(c_moments[:, b, :], m.ctx[:, b, :])
                rstd_of_x(nc, m, dve, s["sd_ready"], s["rstd_ready"], s["shift_ready"])
                nc.vector.tensor_tensor(l_var[:, :], m.rstd[:, :], m.rstd[:, :], ALU.mult).then_inc(s["lat_scale"], 1)
                dve.wait_ge(s["lat_scale"], 1)
                nc.vector.tensor_tensor(l_var[:, :], l_var[:, :], m.var[:, :], ALU.mult).then_inc(s["lat_var"], 1)
                me, qe, mo, qo = (c_moments[:, :, k] for k in (1, 2, 4, 5))
                dve.wait_ge(s["lat_var"], 1)
                nc.vector.tensor_tensor(c_mean2[:, :], me, mo, ALU.add).then_inc(s["ctx_parts"], 1)
                nc.vector.tensor_tensor(c_half[:, :], me, mo, ALU.subtract).then_inc(s["ctx_parts"], 1)
                nc.vector.tensor_tensor(c_var[:, :], qe, qo, ALU.add).then_inc(s["ctx_parts"], 1)
                dve.wait_ge(s["ctx_parts"], 3)
                nc.vector.scalar_tensor_tensor(c_half[:, :], c_half[:, :], 0.25, c_half[:, :], ALU.mult, ALU.mult).then_inc(s["ctx_parts"], 1)
                dve.wait_ge(s["ctx_parts"], 4)
                nc.vector.scalar_tensor_tensor(c_var[:, :], c_var[:, :], 1.0 / D, c_half[:, :], ALU.mult, ALU.add).then_inc(s["ctx_var"], 1)
                dve.wait_ge(s["lat_sd"], 1)
                nc.vector.reciprocal(l_scale[:, :], l_sd[:, :]).then_inc(s["lat_rstd"], 1)
                dve.wait_ge(s["lat_rstd"], 1)
                nc.vector.tensor_tensor(l_shift[:, :], l_scale[:, :], m.shift[:, :], ALU.mult).then_inc(s["lat_shift"], 1)
                nc.vector.tensor_tensor(l_scale[:, :], l_scale[:, :], m.rstd[:, :], ALU.mult).then_inc(s["lat_shift"], 1)
                dve.wait_ge(s["ctx_sd"], 1)
                nc.vector.reciprocal(c_rstd[:, :], c_sd[:, :]).then_inc(s["ctx_rstd"], 1)
                dve.wait_ge(s["ctx_rstd"], 1)
                nc.vector.scalar_tensor_tensor(c_shift[:, :], c_mean2[:, :], -0.5, c_rstd[:, :], ALU.mult, ALU.mult).then_inc(s["ctx_shift"], 1)
                dve.wait_ge(s["ctx_shift"], 1)
                dve.wait_ge(s["lat_shift"], 2)
                dve.wait_ge(s["prep_psum"], PREP)
                nc.vector.tensor_copy(b_cols[:, :, :].rearrange("p t h -> p (t h)"), m.psum[:, 6, 0:2 * H3]).then_inc(s["prep_read"], 1)
                dve.wait_ge(s["prep_read"], PREP)
                nc.vector.tensor_copy(bv_wide[:, :, :], b_cols[:, 1, :].unsqueeze(2).to_broadcast([D, H3, S])).then_inc(s["prep_read"], 1)
                dve.wait_ge(s["prep_psum"], PREP + 3)
                nc.vector.tensor_copy(t0[:, :], m.psum[:, 4, 0:H3]).then_inc(s["w_ready"], 1)
                nc.vector.tensor_tensor(row_out[:, :], row_out[:, :], m.psum[:, 5, 0:D], ALU.add).then_inc(s["w_ready"], 1)
                dve.wait_ge(s["w_ready"], 4)
                nc.vector.tensor_scalar(row_out[:, :], row_out[:, :], gate, None, ALU.mult).then_inc(s["rows_ready"], 1)

                def step(b, par, front, middle, back):
                    nxt = 1 - par
                    if front:
                        wait(dve, s["kvt_in_psum"], b)
                        wait(dve, s["kept"], b * 2)
                        nc.vector.tensor_scalar(kn[0:KC, nxt, 0, :], m.ctx[:, b + 1, :], c_rstd[:, bass.ds(b + 1, 1)],
                                                c_shift[:, bass.ds(b + 1, 1)], ALU.mult, ALU.add).then_inc(s["cn_raw"], 1)
                        nc.vector.tensor_scalar(kn[:, nxt, 1, :], m.x[:, b + 1, :], l_scale[:, bass.ds(b + 1, 1)],
                                                l_shift[:, bass.ds(b + 1, 1)], ALU.mult, ALU.add).then_inc(s["ln_raw"], 1)

                def middle_one(b, par):
                    wait(dve, s["scores_done"], b + 1)
                    wait(dve, s["shifted"], b - 1)
                    sv = m.psum[:, 0:4, 0:HB * KV].rearrange("p n (h k) -> p n h k", h=HB)
                    nc.vector.tensor_reduce(negmax[:, par, :].rearrange("p (n h) -> p n h", h=HB), sv, AX.X, ALU.max, negate=True).then_inc(s["negmax_ready"], 1)

                def full(b, par, front, middle, back):
                    nxt = 1 - par
                    step(b, par, front, middle, back)
                    if middle:
                        middle_one(b, par)
                    if back:
                        wait(dve, s["c_in_psum"], (b - 1) * 2)
                        wait(dve, s["pt_in_psum"], (b - 1) * 4 + 2)
                        nc.vector.tensor_copy(ptc[:, 512:1024], m.psum[0:KC, 4, :]).then_inc(s["pt_read_dve"], 1)
                        wait(dve, s["pt_in_psum"], (b - 1) * 4 + 4)
                        nc.vector.tensor_copy(ptl[:, 512:1024], m.psum[:, 6, :]).then_inc(s["pt_read_dve"], 1)
                    if middle:
                        wait(dve, s["exp_ready"], b + 1)
                        nc.vector.tensor_reduce(total[:, par, :], e[:, par, :, :], AX.X, ALU.add).then_inc(s["sum_ready"], 1)
                        wait(dve, s["sum_ready"], b + 1)
                        wait(dve, s["probs_ready"], b - 1)
                        nc.vector.reciprocal(recip[:, par, :], total[:, par, :]).then_inc(s["recip_ready"], 1)
                    if front:
                        for n in range(2):
                            wait(dve, s["q_in_psum"], (b + 1) * 2 + n + 1)
                            wait(dve, s["scores_done"], b)
                            nc.vector.tensor_tensor(q[:, nxt, n * HH:(n + 1) * HH, :], m.psum[:, Q_BANKS[n], :].rearrange("p (h t) -> p h t", h=HH),
                                                    t0[:, n * HH:(n + 1) * HH].unsqueeze(2).to_broadcast([D, HH, S]), ALU.add).then_inc(s["q_ready"], 1)
                    if back:
                        wait(dve, s["y_done"], b)
                        wait(dve, s["bias_added"], b)
                        nc.vector.scalar_tensor_tensor(m.x[:, b - 1, :], m.psum[:, 7, 256:256 + D], gate, m.x[:, b - 1, :],
                                                       ALU.mult, ALU.add).then_inc(s["x_done"], 1)

                pipeline(dve, full)
                dve.wait_ge(s["x_done"], B)
                for b in range(B):
                    nc.vector.bn_stats(m.moments[:, b, :], m.x[:, b, :])

            @block.tensor
            def _(pe):
                pe.wait_ge(s["loaded"], LOADED)
                for n in range(PREP - 1):
                    for h in range(HH):
                        head = HH * (n % 2) + h
                        w = wq[:, head * D:(head + 1) * D] if n < 2 else wkv[:, n // 2 - 1, head * D:(head + 1) * D]
                        mm = nc.tensor.transpose(m.psum[:, n, h * D:(h + 1) * D], w, m.ident[:, :])
                    mm.then_inc(s["prep_psum"], 1)
                for t in range(2):
                    mm = nc.tensor.transpose(m.psum[:, 6, t * H3:(t + 1) * H3], b_rows[:, t, :], m.ident[0:H3, 0:H3])
                mm.then_inc(s["prep_psum"], 1)
                pe.wait_ge(s["prep_read"], PREP + 1)
                for h in range(H3):
                    mm = nc.tensor.matmul(m.psum[:, h // HH, (h % HH) * D:(h % HH + 1) * D], w_t[:, 0, h, :], w_t[:, 1, h, :], start=True, stop=True)
                mm.then_inc(s["prep_psum"], 1)
                for h in range(H3):
                    mm = nc.tensor.matmul(m.psum[:, 2 + h // HH, (h % HH) * D:(h % HH + 1) * D], w_t[:, 2, h, :], wo[:, h, :], start=True, stop=True)
                mm.then_inc(s["prep_psum"], 1)
                for h in range(H3):
                    nc.tensor.matmul(m.psum[:, 4, h:h + 1], w_t[:, 1, h, :], b_cols[:, 0, h:h + 1], start=True, stop=True)
                for h in range(H3):
                    mm = nc.tensor.matmul(m.psum[:, 5, 0:D], bv_wide[:, h, :], wo[:, h, :], start=(h == 0), stop=(h == H3 - 1))
                mm.then_inc(s["prep_psum"], 1)
                pe.wait_ge(s["w_ready"], 4)

                def step(b, par, front, middle, back):
                    nxt = 1 - par
                    if middle:
                        wait(pe, s["q_ready"], (b + 1) * 2)
                        wait(pe, s["exp_ready"], b)
                        for h in range(H3):
                            mm = nc.tensor.matmul(m.psum[:, h // HB, (h % HB) * KV:(h % HB + 1) * KV], q[:, par, h, :], kvt[:, par, :],
                                                  start=(h % HB == 0), stop=True, skip_group_check=True)
                        mm.then_inc(s["scores_done"], 1)
                    if front:
                        wait(pe, s["cn_ready"], b + 2)
                        wait(pe, s["ln_ready"], b + 2)
                        wait(pe, s["kvt_ready"], b + 1)
                        wait(pe, s["x_done"], b - 1)
                        nc.tensor.transpose(m.psum[:, 7, 0:KC], kv[0:KC, nxt, 0, :], m.ident[0:KC, 0:KC])
                        nc.tensor.transpose(m.psum[:, 7, KC:KV], kv[:, nxt, 1, :], m.ident[:, :]).then_inc(s["kvt_in_psum"], 1)
                    if back:
                        wait(pe, s["probs_ready"], b)
                        wait(pe, s["q_ready"], b * 2) if not middle else None
                        wait(pe, s["c_ready"], (b - 1) * 2)
                        for n, (bank, keys, half) in enumerate(((6, 0, 0), (4, 0, 1), (5, 1, 0), (6, 1, 1))):
                            k0, k1 = (0, KC) if keys == 0 else (KC, KV)
                            if n == 0:
                                wait(pe, s["pt_read_dve"], (b - 1) * 2)
                            if n == 3:
                                wait(pe, s["pt_read_act"], (b - 1) * 2 + 1)
                            for h in range(HH):
                                mm = nc.tensor.transpose(m.psum[0:k1 - k0, bank, h * S:(h + 1) * S], e[:, nxt, half * HH + h, k0:k1], m.ident[:, :])
                            mm.then_inc(s["pt_in_psum"], 1)
                    if middle:
                        wait(pe, s["negmax_ready"], b + 1)
                        for n in range(4):
                            mm = nc.tensor.matmul(m.psum[:, n, 0:HB * KV].rearrange("p (h k) -> p h k", k=KV), m.ident_bf[:, :],
                                                  negmax[:, par, n * HB:(n + 1) * HB].unsqueeze(2).to_broadcast([S, HB, KV]),
                                                  start=False, stop=True, skip_group_check=True)
                        mm.then_inc(s["shifted"], 1)
                    if back:
                        wait(pe, s["kept"], b * 2)
                        for half in range(2):
                            wait(pe, s["pt_read_act"], b * 2)
                            wait(pe, s["pt_read_dve"], b * 2 - 1 + half)
                            cols = slice(half * 512, (half + 1) * 512)
                            nc.tensor.matmul(m.psum[:, 4 + half, :], kept[0:KC, nxt, 0, :], ptc[:, cols], start=True, stop=False)
                            nc.tensor.matmul(m.psum[:, 4 + half, :], kept[:, nxt, 1, :], ptl[:, cols], start=False, stop=True).then_inc(s["c_in_psum"], 1)
                    if front:
                        wait(pe, s["kvt_ready"], b + 2)
                        for n in range(2):
                            if n == 0 and back:
                                wait(pe, s["pt_read_dve"], b * 2)
                            if n == 1 and back:
                                wait(pe, s["c_ready"], b * 2 - 1)
                            for h in range(HH):
                                mm = nc.tensor.matmul(m.psum[:, Q_BANKS[n], h * S:(h + 1) * S], w_qk[:, n * HH + h, :], kvt[:, nxt, KC:KV],
                                                      start=True, stop=True)
                            mm.then_inc(s["q_in_psum"], 1)
                    if back:
                        wait(pe, s["c_ready"], b * 2)
                        for h in range(H3):
                            mm = nc.tensor.matmul(m.psum[:, 7, 256:256 + D], c[:, h, :], w_vo[:, h, :], start=(h == 0), stop=(h == H3 - 1))
                        mm.then_inc(s["y_done"], 1)

                pipeline(pe, step)


def store(nc, m, a, sem):
    stored = sem("stored")
    with nc.Block() as block:
        @block.sync
        def _(sync):
            sync.dma_start(a["out"].rearrange("b s d -> s b d"), m.x[:, :, :]).then_inc(stored, 16)
            sync.wait_ge(stored, 16)


def program(nc, a, last_phase=99, first_phase=0):
    with ExitStack() as ctx:
        m = allocate(nc, ctx)
        m.a = a
        previous = []

        def phase(build, *args):
            held = []

            def sem(name):
                held.append(nc.alloc_semaphore(name))
                return held[-1]

            def clear(pool):
                for old in previous:
                    pool.sem_clear(old)

            build(nc, m, sem, *args, clear)
            for old in previous:
                nc.release_semaphore(old)
            previous[:] = held

        prepare(nc, ctx, m, a)
        if first_phase < 1 <= last_phase:
            phase(head_attention, 0, (m.wq0, m.wk0, m.wv0, m.wo0))
        if first_phase < 2 <= last_phase:
            phase(experts, 0, m.router_t, lambda e: a["L0_ffn_w1"][e], None, lambda e: a["L0_ffn_w2"][e], E0, 0)
        if first_phase < 3 <= last_phase:
            phase(competitive_attention)
        if first_phase < 4 <= last_phase:
            phase(dense_feed_forward)
        if first_phase < 5 <= last_phase:
            phase(head_attention, 2, (m.wq2, m.wk2, m.wv2, m.wo2))
        if first_phase < 6 <= last_phase:
            phase(controller_feed_forward)
        if first_phase < 7 <= last_phase:
            phase(latent_attention)
        if first_phase < 8 <= last_phase:
            phase(experts, 3, m.wg3, lambda e: a["L3_ffn_Ws1"] if isinstance(e, int) and e == 0 else a["L3_ffn_We1"][e - 1],
                  lambda e: a["L3_ffn_Ws3"] if isinstance(e, int) and e == 0 else a["L3_ffn_We3"][e - 1],
                  lambda e: a["L3_ffn_Ws2"] if isinstance(e, int) and e == 0 else a["L3_ffn_We2"][e - 1], E3 + 1, 1)
        store(nc, m, a, lambda n: ctx.enter_context(nc.semaphore(n)))


_OUTS = [((B, S, D), "float32")]


def kernel(**inputs):
    import numpy as _np
    import concourse.bacc as _bacc
    from concourse import mybir as _mybir
    from concourse.bass_utils import run_bass_kernel_spmd as _run

    nc = _bacc.Bacc("TRN2", target_bir_lowering=False, num_devices=1)
    arrays, args = {}, {}
    for name in inputs:
        v = _np.ascontiguousarray(inputs[name])
        arrays[f"in_{name}_dram"] = v
        args[name] = nc.dram_tensor(f"in_{name}_dram", v.shape, _mybir.dt.from_np(v.dtype), kind="ExternalInput").ap()
    for i, (shape, dtype) in enumerate(_OUTS):
        args["out"] = nc.dram_tensor(f"out_{i}_dram", shape, _mybir.dt.from_np(_np.dtype(dtype)), kind="ExternalOutput").ap()
    program(nc, args)
    r = _run(nc, [arrays], core_ids=[0])
    return r.results[0]["out_0_dram"]
```

```python
from contextlib import ExitStack

import concourse.bass as bass
from concourse import mybir

ALU = mybir.AluOpType
ACT = mybir.ActivationFunctionType
AX = mybir.AxisListType
F32 = mybir.dt.float32
BF16 = mybir.dt.bfloat16
F32R = mybir.dt.float32r

B = 32
S = 128
D = 128
KC = 77
HEADS = 16
DK = D // HEADS
HG = 4
NG = HEADS // HG
GB = 4
NGB = B // GB
GT = GB * S
E0, F0 = 8, 512
MX, MY, ML = 8, 64, 64
E3, F3 = 8, 256
H3 = 8
KV = KC + S
EPS = 1e-5
VPAD = D // HG + DK


def wait(eng, sem, value):
    if isinstance(value, int) and value <= 0:
        return
    eng.wait_ge(sem, value)


def pipeline(eng, step, n=B):
    step(-1, 1, True, False, False)
    step(0, 0, True, True, False)
    step(1, 1, True, True, True)
    with eng.Fori(0, (n - 4) // 2) as i:
        step(i * 2 + 2, 0, True, True, True)
        step(i * 2 + 3, 1, True, True, True)
    step(n - 2, 0, True, True, True)
    step(n - 1, 1, False, True, True)
    step(n, 0, False, False, True)


def pipeline4(eng, step, n=B):
    for i in range(-1, 4):
        step(i, i % 2, True, i >= 0, i >= 1, i >= 2)
    with eng.Fori(0, (n - 6) // 2) as i:
        step(i * 2 + 4, 0, True, True, True, True)
        step(i * 2 + 5, 1, True, True, True, True)
    for i in range(n - 2, n + 2):
        step(i, i % 2, i < n - 1, i < n, i <= n, True)


class Memory:
    pass


def row_of(ap):
    return ap.partition_broadcast(128)


def column_of(ap):
    return ap.rearrange("(p a) -> p a", a=1)


def allocate(nc, ctx):
    def sb(name, shape, dtype=F32):
        return ctx.enter_context(nc.sbuf_tensor(name, shape, dtype))

    m = Memory()
    m.x = sb("x_residual", [S, B, D])
    m.ctx = sb("context_rows", [KC, B, D])
    m.ctx_t = sb("context_transposed", [D, B * KC])
    m.moments = sb("x_moments", [S, B, 6])
    m.mean2 = sb("x_mean_doubled", [S, B])
    m.halves = sb("x_halves_difference", [S, B])
    m.var = sb("x_variance", [S, B])
    m.sd = sb("x_deviation", [S, B])
    m.rstd = sb("x_rstd", [S, B])
    m.shift = sb("x_shift", [S, B])
    m.eps = sb("layernorm_eps", [128, 1])
    m.unused = sb("unused_outputs", [128, 32])
    m.unused_columns = iter(range(32))
    m.one = sb("one", [128, 1])
    m.ident = sb("identity", [128, 128])
    m.ident_bf = sb("identity_bf16", [128, 128], BF16)
    m.group_mask = sb("head_in_group_mask", [128, HG])
    m.gate = sb("tanh_gates", [128, 8])
    m.down = sb("descending_count", [128, 128])
    m.psum = ctx.enter_context(nc.psum_tensor("psum", [128, 8, 512], F32))
    m.wq0, m.wk0, m.wv0, m.wo0 = (sb(f"L0_w{c}", [D, D]) for c in "qkvo")
    m.wq2, m.wk2, m.wv2, m.wo2 = (sb(f"L2_w{c}_transposed", [D, D]) for c in "qkvo")
    m.w2_raw = sb("L2_weights_raw", [D, 4, D])
    m.bias_columns = sb("L0_bias_columns", [D, 3])
    m.row_bo0 = sb("L0_bo_row", [128, D])
    m.router_raw = sb("L0_router_raw", [E0, D])
    m.router_t = sb("L0_router_transposed", [D, E0])
    m.wg3 = sb("L3_router", [D, E3])
    m.alpha_beta = sb("L1_alpha_beta", [S, 2])
    m.up1, m.down1 = sb("L1_w_up", [D, F0]), sb("L1_w_down", [128, F0 // 128, D])
    m.b1_columns = sb("L1_b1_columns", [128, F0 // 128])
    m.row_b2, m.row_gamma, m.row_beta = (sb(f"L1_{n}_row", [S, D]) for n in ("b2", "gamma", "beta"))
    m.m1, m.m2 = sb("L2_m1", [D, ML]), sb("L2_m2_and_mb", [ML + 1, MX * MY])
    m.w1_2, m.w2_2 = sb("L2_w1", [D, MX * MY]), sb("L2_w2", [128, MX * MY // 128, D])
    m.row_b2_2 = sb("L2_b2_row", [S, D])
    m.wq3, m.wkv3, m.wo3 = sb("L3_wq", [D, H3 * D]), sb("L3_wkv", [D, 2, H3 * D]), sb("L3_wo", [D, H3, D])
    m.b_rows3 = sb("L3_bias_rows", [H3, 2, D])
    m.row_out3 = sb("L3_output_bias_row", [S, D])
    m.rows3 = sb("L3_norm_rows", [S, 4, D])
    m.c_moments = sb("context_moments", [KC, B, 6])
    return m


def later_loads(m, a):
    loads = [(m.alpha_beta[:, 0:1], row_of(a["L1_xattn_sim_alpha"])), (m.alpha_beta[:, 1:2], row_of(a["L1_xattn_sim_beta"])),
             (m.up1[:, :], a["L1_ffn_w1"][0]), (m.down1[:, :, :], a["L1_ffn_w2"][0].rearrange("(c f) d -> f c d", f=128))]
    loads += [(m.b1_columns[:, c:c + 1], column_of(a["L1_ffn_b1"][0, c * 128:(c + 1) * 128])) for c in range(F0 // 128)]
    loads += [(m.row_b2[:, :], row_of(a["L1_ffn_b2"][0])), (m.row_gamma[:, :], row_of(a["L1_ffn_gamma"])),
              (m.row_beta[:, :], row_of(a["L1_ffn_beta"]))]
    loads += [(m.m1[:, :], a["L2_ffn_m1"]), (m.m2[0:ML, :], a["L2_ffn_m2"].rearrange("l x y -> l (x y)")),
              (m.m2[ML:ML + 1, :], a["L2_ffn_mb"].rearrange("(o x) y -> o (x y)", o=1)),
              (m.w1_2[:, :], a["L2_ffn_w1"].rearrange("d x y -> d (x y)")), (m.row_b2_2[:, :], row_of(a["L2_ffn_b2"]))]
    w2_blocks = a["L2_ffn_w2"].rearrange("y (c i) d -> i y c d", i=2)
    loads += [(m.w2_2[i * MY:(i + 1) * MY, :, :], w2_blocks[i]) for i in range(2)]
    loads += [(m.wq3[:, :], a["L3_xattn_Wq"]), (m.wkv3[:, :, :], a["L3_xattn_Wkv"].rearrange("d (t n) -> d t n", t=2)),
              (m.wo3[:, :, :], a["L3_xattn_Wo"].rearrange("(h c) d -> c h d", c=D)),
              (m.b_rows3[:, 0, :], a["L3_xattn_bq"].rearrange("(h c) -> h c", c=D)),
              (m.b_rows3[:, 1, :], a["L3_xattn_bkv"][H3 * D:2 * H3 * D].rearrange("(h c) -> h c", c=D)),
              (m.row_out3[:, :], row_of(a["L3_xattn_bo"]))]
    loads += [(m.rows3[:, i, :], row_of(a[f"L3_xattn_{n}"])) for i, n in enumerate(("gamma_media", "beta_media", "gamma_lat", "beta_lat"))]
    return loads


def prepare(nc, ctx, m, a):
    def sem(name):
        return ctx.enter_context(nc.semaphore(name))

    ctx_loaded, small_loaded, w_loaded = (sem(n) for n in ("ctx_loaded", "small_loaded", "w_loaded"))
    blank, ident_ready, mask_ready, down_ready = (sem(n) for n in ("blank", "ident_ready", "mask_ready", "down_ready"))
    identb_ready, tanh_done = sem("identb_ready"), sem("tanh_done")
    tr_done, tr_read = sem("tr_done"), sem("tr_read")
    gated = sem("gated")
    m.later_loaded = sem("later_loaded")
    m.later_count = 16 * len(later_loads(m, a))
    NT = B // GB
    LOADS_X = 4
    x_loaded = [sem(f"x_loaded_{q}") for q in range(LOADS_X)]
    with nc.Block() as block:
        @block.sync
        def _(sync):
            for q in range(LOADS_X):
                rows = slice(q * B // LOADS_X, (q + 1) * B // LOADS_X)
                sync.dma_start(m.x[:, rows, :], a["x"][rows].rearrange("b s d -> s b d")).then_inc(x_loaded[q], 16)
            sync.dma_start(m.w2_raw[:, 0, :], a["L2_xattn_Wq"]).then_inc(w_loaded, 16)
            sync.dma_start(m.w2_raw[:, 1, :], a["L2_xattn_Wk"]).then_inc(w_loaded, 16)
            sync.dma_start(m.w2_raw[:, 2, :], a["L2_xattn_Wv"]).then_inc(w_loaded, 16)
            sync.dma_start(m.w2_raw[:, 3, :], a["L2_xattn_Wo"]).then_inc(w_loaded, 16)
            sync.dma_start(m.router_raw[:, :], a["L0_ffn_router_w"]).then_inc(w_loaded, 16)
            for to, of in later_loads(m, a):
                sync.dma_start(to, of).then_inc(m.later_loaded, 16)
            sync.wait_ge(small_loaded, 16 * 11)
            sync.wait_ge(ctx_loaded, 16)

        @block.scalar
        def _(act):
            act.dma_start(m.ctx[:, :, :], a["ctx_1024"].rearrange("b k d -> k b d")).then_inc(ctx_loaded, 16)
            act.dma_start(m.gate[:, 0:4], row_of(a["g_xattn"])).then_inc(small_loaded, 16)
            act.dma_start(m.gate[:, 4:8], row_of(a["g_ffn"])).then_inc(small_loaded, 16)
            act.dma_start(m.wq0[:, :], a["L0_xattn_Wq"]).then_inc(small_loaded, 16)
            act.dma_start(m.wk0[:, :], a["L0_xattn_Wk"]).then_inc(small_loaded, 16)
            act.dma_start(m.wv0[:, :], a["L0_xattn_Wv"]).then_inc(small_loaded, 16)
            act.dma_start(m.wo0[:, :], a["L0_xattn_Wo"]).then_inc(small_loaded, 16)
            act.dma_start(m.wg3[:, :], a["L3_ffn_Wg"]).then_inc(small_loaded, 16)
            act.dma_start(m.bias_columns[:, 0:1], column_of(a["L0_xattn_bq"])).then_inc(small_loaded, 16)
            act.dma_start(m.bias_columns[:, 1:2], column_of(a["L0_xattn_bk"])).then_inc(small_loaded, 16)
            act.dma_start(m.bias_columns[:, 2:3], column_of(a["L0_xattn_bv"])).then_inc(small_loaded, 16)
            act.dma_start(m.row_bo0[:, :], row_of(a["L0_xattn_bo"])).then_inc(small_loaded, 16)
            act.wait_ge(small_loaded, 16 * 11)
            nc.scalar.activation(m.gate[:, :], m.gate[:, :], ACT.Tanh).then_inc(tanh_done, 1)
            for t in range(1, NT, 2):
                act.wait_ge(tr_done, t + 1)
                nc.scalar.copy(m.ctx_t[:, t * GB * KC:(t + 1) * GB * KC],
                               m.psum[:, t % 8, 0:GB * KC]).then_inc(tr_read, 1)
            act.wait_ge(tr_done, NT + 2)
            for u, w in enumerate((m.wq2, m.wk2, m.wv2, m.wo2)):
                nc.scalar.copy(w[:, :], m.psum[:, 0, u * D:(u + 1) * D]).then_inc(tr_read, 1)
            nc.scalar.copy(m.router_t[:, :], m.psum[:, 1, 0:E0]).then_inc(tr_read, 1)
            preload(nc, m, ACT.Sqrt)

        @block.gpsimd
        def _(pool):
            nc.gpsimd.memset(m.ident[:, :], 0.0).then_inc(blank, 1)
            nc.gpsimd.memset(m.eps[:, :], EPS).then_inc(blank, 1)
            nc.gpsimd.memset(m.one[:, :], 1.0).then_inc(blank, 1)
            nc.gpsimd.iota(m.down[:, :], [[-1, 128]], base=128, channel_multiplier=0,
                           allow_small_or_imprecise_dtypes=True).then_inc(down_ready, 1)
            pool.wait_ge(blank, 3)
            nc.gpsimd.affine_select(out=m.ident[:, :], in_=m.ident[:, :], compare_op=ALU.not_equal, fill=1.0,
                                    base=0, pattern=[[-1, 128]], channel_multiplier=1).then_inc(ident_ready, 1)

        @block.tensor
        def _(pe):
            pe.wait_ge(ident_ready, 1)
            pe.wait_ge(ctx_loaded, 16)
            for t in range(NT):
                for u in range(GB):
                    last = nc.tensor.transpose(m.psum[:, t % 8, u * KC:(u + 1) * KC], m.ctx[:, t * GB + u, :],
                                               m.ident[0:KC, 0:KC])
                last.then_inc(tr_done, 1)
            pe.wait_ge(w_loaded, 16 * 5)
            pe.wait_ge(tr_read, NT)
            for u in range(4):
                last = nc.tensor.transpose(m.psum[:, 0, u * D:(u + 1) * D], m.w2_raw[:, u, :], m.ident[:, :])
            last.then_inc(tr_done, 1)
            nc.tensor.transpose(m.psum[:, 1, 0:E0], m.router_raw[:, :], m.ident[0:E0, 0:E0]).then_inc(tr_done, 1)

        @block.vector
        def _(dve):
            dve.wait_ge(ident_ready, 1)
            nc.vector.tensor_copy(m.ident_bf[:, :], m.ident[:, :]).then_inc(identb_ready, 1)
            nc.vector.tensor_reduce(m.group_mask[:, :], m.ident[:, :].rearrange("p (j h d) -> p h j d", h=HG, d=DK),
                                    AX.XY, ALU.add).then_inc(mask_ready, 1)
            for t in range(0, NT, 2):
                dve.wait_ge(tr_done, t + 1)
                nc.vector.tensor_copy(m.ctx_t[:, t * GB * KC:(t + 1) * GB * KC],
                                      m.psum[:, t % 8, 0:GB * KC]).then_inc(tr_read, 1)
            for b in range(B):
                dve.wait_ge(x_loaded[b * LOADS_X // B], 16)
                nc.vector.bn_stats(m.moments[:, b, :], m.x[:, b, :])
            dve.wait_ge(tanh_done, 1)
            nc.vector.tensor_scalar(m.row_bo0[:, :], m.row_bo0[:, :], m.gate[:, 0:1], None, ALU.mult).then_inc(gated, 1)


def preload(nc, m, func):
    column = next(m.unused_columns)
    nc.scalar.activation(m.unused[:, column:column + 1], m.one[:, 0:1], func)


def variance_of_x(nc, m, dve, parts_ready, var_ready):
    even_mean, even_m2, odd_mean, odd_m2 = (m.moments[:, :, c] for c in (1, 2, 4, 5))
    nc.vector.tensor_tensor(m.mean2[:, :], even_mean, odd_mean, ALU.add).then_inc(parts_ready, 1)
    nc.vector.tensor_tensor(m.halves[:, :], even_mean, odd_mean, ALU.subtract).then_inc(parts_ready, 1)
    nc.vector.tensor_tensor(m.var[:, :], even_m2, odd_m2, ALU.add).then_inc(parts_ready, 1)
    dve.wait_ge(parts_ready, 3)
    nc.vector.scalar_tensor_tensor(m.halves[:, :], m.halves[:, :], 0.25, m.halves[:, :], ALU.mult, ALU.mult).then_inc(parts_ready, 1)
    dve.wait_ge(parts_ready, 4)
    nc.vector.scalar_tensor_tensor(m.var[:, :], m.var[:, :], 1.0 / D, m.halves[:, :], ALU.mult, ALU.add).then_inc(var_ready, 1)


def rstd_of_x(nc, m, dve, sd_ready, rstd_ready, shift_ready):
    dve.wait_ge(sd_ready, 1)
    nc.vector.reciprocal(m.rstd[:, :], m.sd[:, :]).then_inc(rstd_ready, 1)
    dve.wait_ge(rstd_ready, 1)
    nc.vector.scalar_tensor_tensor(m.shift[:, :], m.mean2[:, :], -0.5, m.rstd[:, :], ALU.mult, ALU.mult).then_inc(shift_ready, 1)
    dve.wait_ge(shift_ready, 1)


def head_attention(nc, m, sem, layer, w, clear):
    over_heads = layer == 2
    wq, wk, wv, wo = w
    n_rec = KC if over_heads else HEADS
    names = ("sd_ready rstd_ready shift_ready xn_ready xt_in_psum xt_ready proj_in_psum q_ready k_ready "
             "parts_ready var_ready scores_done negmax_ready shifted exp_ready sum_ready recip_ready probs_ready pt_in_psum "
             "ct_ready v_in_psum ot_in_psum ot_ready v_ready y_done x_done bias_added zeroed "
             "pt_read_0 pt_read_1 pt_read_2 pt_read_3")
    s = {n: sem(f"{n}_{layer}") for n in names.split()}
    pt_read = [s[f"pt_read_{g}"] for g in range(NG)]
    gate = m.gate[:, layer:layer + 1]
    with ExitStack() as ctx:
        def sb(name, shape, dtype=F32):
            return ctx.enter_context(nc.sbuf_tensor(f"{name}_{layer}", shape, dtype))

        xn = sb("xn", [S, 2, D])
        xt = sb("xt", [D, 2, S])
        qt = sb("qt", [D, 2, S])
        ktm = sb("kt_masked", [D, 2, HG, KC])
        vpad = sb("v_padded", [KC, 2, HEADS, VPAD])
        e = sb("exp_scores", [S, 2, HEADS, KC])
        negmax = sb("negated_max", [S, 2, n_rec], BF16)
        total = sb("softmax_sum", [S, 2, n_rec])
        recip = sb("softmax_recip", [S, 2, n_rec])
        pt = sb("probs_transposed", [KC, HEADS, S])
        ot = sb("heads_out", [D, S])
        cts = sb("context_slot", [D, 2, KC])

        def scores_view():
            t = m.psum[:, 0:NG, 0:HG * KC]
            return t.rearrange("p j (h k) -> p k j h", k=KC) if over_heads else t.rearrange("p j (h k) -> p j h k", k=KC)

        def per_row(t, par):
            return t[:, par, :] if over_heads else t[:, par, :].rearrange("p (j h) -> p j h", h=HG)

        with nc.Block() as block:
            @block.gpsimd
            def _(pool):
                clear(pool)
                nc.gpsimd.memset(vpad[:, :, :, :], 0.0).then_inc(s["zeroed"], 1)

                def step(b, par, front, middle, back, tail):
                    if front:
                        wait(pool, s["v_in_psum"], b)
                        nc.gpsimd.tensor_copy(cts[:, 1 - par, :], m.ctx_t[:, bass.ds((b + 1) * KC, KC)]).then_inc(s["ct_ready"], 1)
                    if front and layer == 0:
                        wait(pool, s["xn_ready"], b + 2)
                        nc.gpsimd.tensor_tensor(m.x[:, b + 1, :], m.x[:, b + 1, :], m.row_bo0[:, :],
                                                ALU.add).then_inc(s["bias_added"], 1)
                    if middle:
                        wait(pool, s["recip_ready"], b + 1)
                        for g in range(NG):
                            heads = slice(g * HG, (g + 1) * HG)
                            rec = recip[:, par, :].unsqueeze(1) if over_heads else recip[:, par, heads].unsqueeze(2)
                            nc.gpsimd.tensor_tensor(e[:, par, heads, :], e[:, par, heads, :], rec.to_broadcast([S, HG, KC]),
                                                    ALU.mult).then_inc(s["probs_ready"], 1)

                pipeline4(pool, step)

            @block.scalar
            def _(act):
                act.wait_ge(s["var_ready"], 1)
                nc.scalar.activation(m.sd[:, :], m.var[:, :], ACT.Sqrt, bias=m.eps[:, 0:1]).then_inc(s["sd_ready"], 1)
                preload(nc, m, ACT.Exp)

                def copy_group(b, g):
                    wait(act, s["pt_in_psum"], (b - 1) * NG + g + 1)
                    wait(act, s["ot_in_psum"], b - 1)
                    nc.scalar.copy(pt[:, g * HG:(g + 1) * HG, :],
                                   m.psum[0:KC, 4 + g % 2, :].rearrange("p (h s) -> p h s", s=S)).then_inc(pt_read[g], 1)

                def step(b, par, front, middle, back, tail):
                    nxt = 1 - par
                    if tail:
                        wait(act, s["ot_in_psum"], b - 1)
                        wait(act, s["y_done"], b - 2)
                        if layer == 0:
                            nc.scalar.activation(ot[:, :], m.psum[:, 7, 0:S], ACT.Identity,
                                                 bias=m.bias_columns[:, 2:3]).then_inc(s["ot_ready"], 1)
                        else:
                            nc.scalar.copy(ot[:, :], m.psum[:, 7, 0:S]).then_inc(s["ot_ready"], 1)
                    if front:
                        wait(act, s["xt_in_psum"], b + 2)
                        wait(act, s["proj_in_psum"], b)
                        nc.scalar.copy(xt[:, nxt, :], m.psum[:, 6, 0:S]).then_inc(s["xt_ready"], 1)
                    if back:
                        copy_group(b, 0)
                        copy_group(b, 1)
                    if middle:
                        wait(act, s["shifted"], b + 1)
                        wait(act, s["pt_in_psum"], (b - 1) * NG)
                        nc.scalar.activation(e[:, par, :, :].rearrange("p (j h) k -> p j (h k)", h=HG),
                                             m.psum[:, 0:NG, 0:HG * KC], ACT.Exp, scale=DK ** -0.5).then_inc(s["exp_ready"], 1)
                    if front:
                        wait(act, s["proj_in_psum"], b + 2)
                        wait(act, s["scores_done"], b)
                        if layer == 0:
                            nc.scalar.activation(qt[:, nxt, :], m.psum[:, 6, S:2 * S], ACT.Identity,
                                                 bias=m.bias_columns[:, 0:1]).then_inc(s["q_ready"], 1)
                        else:
                            nc.scalar.copy(qt[:, nxt, :], m.psum[:, 6, S:2 * S]).then_inc(s["q_ready"], 1)
                    if middle:
                        if isinstance(b, int) and b == 0:
                            act.wait_ge(s["zeroed"], 1)
                        wait(act, s["v_in_psum"], b + 1)
                        wait(act, s["ot_in_psum"], b - 1)
                        nc.scalar.copy(vpad[:, par, :, 0:DK], m.psum[0:KC, 6, 3 * S:4 * S].rearrange("p (h d) -> p h d", d=DK))\
                            .then_inc(s["v_ready"], 1)
                    if back:
                        copy_group(b, 3)

                pipeline4(act, step)
                preload(nc, m, ACT.Sqrt)

            @block.vector
            def _(dve):
                variance_of_x(nc, m, dve, s["parts_ready"], s["var_ready"])
                rstd_of_x(nc, m, dve, s["sd_ready"], s["rstd_ready"], s["shift_ready"])

                def step(b, par, front, middle, back, tail):
                    nxt = 1 - par
                    if front:
                        wait(dve, s["xt_in_psum"], b)
                        nc.vector.tensor_scalar(xn[:, nxt, :], m.x[:, b + 1, :], m.rstd[:, bass.ds(b + 1, 1)],
                                                m.shift[:, bass.ds(b + 1, 1)], ALU.mult, ALU.add).then_inc(s["xn_ready"], 1)
                    if middle:
                        wait(dve, s["scores_done"], b + 1)
                        wait(dve, s["shifted"], b - 1)
                        nc.vector.tensor_reduce(per_row(negmax, par), scores_view(), AX.XY if over_heads else AX.X,
                                                ALU.max, negate=True).then_inc(s["negmax_ready"], 1)
                    if tail:
                        wait(dve, s["y_done"], b - 1)
                        if layer == 0:
                            wait(dve, s["bias_added"], b - 1)
                        nc.vector.scalar_tensor_tensor(m.x[:, b - 2, :], m.psum[:, 7, S:2 * S], gate, m.x[:, b - 2, :],
                                                       ALU.mult, ALU.add).then_inc(s["x_done"], 1)
                    if back:
                        wait(dve, s["pt_in_psum"], (b - 1) * NG + 3)
                        wait(dve, s["ot_in_psum"], b - 1)
                        nc.vector.tensor_copy(pt[:, 2 * HG:3 * HG, :], m.psum[0:KC, 4, :].rearrange("p (h s) -> p h s", s=S)).then_inc(pt_read[2], 1)
                    if front:
                        wait(dve, s["q_ready"], b + 2)
                        wait(dve, s["v_ready"], b + 1)
                        kin = m.psum[:, 6, 2 * S:2 * S + KC].unsqueeze(1).to_broadcast([D, HG, KC])
                        mask = m.group_mask[:, :].unsqueeze(2).to_broadcast([D, HG, KC])
                        nc.vector.scalar_tensor_tensor(ktm[:, nxt, :, :], kin, m.bias_columns[:, 1:2] if layer == 0 else 0.0,
                                                       mask, ALU.add, ALU.mult).then_inc(s["k_ready"], 1)
                    if middle:
                        wait(dve, s["exp_ready"], b + 1)
                        nc.vector.tensor_reduce(total[:, par, :], e[:, par, :, :].rearrange("p h k -> p k h") if over_heads else e[:, par, :, :],
                                                AX.X, ALU.add).then_inc(s["sum_ready"], 1)
                        wait(dve, s["sum_ready"], b + 1)
                        wait(dve, s["probs_ready"], (b - 1) * NG)
                        nc.vector.reciprocal(recip[:, par, :], total[:, par, :]).then_inc(s["recip_ready"], 1)
                    if tail:
                        wait(dve, s["x_done"], b - 1)
                        nc.vector.bn_stats(m.moments[:, b - 2, :], m.x[:, b - 2, :])

                pipeline4(dve, step)

            @block.tensor
            def _(pe):
                def transposes(b, nxt, g):
                    if g >= 2:
                        wait(pe, pt_read[g - 2], b)
                    else:
                        wait(pe, pt_read[g + 2], b - 1)
                    wait(pe, s["probs_ready"], (b - 1) * NG + g + 1)
                    for h in range(HG):
                        last = nc.tensor.transpose(m.psum[0:KC, 4 + g % 2, h * S:(h + 1) * S], e[:, nxt, g * HG + h, :], m.ident[:, :])
                    last.then_inc(s["pt_in_psum"], 1)

                def step(b, par, front, middle, back, tail):
                    nxt = 1 - par
                    if middle:
                        wait(pe, s["q_ready"], b + 1)
                        wait(pe, s["k_ready"], b + 1)
                        wait(pe, s["exp_ready"], b)
                        for j in range(NG):
                            rows = slice(32 * j, 32 * j + 32)
                            last = nc.tensor.matmul(m.psum[:, j, 0:HG * KC], qt[rows, par, :],
                                                    ktm[rows, par, :, :].rearrange("p h k -> p (h k)"), start=True, stop=True)
                        last.then_inc(s["scores_done"], 1)
                    if front:
                        wait(pe, s["xn_ready"], b + 2)
                        wait(pe, s["q_ready"], b + 1)
                        wait(pe, s["k_ready"], b + 1)
                        wait(pe, s["v_ready"], b)
                        nc.tensor.transpose(m.psum[:, 6, 0:S], xn[:, nxt, :], m.ident[:, :]).then_inc(s["xt_in_psum"], 1)
                    if tail:
                        wait(pe, s["ot_ready"], b - 1)
                        nc.tensor.matmul(m.psum[:, 7, S:2 * S], ot[:, :], wo[:, :], start=True, stop=True).then_inc(s["y_done"], 1)
                    if back:
                        transposes(b, nxt, 0)
                        transposes(b, nxt, 1)
                    if middle:
                        wait(pe, s["negmax_ready"], b + 1)
                        for j in range(NG):
                            nm = negmax[:, par, :]
                            nm = nm.unsqueeze(1) if over_heads else nm[:, j * HG:(j + 1) * HG].unsqueeze(2)
                            last = nc.tensor.matmul(m.psum[:, j, 0:HG * KC].rearrange("p (h k) -> p h k", k=KC), m.ident_bf[:, :],
                                                    nm.to_broadcast([S, HG, KC]), start=False, stop=True, skip_group_check=True)
                        last.then_inc(s["shifted"], 1)
                    if front:
                        wait(pe, s["xt_ready"], b + 2)
                    if middle:
                        wait(pe, s["ct_ready"], b + 1)
                        if not front:
                            wait(pe, s["k_ready"], b + 1)
                            wait(pe, s["v_ready"], b)
                        nc.tensor.matmul(m.psum[0:KC, 6, 3 * S:4 * S], cts[:, par, :], wv[:, :], start=True, stop=True).then_inc(s["v_in_psum"], 1)
                    if front:
                        nc.tensor.matmul(m.psum[:, 6, S:2 * S], wq[:, :], xt[:, nxt, :], start=True, stop=True)
                        wait(pe, s["ct_ready"], b + 2)
                        nc.tensor.matmul(m.psum[:, 6, 2 * S:2 * S + KC], wk[:, :], cts[:, nxt, :], start=True, stop=True)\
                            .then_inc(s["proj_in_psum"], 1)
                    if back:
                        transposes(b, nxt, 2)
                        transposes(b, nxt, 3)
                        wait(pe, s["v_ready"], b)
                        wait(pe, s["x_done"], b - 1)
                        wait(pe, s["ot_ready"], b - 1)
                        for pair in ((0, 1), (2, 3)):
                            for g in pair:
                                wait(pe, pt_read[g], b)
                            for h in range(HG):
                                for g in pair:
                                    at = (g * HG + h) * VPAD - h * DK
                                    lhs = vpad[:, nxt, :, :].rearrange("p h c -> p (h c)")[:, at:at + 32]
                                    last = nc.tensor.matmul(m.psum[32 * g:32 * g + 32, 7, 0:S], lhs, pt[:, g * HG + h, :],
                                                            start=(h == 0), stop=(h == HG - 1), skip_group_check=True)
                        last.then_inc(s["ot_in_psum"], 1)

                pipeline4(pe, step)


def top_two_steps(nc, m, s, p, work, m1, m2, pick1, pick2):
    wide = [S, GB, E0]
    down = m.down[:, 0:E0].unsqueeze(1).to_broadcast(wide)

    def spread(t):
        return t[:, :].unsqueeze(2).to_broadcast(wide)

    steps = []
    for value, pick in ((m1, pick1), (m2, pick2)):
        steps += [lambda value=value: nc.vector.tensor_reduce(value[:, :], p[:, :, :], AX.X, ALU.max),
                  lambda value=value, pick=pick: nc.vector.tensor_tensor(pick[:, :, :], p[:, :, :], spread(value), ALU.is_ge),
                  lambda pick=pick: nc.vector.tensor_tensor(pick[:, :, :], pick[:, :, :], down, ALU.mult),
                  lambda pick=pick: nc.vector.tensor_reduce(work[:, :], pick[:, :, :], AX.X, ALU.max),
                  lambda pick=pick: nc.vector.tensor_tensor(pick[:, :, :], pick[:, :, :], spread(work), ALU.is_equal)]
        if pick is pick1:
            steps.append(lambda: nc.vector.scalar_tensor_tensor(p[:, :, :], pick1[:, :, :], -4.0, p[:, :, :], ALU.mult, ALU.add))
    return steps


def experts(nc, m, sem, layer, router_t, w_up, w_gate, w_down, n_exp, shared, clear, out=None):
    hidden = F0 if layer == 0 else F3
    chunks = hidden // 128
    names = ("parts_ready var_ready sd_ready rstd_ready shift_ready xn_ready xt_in_psum xts_ready xt_high_ready xt_low_ready "
             "logits_in_psum link exp_wanted exp_ready hidden_in_psum silu_ready hidden_ready y_done y_read up_loaded down_loaded w_split stored")
    s = {n: sem(f"{n}_ffn{layer}") for n in names.split()}
    gate = m.gate[:, 4 + layer:5 + layer]
    sides = 1 if layer == 0 else 2
    TRANSPOSE_AT, LOGITS_AT, ROUTE_AT = 1, 2, 3
    with ExitStack() as ctx:
        def sb(name, shape, dtype=F32):
            return ctx.enter_context(nc.sbuf_tensor(f"{name}_ffn{layer}", shape, dtype))

        xn = sb("xn", [S, GB, D])
        xts = sb("xt", [D, GT])
        xt_high, xt_low = sb("xt_high", [D, 2, GT], F32R), sb("xt_low", [D, 2, GT], F32R)
        logits = sb("logits", [S, GB, E0])
        m1, m2, work, rec = (sb(n, [S, GB]) for n in ("top1", "top2", "pick_code", "weight_recip"))
        pick1, pick2 = sb("pick1", [S, GB, E0]), sb("pick2", [S, GB, E0])
        weight = sb("expert_weight", [S, 2, n_exp, GB])
        raw = sb("w_up_raw", [D, 2, sides, hidden])
        high, low = sb("w_up_high", [D, n_exp, sides, hidden], F32R), sb("w_up_low", [D, n_exp, sides, hidden], F32R)
        down = sb("w_down", [128, n_exp, chunks, D])
        silu = sb("silu", [128, 2, GT]) if layer == 3 else None
        hid = sb("hidden", [128, 2, chunks, GT])

        def units(g, par, front, middle, do, insert):
            def unit(e):
                if e < n_exp:
                    return (par, e, g, g * n_exp + e)
                return (1 - par, 0, g + 1, (g + 1) * n_exp)

            if not middle:
                if front:
                    for e in (TRANSPOSE_AT, LOGITS_AT, ROUTE_AT, ROUTE_AT + 1, ROUTE_AT + 2, ROUTE_AT + 3):
                        insert(e)
                    do(unit(n_exp), None)
                return
            for e in range(n_exp):
                do(unit(e + 1) if e + 1 < n_exp or front else None, unit(e))
                if front:
                    insert(e)

        with nc.Block() as block:
            @block.sync
            def _(sync):
                for e in range(n_exp):
                    if e >= 2:
                        sync.wait_ge(s["w_split"], 2 * (e - 1))
                    for side, w in enumerate((w_up, w_gate)[:sides]):
                        sync.dma_start(raw[:, e % 2, side, :], w(e)).then_inc(s["up_loaded"], 16)
                    sync.dma_start(down[:, e, :, :], w_down(e).rearrange("(c f) d -> f c d", f=128)).then_inc(s["down_loaded"], 16)
                    sync.wait_ge(s["up_loaded"], (e + 1) * 16 * sides)
                    sync.wait_ge(s["down_loaded"], (e + 1) * 16)
                if out is not None:
                    for g in range(NGB):
                        sync.wait_ge(s["y_read"], (g + 1) * n_exp)
                        rows = slice(g * GB, (g + 1) * GB)
                        sync.dma_start(out[rows].rearrange("b s d -> s b d"), m.x[:, rows, :]).then_inc(s["stored"], 16)
                    sync.wait_ge(s["stored"], 16 * NGB)

            @block.gpsimd
            def _(pool):
                clear(pool)

                def split(e):
                    pool.wait_ge(s["up_loaded"], (e + 1) * 16 * sides)
                    nc.gpsimd.tensor_copy(high[:, e, :, :], raw[:, e % 2, :, :]).then_inc(s["w_split"], 1)
                    pool.wait_ge(s["w_split"], 2 * e + 1)
                    nc.gpsimd.tensor_tensor(low[:, e, :, :], raw[:, e % 2, :, :], high[:, e, :, :], ALU.subtract).then_inc(s["w_split"], 1)

                def step(g, par, front, middle, back):
                    nxt = 1 - par
                    if front:
                        wait(pool, s["xt_high_ready"], g + 2)
                        nc.gpsimd.tensor_tensor(xt_low[:, nxt, :], xts[:, :], xt_high[:, nxt, :], ALU.subtract).then_inc(s["xt_low_ready"], 1)
                    if isinstance(g, int) and g == -1:
                        for e in range(1, n_exp):
                            split(e)

                split(0)
                pipeline(pool, step, NGB)

            @block.scalar
            def _(act):
                act.wait_ge(s["var_ready"], 1)
                nc.scalar.activation(m.sd[:, :], m.var[:, :], ACT.Sqrt, bias=m.eps[:, 0:1]).then_inc(s["sd_ready"], 1)
                preload(nc, m, ACT.Exp)

                def step(g, par, front, middle, back):
                    def do(ahead, now):
                        if ahead is None:
                            return
                        p, e, group, n = ahead
                        slot = (p * n_exp + e) % 2
                        for c in range(chunks):
                            wait(act, s["hidden_in_psum"], n * chunks + c + 1)
                            if layer == 0:
                                if c == 0:
                                    wait(act, s["y_done"], n - 1)
                                nc.scalar.activation(hid[:, slot, c, :], m.psum[:, c, :], ACT.Gelu).then_inc(s["hidden_ready"], 1)
                            else:
                                wait(act, s["hidden_ready"], (n - 1) * chunks + c + 1)
                                nc.scalar.activation(silu[:, c, :], m.psum[:, c, :], ACT.Silu).then_inc(s["silu_ready"], 1)

                    def insert(e):
                        if e == TRANSPOSE_AT:
                            wait(act, s["xt_in_psum"], g + 2)
                            wait(act, s["logits_in_psum"], g + 1)
                            wait(act, s["xt_low_ready"], g + 1)
                            nc.scalar.copy(xts[:, :], m.psum[:, 6, :]).then_inc(s["xts_ready"], 1)
                            wait(act, s["hidden_in_psum"], g * n_exp * chunks)
                            nc.scalar.copy(xt_high[:, 1 - par, :], m.psum[:, 6, :]).then_inc(s["xt_high_ready"], 1)
                        if e == ROUTE_AT:
                            wait(act, s["exp_wanted"], g + 2)
                            nc.scalar.activation(logits[:, :, :], logits[:, :, :], ACT.Exp,
                                                 scale=1.0 if layer == 0 else -1.0).then_inc(s["exp_ready"], 1)

                    units(g, par, front, middle, do, insert)

                pipeline(act, step, NGB)
                if out is None:
                    preload(nc, m, ACT.Sqrt)

            @block.vector
            def _(dve):
                variance_of_x(nc, m, dve, s["parts_ready"], s["var_ready"])
                rstd_of_x(nc, m, dve, s["sd_ready"], s["rstd_ready"], s["shift_ready"])
                wide = [S, GB, E0]

                def spread(t):
                    return t[:, :].unsqueeze(2).to_broadcast(wide)

                find = top_two_steps(nc, m, s, logits, work, m1, m2, pick1, pick2)
                before = 4 if layer == 0 else 2
                LINKS = before + len(find) + 7 + 2 * shared

                def route(g, nxt, link, part):
                    if part == 0:
                        wait(dve, s["logits_in_psum"], g + 2)
                        raw_logits = m.psum[:, 7, 0:GB * E0].rearrange("p (t e) -> p t e", e=E0)
                        if layer == 0:
                            link(nc.vector.tensor_reduce(work[:, :], raw_logits, AX.X, ALU.max))
                            nc.vector.tensor_tensor(logits[:, :, :], raw_logits, spread(work), ALU.subtract).then_inc(s["exp_wanted"], 1)
                        else:
                            nc.vector.tensor_copy(logits[:, :, :], raw_logits).then_inc(s["exp_wanted"], 1)
                    if part == 1:
                        wait(dve, s["exp_ready"], g + 2)
                        if layer == 0:
                            link(nc.vector.tensor_reduce(work[:, :], logits[:, :, :], AX.X, ALU.add))
                            link(nc.vector.reciprocal(rec[:, :], work[:, :]))
                            link(nc.vector.tensor_tensor(logits[:, :, :], logits[:, :, :], spread(rec), ALU.mult))
                        else:
                            link(nc.vector.tensor_scalar(logits[:, :, :], logits[:, :, :], 1.0, None, ALU.add))
                            link(nc.vector.reciprocal(logits[:, :, :], logits[:, :, :]))
                        for step in find[:4]:
                            link(step())
                    if part == 2:
                        for step in find[4:]:
                            link(step())
                    if part == 3:
                        wait(dve, s["y_read"], g * n_exp)
                        link(nc.vector.scalar_tensor_tensor(work[:, :], m1[:, :], 1e-9 if layer == 0 else 0.0, m2[:, :], ALU.add, ALU.add))
                        link(nc.vector.reciprocal(rec[:, :], work[:, :]))
                        link(nc.vector.tensor_scalar(rec[:, :], rec[:, :], gate, 1.0 if layer == 0 else 1.0 / 3.0, ALU.mult, ALU.mult))
                        link(nc.vector.tensor_tensor(pick1[:, :, :], pick1[:, :, :], spread(m1), ALU.mult))
                        link(nc.vector.tensor_tensor(pick2[:, :, :], pick2[:, :, :], spread(m2), ALU.mult))
                        link(nc.vector.tensor_tensor(pick1[:, :, :], pick1[:, :, :], pick2[:, :, :], ALU.add))
                        link(nc.vector.tensor_tensor(weight[:, nxt, shared:shared + E0, :].rearrange("p e b -> p b e"), pick1[:, :, :],
                                                     spread(rec), ALU.mult))
                        if shared:
                            link(nc.vector.memset(weight[:, nxt, 0, :], 1.0 / 3.0))
                            link(nc.vector.tensor_scalar(weight[:, nxt, 0, :], weight[:, nxt, 0, :], gate, None, ALU.mult))

                def step(g, par, front, middle, back):
                    link = chain(dve, s["link"], g + 1, LINKS)

                    def do(ahead, now):
                        if ahead is not None and layer == 3:
                            p, e, group, n = ahead
                            slot = (p * n_exp + e) % 2
                            for c in range(chunks):
                                wait(dve, s["silu_ready"], n * chunks + c + 1)
                                if c == 0:
                                    wait(dve, s["y_done"], n - 1)
                                nc.vector.tensor_tensor(hid[:, slot, c, :], silu[:, c, :], m.psum[:, 2 + c, :], ALU.mult)\
                                    .then_inc(s["hidden_ready"], 1)
                        if now is not None:
                            p, e, group, n = now
                            wait(dve, s["y_done"], n + 1)
                            wait(dve, s["y_read"], n)
                            for t in range(GB):
                                ins = nc.vector.scalar_tensor_tensor(m.x[:, group * GB + t, :], m.psum[:, 4 + (p * n_exp + e) % 2, t * D:(t + 1) * D],
                                                                     weight[:, p, e, t:t + 1], m.x[:, group * GB + t, :], ALU.mult, ALU.add)
                            ins.then_inc(s["y_read"], 1)

                    def insert(e):
                        if e == TRANSPOSE_AT - 1 or (not middle and e == TRANSPOSE_AT):
                            wait(dve, s["xt_in_psum"], g + 1)
                            for t in range(GB):
                                at = (g + 1) * GB + t
                                ins = nc.vector.tensor_scalar(xn[:, t, :], m.x[:, at, :], m.rstd[:, bass.ds(at, 1)],
                                                              m.shift[:, bass.ds(at, 1)], ALU.mult, ALU.add)
                            ins.then_inc(s["xn_ready"], 1)
                        if ROUTE_AT <= e < ROUTE_AT + 4:
                            route(g, 1 - par, link, e - ROUTE_AT)

                    units(g, par, front, middle, do, insert)
                    if middle and out is None:
                        wait(dve, s["y_read"], (g + 1) * n_exp)
                        for t in range(GB):
                            nc.vector.bn_stats(m.moments[:, g * GB + t, :], m.x[:, g * GB + t, :])

                pipeline(dve, step, NGB)

            @block.tensor
            def _(pe):
                def up_project(par, e, side, c):
                    cols = slice(c * 128, (c + 1) * 128)
                    terms = ((low, xt_high), (high, xt_low), (high, xt_high))
                    for n, (weights, moving) in enumerate(terms):
                        mm = nc.tensor.matmul(m.psum[:, 2 * side + c, :], weights[:, e, side, cols], moving[:, par, :],
                                              start=(n == 0), stop=(n == len(terms) - 1))
                    return mm

                def step(g, par, front, middle, back):
                    def do(ahead, now):
                        if ahead is not None:
                            p, e, group, n = ahead
                            if isinstance(group, int) and group == 0:
                                pe.wait_ge(s["w_split"], 2 * e + 2)
                            if e == 0:
                                wait(pe, s["xt_high_ready"], group + 1)
                                wait(pe, s["xt_low_ready"], group + 1)
                            for c in range(chunks):
                                wait(pe, s["hidden_ready"], (n - 1) * chunks + c + 1)
                                for side in range(sides):
                                    mm = up_project(p, e, side, c)
                                mm.then_inc(s["hidden_in_psum"], 1)
                        if now is not None:
                            p, e, group, n = now
                            slot = (p * n_exp + e) % 2
                            if isinstance(group, int) and group == 0:
                                pe.wait_ge(s["down_loaded"], 16 * (e + 1))
                            wait(pe, s["hidden_ready"], (n + 1) * chunks)
                            wait(pe, s["y_read"], n - 1)
                            for t in range(GB):
                                for c in range(chunks):
                                    mm = nc.tensor.matmul(m.psum[:, 4 + slot, t * D:(t + 1) * D], hid[:, slot, c, t * S:(t + 1) * S],
                                                          down[:, e, c, :], start=(c == 0), stop=(c == chunks - 1))
                            mm.then_inc(s["y_done"], 1)

                    def insert(e):
                        if e == TRANSPOSE_AT:
                            wait(pe, s["xn_ready"], g + 2)
                            wait(pe, s["xt_high_ready"], g + 1)
                            for t in range(GB):
                                mm = nc.tensor.transpose(m.psum[:, 6, t * S:(t + 1) * S], xn[:, t, :], m.ident[:, :])
                            mm.then_inc(s["xt_in_psum"], 1)
                        if e == LOGITS_AT:
                            wait(pe, s["xts_ready"], g + 2)
                            wait(pe, s["exp_wanted"], g + 1)
                            for t in range(GB):
                                mm = nc.tensor.matmul(m.psum[:, 7, t * E0:(t + 1) * E0], xts[:, t * S:(t + 1) * S], router_t[:, :],
                                                      start=True, stop=True)
                            mm.then_inc(s["logits_in_psum"], 1)

                    units(g, par, front, middle, do, insert)

                pipeline(pe, step, NGB)


def chain(eng, sem, done, length):
    count = [0]

    def link(ins):
        count[0] += 1
        assert count[0] <= length
        ins.then_inc(sem, 1)
        wait(eng, sem, done * length + count[0])

    return link


def competitive_attention(nc, m, sem, clear):
    names = ("parts_ready var_ready sd_ready rstd_ready shift_ready neg_ready ones_ready xn_ready xt_in_psum xt_ready "
             "z_in_psum exp_ready one_added xn_used x_moved best_ready weighted_ready sim_ready pick_ready simt_in_psum simt_ready agg_in_psum y_done x_done mid_link back_link")
    s = {n: sem(f"{n}_1") for n in names.split()}
    gate = m.gate[:, 1:2]
    MID, BACK = 3, 4
    with ExitStack() as ctx:
        def sb(name, shape, dtype=F32):
            return ctx.enter_context(nc.sbuf_tensor(f"{name}_xattn1", shape, dtype))

        xn = sb("xn", [S, 2, GB, D])
        xt = sb("xt", [D, 2, GT])
        minus_alpha_beta = sb("minus_alpha_beta", [S, 2])
        sim = sb("sim", [S, 2, GB, KC])
        pick = sb("pick", [S, 2, GB, KC])
        best = sb("best_sim", [S, 2, GB])
        code = sb("pick_code", [S, GB])
        gated = sb("gated_xn", [S, GB * D])
        weighted = sb("weighted_tokens", [S, 2, GB, D + 1])
        simt = sb("sim_transposed", [KC, GT])
        rows = sb("context_out", [KC, GB, D])
        tally = sb("token_count", [KC, 2, 2])
        with nc.Block() as block:
            @block.gpsimd
            def _(pool):
                clear(pool)
                nc.gpsimd.memset(weighted[:, :, :, :], 1.0).then_inc(s["ones_ready"], 1)
                pool.wait_ge(s["ones_ready"], 1)

                def step(g, par, front, middle, back):
                    if middle:
                        wait(pool, s["best_ready"], g + 1)
                        wait(pool, s["agg_in_psum"], g - 1)
                        nc.gpsimd.tensor_tensor(weighted[:, par, :, 0:D], xn[:, par, :, :], best[:, par, :].unsqueeze(2).to_broadcast([S, GB, D]),
                                                ALU.mult).then_inc(s["weighted_ready"], 1)
                        wait(pool, s["x_moved"], g)
                        nc.gpsimd.tensor_tensor(gated[:, :], xn[:, par, :, :].rearrange("p b d -> p (b d)"), m.gate[:, 1:2].to_broadcast([S, GB * D]),
                                                ALU.mult).then_inc(s["xn_used"], 1)
                        wait(pool, s["xn_used"], g + 1)
                        xg = m.x[:, bass.ds(g * GB, GB), :].rearrange("p b d -> p (b d)")
                        nc.gpsimd.tensor_tensor(xg, xg, gated[:, :], ALU.add).then_inc(s["x_moved"], 1)

                pipeline(pool, step, NGB)

            @block.scalar
            def _(act):
                act.wait_ge(s["var_ready"], 1)
                nc.scalar.activation(m.sd[:, :], m.var[:, :], ACT.Sqrt, bias=m.eps[:, 0:1]).then_inc(s["sd_ready"], 1)
                preload(nc, m, ACT.Exp)
                act.wait_ge(s["neg_ready"], 1)
                act.wait_ge(s["shift_ready"], 1)

                def step(g, par, front, middle, back):
                    nxt = 1 - par
                    if front:
                        wait(act, s["xt_in_psum"], g)
                        wait(act, s["xn_used"], g)
                        for t in range(GB):
                            at = (g + 1) * GB + t
                            ins = nc.scalar.activation(xn[:, nxt, t, :], m.x[:, at, :], ACT.Identity, scale=m.rstd[:, bass.ds(at, 1)],
                                                       bias=m.shift[:, bass.ds(at, 1)])
                        ins.then_inc(s["xn_ready"], 1)
                    if back:
                        wait(act, s["simt_in_psum"], g)
                        wait(act, s["y_done"], g - 1)
                        nc.scalar.copy(simt[:, :], m.psum[0:KC, 2, :]).then_inc(s["simt_ready"], 1)
                    if front:
                        wait(act, s["xt_in_psum"], g + 2)
                        wait(act, s["z_in_psum"], g)
                        nc.scalar.copy(xt[:, nxt, :], m.psum[:, 0, :]).then_inc(s["xt_ready"], 1)
                    if front:
                        wait(act, s["z_in_psum"], g + 2)
                        wait(act, s["simt_in_psum"], g)
                        sv = sim[:, nxt, :, :].rearrange("p b k -> p (b k)")
                        nc.scalar.activation(sv, m.psum[:, 1, 0:GB * KC], ACT.Exp,
                                             scale=minus_alpha_beta[:, 0:1], bias=minus_alpha_beta[:, 1:2]).then_inc(s["exp_ready"], 1)
                        wait(act, s["exp_ready"], g + 2)
                        nc.scalar.activation(sv, sv, ACT.Identity, bias=m.one[:, 0:1]).then_inc(s["one_added"], 1)

                pipeline(act, step, NGB)
                preload(nc, m, ACT.Sqrt)

            @block.vector
            def _(dve):
                dve.wait_ge(m.later_loaded, m.later_count)
                nc.vector.tensor_scalar(minus_alpha_beta[:, :], m.alpha_beta[:, :], -1.0, None, ALU.mult).then_inc(s["neg_ready"], 1)
                variance_of_x(nc, m, dve, s["parts_ready"], s["var_ready"])
                rstd_of_x(nc, m, dve, s["sd_ready"], s["rstd_ready"], s["shift_ready"])
                dve.wait_ge(s["ones_ready"], 1)
                wide = [S, GB, KC]

                def step(g, par, front, middle, back):
                    nxt = 1 - par
                    link_m = chain(dve, s["mid_link"], g, MID)
                    sv, pv = sim[:, par, :, :], pick[:, par, :, :]
                    tl = tally[:, :, :].rearrange("p j u -> p (j u)")
                    if middle:
                        wait(dve, s["one_added"], g + 1)
                        nc.vector.reciprocal(sv, sv).then_inc(s["sim_ready"], 1)
                    if back:
                        wait(dve, s["agg_in_psum"], g)
                        wait(dve, s["y_done"], g - 1)
                        agg = m.psum[0:KC, 3:5, 0:2 * (D + 1)].rearrange("p j (u c) -> p j u c", u=2)
                        nc.vector.tensor_scalar(tally[:, :, :].unsqueeze(3), agg[:, :, :, D:D + 1], 1.0, None, ALU.add).then_inc(s["back_link"], 1)
                        nc.vector.tensor_tensor(rows[:, :, :].rearrange("p (j u) d -> p j u d", u=2), agg[:, :, :, 0:D],
                                                m.ctx[:, bass.ds((g - 1) * GB, GB), :].rearrange("p (j u) d -> p j u d", u=2), ALU.add)\
                            .then_inc(s["back_link"], 1)
                        wait(dve, s["back_link"], (g - 1) * BACK + 2)
                        nc.vector.reciprocal(tl, tl).then_inc(s["back_link"], 1)
                        wait(dve, s["back_link"], (g - 1) * BACK + 3)
                        nc.vector.tensor_tensor(rows[:, :, :], rows[:, :, :], tl.unsqueeze(2).to_broadcast([KC, GB, D]), ALU.mult)\
                            .then_inc(s["back_link"], 1)
                    if middle:
                        wait(dve, s["sim_ready"], g + 1)
                        wait(dve, s["weighted_ready"], g - 1)
                        nc.vector.tensor_reduce(best[:, par, :], sv, AX.X, ALU.max).then_inc(s["best_ready"], 1)
                        wait(dve, s["best_ready"], g + 1)
                        wait(dve, s["agg_in_psum"], g - 1)
                        link_m(nc.vector.tensor_tensor(pv, sv, best[:, par, :].unsqueeze(2).to_broadcast(wide), ALU.is_ge))
                        link_m(nc.vector.tensor_tensor(pv, pv, m.down[:, 0:KC].unsqueeze(1).to_broadcast(wide), ALU.mult))
                        link_m(nc.vector.tensor_reduce(code[:, :], pv, AX.X, ALU.max))
                        nc.vector.tensor_tensor(pv, pv, code[:, :].unsqueeze(2).to_broadcast(wide), ALU.is_equal).then_inc(s["pick_ready"], 1)
                    if back:
                        wait(dve, s["y_done"], g)
                        wait(dve, s["x_moved"], g)
                        xg = m.x[:, bass.ds((g - 1) * GB, GB), :].rearrange("p b d -> p (b d)")
                        nc.vector.scalar_tensor_tensor(xg, m.psum[:, 5, :], gate, xg, ALU.mult, ALU.add).then_inc(s["x_done"], 1)
                        wait(dve, s["x_done"], g)
                        for t in range(GB):
                            nc.vector.bn_stats(m.moments[:, (g - 1) * GB + t, :], m.x[:, (g - 1) * GB + t, :])

                pipeline(dve, step, NGB)

            @block.tensor
            def _(pe):
                def step(g, par, front, middle, back):
                    nxt = 1 - par
                    if back:
                        wait(pe, s["pick_ready"], g)
                        wait(pe, s["weighted_ready"], g)
                        wait(pe, s["back_link"], (g - 1) * BACK)
                        for t in range(GB):
                            mm = nc.tensor.matmul(m.psum[0:KC, 3 + t // 2, (t % 2) * (D + 1):(t % 2 + 1) * (D + 1)], pick[:, nxt, t, :],
                                                  weighted[:, nxt, t, :], start=True, stop=True)
                        mm.then_inc(s["agg_in_psum"], 1)
                        wait(pe, s["simt_ready"], g - 1)
                        for t in range(GB):
                            mm = nc.tensor.transpose(m.psum[0:KC, 2, t * S:(t + 1) * S], sim[:, nxt, t, :], m.ident[:, :])
                        mm.then_inc(s["simt_in_psum"], 1)
                    if front:
                        wait(pe, s["xn_ready"], g + 2)
                        wait(pe, s["xt_ready"], g + 1)
                        for t in range(GB):
                            mm = nc.tensor.transpose(m.psum[:, 0, t * S:(t + 1) * S], xn[:, nxt, t, :], m.ident[:, :])
                        mm.then_inc(s["xt_in_psum"], 1)
                    if front:
                        wait(pe, s["xt_ready"], g + 2)
                        wait(pe, s["exp_ready"], g + 1)
                        for t in range(GB):
                            mm = nc.tensor.matmul(m.psum[:, 1, t * KC:(t + 1) * KC], xt[:, nxt, t * S:(t + 1) * S],
                                                  m.ctx_t[:, bass.ds(((g + 1) * GB + t) * KC, KC)], start=True, stop=True)
                        mm.then_inc(s["z_in_psum"], 1)
                    if back:
                        wait(pe, s["back_link"], g * BACK)
                        wait(pe, s["simt_ready"], g)
                        wait(pe, s["x_done"], g - 1)
                        for t in range(GB):
                            mm = nc.tensor.matmul(m.psum[:, 5, t * D:(t + 1) * D], simt[:, t * S:(t + 1) * S], rows[:, t, :],
                                                  start=True, stop=True)
                        mm.then_inc(s["y_done"], 1)

                pipeline(pe, step, NGB)


def dense_feed_forward(nc, m, sem, clear):
    names = ("parts_ready var_ready sd_ready rstd_ready shift_ready rows_ready xn_ready xt_in_psum xt_ready base_ready "
             "hidden_in_psum hidden_ready y_done z_ready z_var_ready z_sd_ready zn_ready scaled moved x_done link")
    s = {n: sem(f"{n}_ffn1") for n in names.split()}
    chunks = F0 // 128
    LINKS = 6
    with ExitStack() as ctx:
        def sb(name, shape, dtype=F32):
            return ctx.enter_context(nc.sbuf_tensor(f"{name}_ffn1", shape, dtype))

        xn = sb("xn", [S, 2, GB, D])
        xt = sb("xt", [D, 2, GT])
        base = sb("xn_and_bias", [S, 2, GB, D])
        up, down, b1, row_b2, row_gamma, row_beta = m.up1, m.down1, m.b1_columns, m.row_b2, m.row_gamma, m.row_beta
        hid = sb("hidden", [128, 2, chunks, GT])
        z = sb("z", [S, 2, GB, D])
        zst = sb("z_stats", [S, GB, 6])
        mean2, halves, var, sd, rstd, shift = (sb(n, [S, GB]) for n in ("z_mean2", "z_halves", "z_var", "z_sd", "z_rstd", "z_shift"))
        with nc.Block() as block:
            @block.gpsimd
            def _(pool):
                clear(pool)
                pool.wait_ge(s["rows_ready"], 2)

                def step(g, par, front, middle, back, tail):
                    nxt = 1 - par
                    wide = [S, GB, D]
                    if front:
                        wait(pool, s["xn_ready"], g + 2)
                        wait(pool, s["z_ready"], g)
                        nc.gpsimd.tensor_tensor(base[:, nxt, :, :], xn[:, nxt, :, :], row_b2[:, :].unsqueeze(1).to_broadcast(wide),
                                                ALU.add).then_inc(s["base_ready"], 1)
                        xv = m.x[:, bass.ds((g + 1) * GB, GB), :]
                        nc.gpsimd.tensor_tensor(xv, xv, row_beta[:, :].unsqueeze(1).to_broadcast(wide), ALU.add).then_inc(s["moved"], 1)
                    if back:
                        zv, xv = z[:, nxt, :, :], m.x[:, bass.ds((g - 1) * GB, GB), :]
                        wait(pool, s["zn_ready"], g)
                        nc.gpsimd.tensor_tensor(zv, zv, row_gamma[:, :].unsqueeze(1).to_broadcast(wide), ALU.mult).then_inc(s["scaled"], 1)
                        wait(pool, s["scaled"], g)
                        wait(pool, s["moved"], g)
                        nc.gpsimd.tensor_tensor(xv, xv, zv, ALU.add).then_inc(s["x_done"], 1)

                pipeline4(pool, step, NGB)

            @block.scalar
            def _(act):
                act.wait_ge(s["var_ready"], 1)
                nc.scalar.activation(m.sd[:, :], m.var[:, :], ACT.Sqrt, bias=m.eps[:, 0:1]).then_inc(s["sd_ready"], 1)
                act.wait_ge(m.later_loaded, m.later_count)

                def step(g, par, front, middle, back, tail):
                    nxt = 1 - par
                    if middle:
                        wait(act, s["y_done"], g - 1)
                        for c in range(chunks):
                            wait(act, s["hidden_in_psum"], g * chunks + c + 1)
                            nc.scalar.activation(hid[:, par, c, :], m.psum[:, c, :], ACT.Relu, bias=b1[:, c:c + 1]).then_inc(s["hidden_ready"], 1)
                    if front:
                        wait(act, s["xt_in_psum"], g + 2)
                        nc.scalar.copy(xt[:, nxt, :], m.psum[:, 5, :]).then_inc(s["xt_ready"], 1)
                    if back:
                        wait(act, s["z_var_ready"], g)
                        nc.scalar.activation(sd[:, :], var[:, :], ACT.Sqrt, bias=m.eps[:, 0:1]).then_inc(s["z_sd_ready"], 1)

                pipeline4(act, step, NGB)
                preload(nc, m, ACT.Sqrt)

            @block.vector
            def _(dve):
                variance_of_x(nc, m, dve, s["parts_ready"], s["var_ready"])
                dve.wait_ge(m.later_loaded, m.later_count)
                gate = m.gate[:, 5:6]
                nc.vector.tensor_scalar(row_gamma[:, :], row_gamma[:, :], gate, None, ALU.mult).then_inc(s["rows_ready"], 1)
                nc.vector.tensor_scalar(row_beta[:, :], row_beta[:, :], gate, None, ALU.mult).then_inc(s["rows_ready"], 1)
                rstd_of_x(nc, m, dve, s["sd_ready"], s["rstd_ready"], s["shift_ready"])

                def step(g, par, front, middle, back, tail):
                    nxt = 1 - par
                    if front:
                        wait(dve, s["xt_in_psum"], g)
                        wait(dve, s["base_ready"], g)
                        for t in range(GB):
                            at = (g + 1) * GB + t
                            ins = nc.vector.tensor_scalar(xn[:, nxt, t, :], m.x[:, at, :], m.rstd[:, bass.ds(at, 1)],
                                                          m.shift[:, bass.ds(at, 1)], ALU.mult, ALU.add)
                        ins.then_inc(s["xn_ready"], 1)
                    if back:
                        link = chain(dve, s["link"], g - 1, LINKS)
                        wait(dve, s["y_done"], g)
                        wait(dve, s["base_ready"], g)
                        wait(dve, s["x_done"], g - 2)
                        zv = z[:, nxt, :, :]
                        nc.vector.tensor_tensor(zv, m.psum[:, 4, :].rearrange("p (t d) -> p t d", d=D), base[:, nxt, :, :],
                                                ALU.add).then_inc(s["z_ready"], 1)
                        wait(dve, s["z_ready"], g)
                        for t in range(GB):
                            ins = nc.vector.bn_stats(zst[:, t, :], zv[:, t, :])
                        link(ins)
                        me, qe, mo, qo = (zst[:, :, c] for c in (1, 2, 4, 5))
                        nc.vector.tensor_tensor(mean2[:, :], me, mo, ALU.add)
                        link(nc.vector.tensor_tensor(halves[:, :], me, mo, ALU.subtract))
                        link(nc.vector.tensor_tensor(var[:, :], qe, qo, ALU.add))
                        link(nc.vector.scalar_tensor_tensor(halves[:, :], halves[:, :], 0.25, halves[:, :], ALU.mult, ALU.mult))
                        nc.vector.scalar_tensor_tensor(var[:, :], var[:, :], 1.0 / D, halves[:, :], ALU.mult, ALU.add)\
                            .then_inc(s["z_var_ready"], 1)
                        wait(dve, s["z_sd_ready"], g)
                        link(nc.vector.reciprocal(rstd[:, :], sd[:, :]))
                        link(nc.vector.scalar_tensor_tensor(shift[:, :], mean2[:, :], -0.5, rstd[:, :], ALU.mult, ALU.mult))
                        for t in range(GB):
                            ins = nc.vector.tensor_scalar(zv[:, t, :], zv[:, t, :], rstd[:, t:t + 1], shift[:, t:t + 1], ALU.mult, ALU.add)
                        ins.then_inc(s["zn_ready"], 1)
                    if middle:
                        for t in range(GB):
                            nc.vector.bn_stats(m.c_moments[:, g * GB + t, :], m.ctx[:, g * GB + t, :])
                    if tail:
                        wait(dve, s["x_done"], g - 1)
                        for t in range(GB):
                            nc.vector.bn_stats(m.moments[:, (g - 2) * GB + t, :], m.x[:, (g - 2) * GB + t, :])

                pipeline4(dve, step, NGB)

            @block.tensor
            def _(pe):
                pe.wait_ge(m.later_loaded, m.later_count)

                def step(g, par, front, middle, back, tail):
                    nxt = 1 - par
                    if middle:
                        wait(pe, s["xt_ready"], g + 1)
                        wait(pe, s["hidden_ready"], g * chunks)
                        for c in range(chunks):
                            nc.tensor.matmul(m.psum[:, c, :], up[:, c * 128:(c + 1) * 128], xt[:, par, :], start=True, stop=True)\
                                .then_inc(s["hidden_in_psum"], 1)
                    if back:
                        wait(pe, s["hidden_ready"], g * chunks)
                        wait(pe, s["z_ready"], g - 1)
                        for t in range(GB):
                            for c in range(chunks):
                                mm = nc.tensor.matmul(m.psum[:, 4, t * D:(t + 1) * D], hid[:, nxt, c, t * S:(t + 1) * S], down[:, c, :],
                                                      start=(c == 0), stop=(c == chunks - 1))
                        mm.then_inc(s["y_done"], 1)
                    if front:
                        wait(pe, s["xn_ready"], g + 2)
                        wait(pe, s["xt_ready"], g + 1)
                        for t in range(GB):
                            mm = nc.tensor.transpose(m.psum[:, 5, t * S:(t + 1) * S], xn[:, nxt, t, :], m.ident[:, :])
                        mm.then_inc(s["xt_in_psum"], 1)

                pipeline4(pe, step, NGB)


def controller_feed_forward(nc, m, sem, clear):
    names = ("parts_ready var_ready sd_ready rstd_ready shift_ready ones_ready row_ready xn_ready xt_in_psum xt_ready "
             "low_in_psum low_ready logits_in_psum full_in_psum bias_added top_ready ge_ready coded code_ready first_ready full_ready picked_ready "
             "rt_in_psum rt_ready y_done x_done")
    s = {n: sem(f"{n}_ffn2") for n in names.split()}
    gate = m.gate[:, 6:7]
    HID = MX * MY
    CH = HID // 128
    with ExitStack() as ctx:
        def sb(name, shape, dtype=F32):
            return ctx.enter_context(nc.sbuf_tensor(f"{name}_ffn2", shape, dtype))

        xn = sb("xn", [S, 2, D])
        xt = sb("xt", [D, 2, S])
        low = sb("low_rank", [ML + 1, 2, S])
        m1, m2, w1, w2, row_b2 = m.m1, m.m2, m.w1_2, m.w2_2, m.row_b2_2
        full = sb("all_hidden", [S, 2, HID])
        top = sb("top_logit", [S, MX])
        code = sb("pick_code", [S, MX])
        pick = sb("pick", [S, 2, MX, MY])
        rt = sb("picked_transposed", [128, CH * S])
        with nc.Block() as block:
            @block.gpsimd
            def _(pool):
                clear(pool)
                nc.gpsimd.memset(low[ML:ML + 1, :, :], 1.0).then_inc(s["ones_ready"], 1)
                pool.wait_ge(s["ones_ready"], 1)
                pool.wait_ge(s["row_ready"], 1)

                def step(b, par, front, middle, back, tail):
                    if front:
                        wait(pool, s["xn_ready"], b + 2)
                        nc.gpsimd.tensor_tensor(m.x[:, b + 1, :], m.x[:, b + 1, :], row_b2[:, :], ALU.add).then_inc(s["bias_added"], 1)
                    if middle:
                        wait(pool, s["ge_ready"], b + 1)
                        for half in range(2):
                            pv = pick[:, par, half * MX // 2:(half + 1) * MX // 2, :]
                            nc.gpsimd.tensor_tensor(pv, pv, m.down[:, 0:MY].unsqueeze(1).to_broadcast([S, MX // 2, MY]),
                                                    ALU.mult).then_inc(s["coded"], 1)

                pipeline4(pool, step)

            @block.scalar
            def _(act):
                act.wait_ge(s["var_ready"], 1)
                nc.scalar.activation(m.sd[:, :], m.var[:, :], ACT.Sqrt, bias=m.eps[:, 0:1]).then_inc(s["sd_ready"], 1)

                def step(b, par, front, middle, back, tail):
                    nxt = 1 - par
                    if front:
                        wait(act, s["xt_in_psum"], b + 2)
                        wait(act, s["full_in_psum"], b)
                        nc.scalar.copy(xt[:, nxt, :], m.psum[:, 0, 0:S]).then_inc(s["xt_ready"], 1)
                        wait(act, s["low_in_psum"], b + 2)
                        wait(act, s["logits_in_psum"], b)
                        nc.scalar.copy(low[0:ML, nxt, :], m.psum[0:ML, 0, S:2 * S]).then_inc(s["low_ready"], 1)
                    if back:
                        wait(act, s["rt_in_psum"], b)
                        wait(act, s["y_done"], b - 1)
                        nc.scalar.copy(rt[:, :], m.psum[:, 5, :]).then_inc(s["rt_ready"], 1)
                    if middle:
                        wait(act, s["full_in_psum"], b + 1)
                        wait(act, s["picked_ready"], b - 1)
                        nc.scalar.activation(full[:, par, :], m.psum[:, 3 + par, :], ACT.Relu).then_inc(s["full_ready"], 1)

                pipeline4(act, step)
                preload(nc, m, ACT.Sqrt)

            @block.vector
            def _(dve):
                variance_of_x(nc, m, dve, s["parts_ready"], s["var_ready"])
                rstd_of_x(nc, m, dve, s["sd_ready"], s["rstd_ready"], s["shift_ready"])
                dve.wait_ge(m.later_loaded, m.later_count)
                nc.vector.tensor_scalar(row_b2[:, :], row_b2[:, :], gate, None, ALU.mult).then_inc(s["row_ready"], 1)
                wide = [S, MX, MY]

                def step(b, par, front, middle, back, tail):
                    nxt = 1 - par
                    if front:
                        wait(dve, s["xt_in_psum"], b)
                        nc.vector.tensor_scalar(xn[:, nxt, :], m.x[:, b + 1, :], m.rstd[:, bass.ds(b + 1, 1)],
                                                m.shift[:, bass.ds(b + 1, 1)], ALU.mult, ALU.add).then_inc(s["xn_ready"], 1)
                    if back:
                        pv = pick[:, nxt, :, :]
                        for half in range(2):
                            blocks = slice(half * MX // 2, (half + 1) * MX // 2)
                            wait(dve, s["coded"], (b - 1) * 2 + half + 1)
                            ins = nc.vector.tensor_reduce(code[:, blocks], pv[:, blocks, :], AX.X, ALU.max)
                        ins.then_inc(s["code_ready"], 1)
                    if back:
                        wait(dve, s["code_ready"], b)
                        nc.vector.tensor_tensor(pv, pv, code[:, :].unsqueeze(2).to_broadcast(wide), ALU.is_equal).then_inc(s["first_ready"], 1)
                    if tail:
                        wait(dve, s["y_done"], b - 1)
                        wait(dve, s["bias_added"], b - 1)
                        nc.vector.scalar_tensor_tensor(m.x[:, b - 2, :], m.psum[:, 6, 0:D], gate, m.x[:, b - 2, :],
                                                       ALU.mult, ALU.add).then_inc(s["x_done"], 1)
                    if middle:
                        wait(dve, s["logits_in_psum"], b + 1)
                        logits = m.psum[:, 1 + par, :].rearrange("p (x y) -> p x y", y=MY)
                        nc.vector.tensor_reduce(top[:, :], logits, AX.X, ALU.max).then_inc(s["top_ready"], 1)
                    if back:
                        wait(dve, s["first_ready"], b)
                        wait(dve, s["full_ready"], b)
                        pf = pv.rearrange("p x y -> p (x y)")
                        nc.vector.tensor_tensor(pf, pf, full[:, nxt, :], ALU.mult).then_inc(s["picked_ready"], 1)
                    if middle:
                        wait(dve, s["top_ready"], b + 1)
                        wait(dve, s["rt_in_psum"], b - 1)
                        nc.vector.tensor_tensor(pick[:, par, :, :], logits, top[:, :].unsqueeze(2).to_broadcast(wide),
                                                ALU.is_ge).then_inc(s["ge_ready"], 1)
                    if tail:
                        wait(dve, s["x_done"], b - 1)
                        nc.vector.bn_stats(m.moments[:, b - 2, :], m.x[:, b - 2, :])

                pipeline4(dve, step)

            @block.tensor
            def _(pe):
                pe.wait_ge(m.later_loaded, m.later_count)
                pe.wait_ge(s["ones_ready"], 1)

                def step(b, par, front, middle, back, tail):
                    nxt = 1 - par
                    if front:
                        wait(pe, s["xn_ready"], b + 2)
                        wait(pe, s["low_ready"], b + 1)
                        nc.tensor.transpose(m.psum[:, 0, 0:S], xn[:, nxt, :], m.ident[:, :]).then_inc(s["xt_in_psum"], 1)
                    if tail:
                        wait(pe, s["rt_ready"], b - 1)
                        wait(pe, s["x_done"], b - 2)
                        for c in range(CH):
                            mm = nc.tensor.matmul(m.psum[:, 6, 0:D], rt[:, c * S:(c + 1) * S], w2[:, c, :], start=(c == 0), stop=(c == CH - 1))
                        mm.then_inc(s["y_done"], 1)
                    if middle:
                        wait(pe, s["low_ready"], b + 1)
                        wait(pe, s["ge_ready"], b - 1)
                        nc.tensor.matmul(m.psum[:, 1 + par, :], low[:, par, :], m2[:, :], start=True, stop=True).then_inc(s["logits_in_psum"], 1)
                    if front:
                        wait(pe, s["xt_ready"], b + 2)
                        nc.tensor.matmul(m.psum[0:ML, 0, S:2 * S], m1[:, :], xt[:, nxt, :], start=True, stop=True).then_inc(s["low_in_psum"], 1)
                    if middle:
                        wait(pe, s["full_ready"], b - 1)
                        nc.tensor.matmul(m.psum[:, 3 + par, :], xt[:, par, :], w1[:, :], start=True, stop=True).then_inc(s["full_in_psum"], 1)
                    if back:
                        wait(pe, s["picked_ready"], b)
                        wait(pe, s["rt_ready"], b - 1)
                        for c in range(CH):
                            mm = nc.tensor.transpose(m.psum[:, 5, c * S:(c + 1) * S],
                                                     pick[:, nxt, :, :].rearrange("p x y -> p (x y)")[:, c * 128:(c + 1) * 128], m.ident[:, :])
                        mm.then_inc(s["rt_in_psum"], 1)

                pipeline4(pe, step)


def latent_attention(nc, m, sem, clear):
    names = ("parts_ready var_ready sd_ready rstd_ready shift_ready ctx_parts ctx_var ctx_sd ctx_rstd ctx_shift "
             "lat_var lat_sd lat_rstd lat_scale lat_shift "
             "prep_psum prep_read rows_ready cn_raw cn_scaled cn_ready ln_raw ln_scaled ln_ready kvt_in_psum kvt_ready "
             "q_in_psum q_ready scores_done negmax_ready shift_bias_ready exp_ready recip_ready probs_ready pt_in_psum "
             "pt_read_act pt_read_dve c_in_psum c_ready y_done x_done bias_added w_ready kept")
    s = {n: sem(f"{n}_3") for n in names.split()}
    gate = m.gate[:, 3:4]
    SCALE = D ** -0.5
    with ExitStack() as ctx:
        def sb(name, shape, dtype=F32):
            return ctx.enter_context(nc.sbuf_tensor(f"{name}_xattn3", shape, dtype))

        wq, wkv, wo, b_rows, row_out, rows, c_moments = m.wq3, m.wkv3, m.wo3, m.b_rows3, m.row_out3, m.rows3, m.c_moments
        b_cols = sb("bias_columns", [D, 2, H3])
        bv_wide = sb("bv_wide", [D, H3, S])
        w_t = sb("weights_transposed", [D, 3, H3, D])
        w_qk, w_vo = sb("w_qk", [D, H3, D]), sb("w_vo", [D, H3, D])
        t0 = sb("key_weights_times_bq", [D, H3])
        c_mean2, c_half, c_var, c_sd, c_rstd, c_shift = (sb(f"context_{n}", [KC, B]) for n in ("mean2", "half", "var", "sd", "rstd", "shift"))
        l_var, l_sd, l_scale, l_shift = (sb(f"latent_{n}", [S, B]) for n in ("var", "sd", "scale", "shift"))
        kn = sb("kv_before_beta", [S, 2, 2, D])
        kv = sb("kv", [S, 2, 2, D])
        kept = sb("kv_kept", [S, 2, 2, D])
        kvt = sb("kv_transposed", [D, 2, KV])
        q = sb("queries", [D, 2, H3, S])
        e = sb("exp_scores", [S, 2, H3, KV])
        negmax = sb("negated_max", [S, 2, H3])
        shift_bias = sb("scaled_negated_max", [S, 2, H3])
        total, recip = sb("softmax_sum", [S, 2, H3]), sb("softmax_recip", [S, 2, H3])
        ptc, ptl = sb("probs_t_context", [KC, H3 * S]), sb("probs_t_latents", [S, H3 * S])
        c = sb("heads_out", [D, H3, S])
        HB = 2
        HH = 4
        Q_BANKS = (6, 4)
        PREP = 3 * H3 // 4 + 1
        with nc.Block() as block:
            @block.gpsimd
            def _(pool):
                clear(pool)
                pool.wait_ge(m.later_loaded, m.later_count)
                pool.wait_ge(s["rows_ready"], 1)

                def step(b, par, front, middle, back):
                    nxt = 1 - par
                    if front:
                        for part, raw, scaled, ready, n in ((0, "cn_raw", "cn_scaled", "cn_ready", KC), (1, "ln_raw", "ln_scaled", "ln_ready", S)):
                            t = kn[0:n, nxt, part, :]
                            wait(pool, s[raw], b + 2)
                            nc.gpsimd.tensor_tensor(t, t, rows[0:n, 2 * part, :], ALU.mult).then_inc(s[scaled], 1)
                            wait(pool, s[scaled], b + 2)
                            nc.gpsimd.tensor_tensor(kv[0:n, nxt, part, :], t, rows[0:n, 2 * part + 1, :], ALU.add).then_inc(s[ready], 1)
                        nc.gpsimd.tensor_tensor(m.x[:, b + 1, :], m.x[:, b + 1, :], row_out[:, :], ALU.add).then_inc(s["bias_added"], 1)
                    if middle:
                        wait(pool, s["c_in_psum"], (b - 1) * 2)
                        nc.gpsimd.tensor_tensor(kept[0:KC, par, 0, :], kn[0:KC, par, 0, :], rows[0:KC, 1, :], ALU.add).then_inc(s["kept"], 1)
                        nc.gpsimd.tensor_tensor(kept[:, par, 1, :], kn[:, par, 1, :], rows[:, 3, :], ALU.add).then_inc(s["kept"], 1)
                        wait(pool, s["recip_ready"], b + 1)
                        ev = e[:, par, :, :]
                        nc.gpsimd.tensor_tensor(ev, ev, recip[:, par, :].unsqueeze(2).to_broadcast([S, H3, KV]), ALU.mult).then_inc(s["probs_ready"], 1)

                pipeline(pool, step)

            @block.scalar
            def _(act):
                act.wait_ge(s["var_ready"], 1)
                nc.scalar.activation(m.sd[:, :], m.var[:, :], ACT.Sqrt, bias=m.eps[:, 0:1]).then_inc(s["sd_ready"], 1)
                act.wait_ge(s["lat_var"], 1)
                nc.scalar.activation(l_sd[:, :], l_var[:, :], ACT.Sqrt, bias=m.eps[:, 0:1]).then_inc(s["lat_sd"], 1)
                act.wait_ge(s["ctx_var"], 1)
                nc.scalar.activation(c_sd[:, :], c_var[:, :], ACT.Sqrt, bias=m.eps[0:KC, 0:1]).then_inc(s["ctx_sd"], 1)
                preload(nc, m, ACT.Exp)
                for n in range(PREP - 1):
                    act.wait_ge(s["prep_psum"], n + 1)
                    nc.scalar.copy(w_t[:, n // 2, HH * (n % 2):HH * (n % 2) + HH, :].rearrange("p h c -> p (h c)"), m.psum[:, n, :]).then_inc(s["prep_read"], 1)
                act.wait_ge(s["prep_psum"], PREP + 1)
                nc.scalar.copy(w_qk[:, :, :].rearrange("p (n h) c -> p n (h c)", n=2), m.psum[:, 0:2, :]).then_inc(s["w_ready"], 1)
                act.wait_ge(s["prep_psum"], PREP + 2)
                nc.scalar.copy(w_vo[:, :, :].rearrange("p (n h) c -> p n (h c)", n=2), m.psum[:, 2:4, :]).then_inc(s["w_ready"], 1)

                def step(b, par, front, middle, back):
                    nxt = 1 - par
                    if front:
                        wait(act, s["kvt_in_psum"], b + 2)
                        wait(act, s["scores_done"], b * 2)
                        nc.scalar.copy(kvt[:, nxt, :], m.psum[:, 7, 0:KV]).then_inc(s["kvt_ready"], 1)
                    if back:
                        wait(act, s["c_in_psum"], (b - 1) * 2)
                        wait(act, s["pt_in_psum"], (b - 1) * 4 + 1)
                        nc.scalar.copy(ptc[:, 0:512], m.psum[0:KC, 6, :]).then_inc(s["pt_read_act"], 1)
                        wait(act, s["pt_in_psum"], (b - 1) * 4 + 3)
                        nc.scalar.copy(ptl[:, 0:512], m.psum[:, 5, :]).then_inc(s["pt_read_act"], 1)
                    if middle:
                        wait(act, s["pt_in_psum"], (b - 1) * 4)
                        wait(act, s["recip_ready"], b - 1)
                        for h in range(H3):
                            if h % HH == 0:
                                wait(act, s["shift_bias_ready"], b * 2 + h // HH + 1)
                            ins = nc.scalar.activation(e[:, par, h, :], m.psum[:, h // HB, (h % HB) * KV:(h % HB + 1) * KV], ACT.Exp,
                                                       scale=SCALE, bias=shift_bias[:, par, h:h + 1], accum_out=total[:, par, h:h + 1])
                        ins.then_inc(s["exp_ready"], 1)
                    if back:
                        for n in range(2):
                            wait(act, s["y_done"], b - 1)
                            wait(act, s["c_in_psum"], (b - 1) * 2 + n + 1)
                            nc.scalar.copy(c[:, n * HH:(n + 1) * HH, :].rearrange("p h t -> p (h t)"), m.psum[:, 4 + n, :]).then_inc(s["c_ready"], 1)

                pipeline(act, step)
                preload(nc, m, ACT.Sqrt)

            @block.vector
            def _(dve):
                variance_of_x(nc, m, dve, s["parts_ready"], s["var_ready"])
                rstd_of_x(nc, m, dve, s["sd_ready"], s["rstd_ready"], s["shift_ready"])
                nc.vector.tensor_tensor(l_var[:, :], m.rstd[:, :], m.rstd[:, :], ALU.mult).then_inc(s["lat_scale"], 1)
                dve.wait_ge(s["lat_scale"], 1)
                nc.vector.tensor_tensor(l_var[:, :], l_var[:, :], m.var[:, :], ALU.mult).then_inc(s["lat_var"], 1)
                me, qe, mo, qo = (c_moments[:, :, k] for k in (1, 2, 4, 5))
                dve.wait_ge(s["lat_var"], 1)
                nc.vector.tensor_tensor(c_mean2[:, :], me, mo, ALU.add).then_inc(s["ctx_parts"], 1)
                nc.vector.tensor_tensor(c_half[:, :], me, mo, ALU.subtract).then_inc(s["ctx_parts"], 1)
                nc.vector.tensor_tensor(c_var[:, :], qe, qo, ALU.add).then_inc(s["ctx_parts"], 1)
                dve.wait_ge(s["ctx_parts"], 3)
                nc.vector.scalar_tensor_tensor(c_half[:, :], c_half[:, :], 0.25, c_half[:, :], ALU.mult, ALU.mult).then_inc(s["ctx_parts"], 1)
                dve.wait_ge(s["ctx_parts"], 4)
                nc.vector.scalar_tensor_tensor(c_var[:, :], c_var[:, :], 1.0 / D, c_half[:, :], ALU.mult, ALU.add).then_inc(s["ctx_var"], 1)
                dve.wait_ge(s["lat_sd"], 1)
                nc.vector.reciprocal(l_scale[:, :], l_sd[:, :]).then_inc(s["lat_rstd"], 1)
                dve.wait_ge(s["lat_rstd"], 1)
                nc.vector.tensor_tensor(l_shift[:, :], l_scale[:, :], m.shift[:, :], ALU.mult).then_inc(s["lat_shift"], 1)
                nc.vector.tensor_tensor(l_scale[:, :], l_scale[:, :], m.rstd[:, :], ALU.mult).then_inc(s["lat_shift"], 1)
                dve.wait_ge(s["ctx_sd"], 1)
                nc.vector.reciprocal(c_rstd[:, :], c_sd[:, :]).then_inc(s["ctx_rstd"], 1)
                dve.wait_ge(s["ctx_rstd"], 1)
                nc.vector.scalar_tensor_tensor(c_shift[:, :], c_mean2[:, :], -0.5, c_rstd[:, :], ALU.mult, ALU.mult).then_inc(s["ctx_shift"], 1)
                dve.wait_ge(s["ctx_shift"], 1)
                dve.wait_ge(s["lat_shift"], 2)
                dve.wait_ge(s["prep_psum"], PREP)
                nc.vector.tensor_copy(b_cols[:, :, :].rearrange("p t h -> p (t h)"), m.psum[:, 6, 0:2 * H3]).then_inc(s["prep_read"], 1)
                dve.wait_ge(s["prep_read"], PREP)
                nc.vector.tensor_copy(bv_wide[:, :, :], b_cols[:, 1, :].unsqueeze(2).to_broadcast([D, H3, S])).then_inc(s["prep_read"], 1)
                dve.wait_ge(s["prep_psum"], PREP + 3)
                nc.vector.tensor_copy(t0[:, :], m.psum[:, 4, 0:H3]).then_inc(s["w_ready"], 1)
                nc.vector.tensor_tensor(row_out[:, :], row_out[:, :], m.psum[:, 5, 0:D], ALU.add).then_inc(s["w_ready"], 1)
                dve.wait_ge(s["w_ready"], 4)
                nc.vector.tensor_scalar(row_out[:, :], row_out[:, :], gate, None, ALU.mult).then_inc(s["rows_ready"], 1)

                def normalize(b, slot):
                    wait(dve, s["kvt_in_psum"], b - 1)
                    wait(dve, s["kept"], (b - 1) * 2)
                    nc.vector.tensor_scalar(kn[0:KC, slot, 0, :], m.ctx[:, b, :], c_rstd[:, bass.ds(b, 1)],
                                            c_shift[:, bass.ds(b, 1)], ALU.mult, ALU.add).then_inc(s["cn_raw"], 1)
                    nc.vector.tensor_scalar(kn[:, slot, 1, :], m.x[:, b, :], l_scale[:, bass.ds(b, 1)],
                                            l_shift[:, bass.ds(b, 1)], ALU.mult, ALU.add).then_inc(s["ln_raw"], 1)

                def middle_one(b, par):
                    for half in range(2):
                        wait(dve, s["scores_done"], b * 2 + half + 1)
                        wait(dve, s["exp_ready"], b - 1)
                        banks, heads = slice(half * 2, half * 2 + 2), slice(half * HH, (half + 1) * HH)
                        sv = m.psum[:, banks, 0:HB * KV].rearrange("p n (h k) -> p n h k", h=HB)
                        nc.vector.tensor_reduce(negmax[:, par, heads].rearrange("p (n h) -> p n h", h=HB), sv, AX.X, ALU.max,
                                                negate=True).then_inc(s["negmax_ready"], 1)
                        wait(dve, s["negmax_ready"], b * 2 + half + 1)
                        nc.vector.tensor_scalar(shift_bias[:, par, heads], negmax[:, par, heads], SCALE, None, ALU.mult)\
                            .then_inc(s["shift_bias_ready"], 1)

                def full(b, par, front, middle, back):
                    nxt = 1 - par
                    if middle:
                        middle_one(b, par)
                    if back:
                        wait(dve, s["c_in_psum"], (b - 1) * 2)
                        wait(dve, s["pt_in_psum"], (b - 1) * 4 + 2)
                        nc.vector.tensor_copy(ptc[:, 512:1024], m.psum[0:KC, 4, :]).then_inc(s["pt_read_dve"], 1)
                        wait(dve, s["pt_in_psum"], (b - 1) * 4 + 4)
                        nc.vector.tensor_copy(ptl[:, 512:1024], m.psum[:, 6, :]).then_inc(s["pt_read_dve"], 1)
                    if middle:
                        wait(dve, s["exp_ready"], b + 1)
                        wait(dve, s["probs_ready"], b - 1)
                        nc.vector.reciprocal(recip[:, par, :], total[:, par, :]).then_inc(s["recip_ready"], 1)
                    if front:
                        for n in range(2):
                            wait(dve, s["q_in_psum"], (b + 1) * 2 + n + 1)
                            wait(dve, s["scores_done"], b * 2)
                            nc.vector.tensor_tensor(q[:, nxt, n * HH:(n + 1) * HH, :], m.psum[:, Q_BANKS[n], :].rearrange("p (h t) -> p h t", h=HH),
                                                    t0[:, n * HH:(n + 1) * HH].unsqueeze(2).to_broadcast([D, HH, S]), ALU.add).then_inc(s["q_ready"], 1)
                    if not isinstance(b, int) or b + 2 < B:
                        normalize(b + 2, par)
                    if back:
                        wait(dve, s["y_done"], b)
                        wait(dve, s["bias_added"], b)
                        nc.vector.scalar_tensor_tensor(m.x[:, b - 1, :], m.psum[:, 7, 256:256 + D], gate, m.x[:, b - 1, :],
                                                       ALU.mult, ALU.add).then_inc(s["x_done"], 1)
                        wait(dve, s["x_done"], b)
                        nc.vector.bn_stats(m.moments[:, b - 1, :], m.x[:, b - 1, :])

                normalize(0, 0)
                pipeline(dve, full)

            @block.tensor
            def _(pe):
                pe.wait_ge(m.later_loaded, m.later_count)
                for n in range(PREP - 1):
                    for h in range(HH):
                        head = HH * (n % 2) + h
                        w = wq[:, head * D:(head + 1) * D] if n < 2 else wkv[:, n // 2 - 1, head * D:(head + 1) * D]
                        mm = nc.tensor.transpose(m.psum[:, n, h * D:(h + 1) * D], w, m.ident[:, :])
                    mm.then_inc(s["prep_psum"], 1)
                for t in range(2):
                    mm = nc.tensor.transpose(m.psum[:, 6, t * H3:(t + 1) * H3], b_rows[:, t, :], m.ident[0:H3, 0:H3])
                mm.then_inc(s["prep_psum"], 1)
                pe.wait_ge(s["prep_read"], PREP + 1)
                for h in range(H3):
                    mm = nc.tensor.matmul(m.psum[:, h // HH, (h % HH) * D:(h % HH + 1) * D], w_t[:, 0, h, :], w_t[:, 1, h, :], start=True, stop=True)
                mm.then_inc(s["prep_psum"], 1)
                for h in range(H3):
                    mm = nc.tensor.matmul(m.psum[:, 2 + h // HH, (h % HH) * D:(h % HH + 1) * D], w_t[:, 2, h, :], wo[:, h, :], start=True, stop=True)
                mm.then_inc(s["prep_psum"], 1)
                for h in range(H3):
                    nc.tensor.matmul(m.psum[:, 4, h:h + 1], w_t[:, 1, h, :], b_cols[:, 0, h:h + 1], start=True, stop=True)
                for h in range(H3):
                    mm = nc.tensor.matmul(m.psum[:, 5, 0:D], bv_wide[:, h, :], wo[:, h, :], start=(h == 0), stop=(h == H3 - 1))
                mm.then_inc(s["prep_psum"], 1)
                pe.wait_ge(s["w_ready"], 4)

                def step(b, par, front, middle, back):
                    nxt = 1 - par
                    if middle:
                        wait(pe, s["q_ready"], (b + 1) * 2)
                        wait(pe, s["exp_ready"], b)
                        for h in range(H3):
                            mm = nc.tensor.matmul(m.psum[:, h // HB, (h % HB) * KV:(h % HB + 1) * KV], q[:, par, h, :], kvt[:, par, :], start=True, stop=True)
                            if h % HH == HH - 1:
                                mm.then_inc(s["scores_done"], 1)
                    if front:
                        wait(pe, s["cn_ready"], b + 2)
                        wait(pe, s["ln_ready"], b + 2)
                        wait(pe, s["kvt_ready"], b + 1)
                        wait(pe, s["x_done"], b - 1)
                        nc.tensor.transpose(m.psum[:, 7, 0:KC], kv[0:KC, nxt, 0, :], m.ident[0:KC, 0:KC])
                        nc.tensor.transpose(m.psum[:, 7, KC:KV], kv[:, nxt, 1, :], m.ident[:, :]).then_inc(s["kvt_in_psum"], 1)
                    if back:
                        wait(pe, s["probs_ready"], b)
                        if not middle:
                            wait(pe, s["q_ready"], b * 2)
                        wait(pe, s["c_ready"], (b - 1) * 2)
                        for n, (bank, keys, half) in enumerate(((6, 0, 0), (4, 0, 1), (5, 1, 0), (6, 1, 1))):
                            k0, k1 = (0, KC) if keys == 0 else (KC, KV)
                            if n == 0:
                                wait(pe, s["pt_read_dve"], (b - 1) * 2)
                            if n == 3:
                                wait(pe, s["pt_read_act"], (b - 1) * 2 + 1)
                            for h in range(HH):
                                mm = nc.tensor.transpose(m.psum[0:k1 - k0, bank, h * S:(h + 1) * S], e[:, nxt, half * HH + h, k0:k1], m.ident[:, :])
                            mm.then_inc(s["pt_in_psum"], 1)
                    if back:
                        wait(pe, s["kept"], b * 2)
                        for half in range(2):
                            wait(pe, s["pt_read_act"], b * 2)
                            wait(pe, s["pt_read_dve"], b * 2 - 1 + half)
                            cols = slice(half * 512, (half + 1) * 512)
                            nc.tensor.matmul(m.psum[:, 4 + half, :], kept[0:KC, nxt, 0, :], ptc[:, cols], start=True, stop=False)
                            nc.tensor.matmul(m.psum[:, 4 + half, :], kept[:, nxt, 1, :], ptl[:, cols], start=False, stop=True).then_inc(s["c_in_psum"], 1)
                    if front:
                        wait(pe, s["kvt_ready"], b + 2)
                        for n in range(2):
                            if n == 0 and back:
                                wait(pe, s["pt_read_dve"], b * 2)
                            if n == 1 and back:
                                wait(pe, s["c_ready"], b * 2 - 1)
                            for h in range(HH):
                                mm = nc.tensor.matmul(m.psum[:, Q_BANKS[n], h * S:(h + 1) * S], w_qk[:, n * HH + h, :], kvt[:, nxt, KC:KV],
                                                      start=True, stop=True)
                            mm.then_inc(s["q_in_psum"], 1)
                    if back:
                        wait(pe, s["c_ready"], b * 2)
                        for h in range(H3):
                            mm = nc.tensor.matmul(m.psum[:, 7, 256:256 + D], c[:, h, :], w_vo[:, h, :], start=(h == 0), stop=(h == H3 - 1))
                        mm.then_inc(s["y_done"], 1)

                pipeline(pe, step)


def store(nc, m, a, sem):
    stored = sem("stored")
    with nc.Block() as block:
        @block.sync
        def _(sync):
            sync.dma_start(a["out"].rearrange("b s d -> s b d"), m.x[:, :, :]).then_inc(stored, 16)
            sync.wait_ge(stored, 16)


def program(nc, a, last_phase=99, first_phase=0):
    with ExitStack() as ctx:
        m = allocate(nc, ctx)
        previous = []

        def phase(build, *args, **more):
            held = []

            def sem(name):
                held.append(nc.alloc_semaphore(name))
                return held[-1]

            def clear(pool):
                for old in previous:
                    pool.sem_clear(old)

            build(nc, m, sem, *args, clear, **more)
            for old in previous:
                nc.release_semaphore(old)
            previous[:] = held

        prepare(nc, ctx, m, a)
        if first_phase < 1 <= last_phase:
            phase(head_attention, 0, (m.wq0, m.wk0, m.wv0, m.wo0))
        if first_phase < 2 <= last_phase:
            phase(experts, 0, m.router_t, lambda e: a["L0_ffn_w1"][e], None, lambda e: a["L0_ffn_w2"][e], E0, 0)
        if first_phase < 3 <= last_phase:
            phase(competitive_attention)
        if first_phase < 4 <= last_phase:
            phase(dense_feed_forward)
        if first_phase < 5 <= last_phase:
            phase(head_attention, 2, (m.wq2, m.wk2, m.wv2, m.wo2))
        if first_phase < 6 <= last_phase:
            phase(controller_feed_forward)
        if first_phase < 7 <= last_phase:
            phase(latent_attention)
        if first_phase < 8 <= last_phase:
            phase(experts, 3, m.wg3, lambda e: a["L3_ffn_Ws1"] if e == 0 else a["L3_ffn_We1"][e - 1],
                  lambda e: a["L3_ffn_Ws3"] if e == 0 else a["L3_ffn_We3"][e - 1],
                  lambda e: a["L3_ffn_Ws2"] if e == 0 else a["L3_ffn_We2"][e - 1], E3 + 1, 1, out=a["out"])
        if last_phase < 8:
            store(nc, m, a, lambda n: ctx.enter_context(nc.semaphore(n)))


_OUTS = [((B, S, D), "float32")]


def kernel(**inputs):
    import numpy as _np
    import concourse.bacc as _bacc
    from concourse import mybir as _mybir
    from concourse.bass_utils import run_bass_kernel_spmd as _run

    nc = _bacc.Bacc("TRN2", target_bir_lowering=False, num_devices=1)
    arrays, args = {}, {}
    for name in inputs:
        v = _np.ascontiguousarray(inputs[name])
        arrays[f"in_{name}_dram"] = v
        args[name] = nc.dram_tensor(f"in_{name}_dram", v.shape, _mybir.dt.from_np(v.dtype), kind="ExternalInput").ap()
    for i, (shape, dtype) in enumerate(_OUTS):
        args["out"] = nc.dram_tensor(f"out_{i}_dram", shape, _mybir.dt.from_np(_np.dtype(dtype)), kind="ExternalOutput").ap()
    program(nc, args)
    r = _run(nc, [arrays], core_ids=[0])
    return r.results[0]["out_0_dram"]
```
